# Optimizing a Trainium2 kernel written in Bass

```python
import numpy as np
import jax
import jax.numpy as jnp

def _softmax(x, axis=-1):
    return jax.nn.softmax(x, axis=axis)

def _gelu(x):
    return jax.nn.gelu(x, approximate=True)

def _silu(x):
    return jax.nn.silu(x)

def _sigmoid(x):
    return jax.nn.sigmoid(x)

def _layernorm(x, axis=-1, eps=1e-05):
    m = jnp.mean(x, axis=axis, keepdims=True)
    v = jnp.var(x, axis=axis, keepdims=True)
    return (x - m) / jnp.sqrt(v + eps)

def _scatter_add(tgt, idx, src, axis=0):
    return tgt.at[idx].add(src)

def _segment_sum(src, seg, n):
    return jax.ops.segment_sum(src, seg, n)
kernel_name = 'mk_gps_d1_gnn_r16_8e442d'

def setup_inputs(seed: int=0):
    np.random.seed(seed)
    _w = jnp.asarray

    def _rec_inputs():
        import jax
        import jax.numpy as jnp
        _gk = jax.random.key(seed)
        x = -0.0003713 + 1 * jax.random.normal(jax.random.fold_in(_gk, 1), (3125, 256), jnp.float32)
        src = jax.random.randint(jax.random.fold_in(_gk, 2), (50000,), 0, 3125, jnp.int32)
        dst = jnp.minimum((3125 * jax.random.uniform(jax.random.fold_in(_gk, 3), (50000,)) ** 2.0).astype(jnp.int32), 49999)
        _o = jnp.argsort(dst, stable=True)
        src = src[_o]
        dst = dst[_o]
        edge_type_3 = jax.random.randint(jax.random.fold_in(_gk, 12), (50000,), 0, 3, jnp.int32)
        return (x, src, dst, edge_type_3)
    x, src, dst, edge_type_3 = _rec_inputs()

    def _L0_gnn_setup():
        import jax, jax.numpy as jnp
        import numpy as np
        N, C, E, STEPS, T = (3125, 256, 100000, 3, 3)
        LEAKY_SLOPE = 0.1
        LN_EPS = 1e-05

        def _gru_cell(m, h, wih, whh, bih, bhh):
            gi = m @ wih.T + bih
            gh = h @ whh.T + bhh
            i_r, i_z, i_n = jnp.split(gi, 3, axis=-1)
            h_r, h_z, h_n = jnp.split(gh, 3, axis=-1)
            r = jax.nn.sigmoid(i_r + h_r)
            z = jax.nn.sigmoid(i_z + h_z)
            n = jnp.tanh(i_n + r * h_n)
            return (1.0 - z) * n + z * h

        def _gated_graph_conv(x, src, dst, emask, W, wih, whh, bih, bhh):
            h = x
            for i in range(STEPS):
                m = h @ W[i]
                msg = m[src] * emask[:, None]
                agg = jax.ops.segment_sum(msg, dst, num_segments=N)
                h = _gru_cell(agg, h, wih, whh, bih, bhh)
            return h
        key = jax.random.key(seed)
        ks = jax.random.split(key, 12)
        h = jax.random.normal(ks[0], (N, C), dtype=jnp.float32)
        edge_index = jax.random.randint(ks[1], (2, E), 0, N, dtype=jnp.int64)
        edge_type = jax.random.randint(ks[2], (E,), 0, T, dtype=jnp.int64)
        s = 1.0 / np.sqrt(C)
        conv_w = jax.random.uniform(ks[3], (T, STEPS, C, C), jnp.float32, -s, s)
        gru_wih = jax.random.uniform(ks[4], (T, 3 * C, C), jnp.float32, -s, s)
        gru_whh = jax.random.uniform(ks[5], (T, 3 * C, C), jnp.float32, -s, s)
        gru_bih = jax.random.uniform(ks[6], (T, 3 * C), jnp.float32, -s, s)
        gru_bhh = jax.random.uniform(ks[7], (T, 3 * C), jnp.float32, -s, s)
        ln_gamma = jnp.ones((C,), jnp.float32)
        ln_beta = jnp.zeros((C,), jnp.float32)
        return dict(h=h, edge_index=edge_index, edge_type=edge_type, conv_w=conv_w, gru_wih=gru_wih, gru_whh=gru_whh, gru_bih=gru_bih, gru_bhh=gru_bhh, ln_gamma=ln_gamma, ln_beta=ln_beta)
    _L0_gnn_all = _L0_gnn_setup()
    _L0_gnn_in = {k: v for k, v in _L0_gnn_all.items() if k in ('conv_w', 'gru_wih', 'gru_whh', 'gru_bih', 'gru_bhh', 'ln_gamma', 'ln_beta')}
    del _L0_gnn_all

    def _L0_mix_setup():
        import jax, jax.numpy as jnp
        import numpy as np
        A, Bc, Cc = (0.5, 1.0, 1.0)
        H = 8
        EPS = 1e-12

        def _normalize(t):
            n = jnp.linalg.norm(t, axis=-1, keepdims=True)
            return t / jnp.maximum(n, EPS)
        key = jax.random.key(seed)
        ks = jax.random.split(key, 5)
        B, N, C = (8, 128, 256)
        D = C // H
        x = jax.random.normal(ks[0], (B, N, C), dtype=jnp.float32)
        Wqkv = jax.random.normal(ks[1], (3 * H * D, C), dtype=jnp.float32) * 0.02
        bqkv = jnp.zeros((3 * H * D,), dtype=jnp.float32)
        Wproj = jax.random.normal(ks[2], (C, H * D), dtype=jnp.float32) * 0.02
        bproj = jnp.zeros((C,), dtype=jnp.float32)
        temperature = jnp.ones((1, H, 1, 1), dtype=jnp.float32)
        return {'x': x, 'Wqkv': Wqkv, 'bqkv': bqkv, 'Wproj': Wproj, 'bproj': bproj, 'temperature': temperature}
    _L0_mix_all = _L0_mix_setup()
    _L0_mix_in = {k: v for k, v in _L0_mix_all.items() if k in ('Wqkv', 'bqkv', 'Wproj', 'bproj', 'temperature')}
    del _L0_mix_all

    def _L0_ffn_setup():
        import jax, jax.numpy as jnp
        import numpy as np
        TOP_K = 2
        key = jax.random.key(seed)
        ks = jax.random.split(key, 4)
        B, L, D, H, E = (8, 256, 256, 1024, 8)
        s = 0.02
        return {'x': jax.random.normal(ks[0], (B, L, D), jnp.float32), 'Wg': jax.random.normal(ks[1], (D, E), jnp.float32) * s, 'bg': jnp.zeros((E,), jnp.float32), 'W1': jax.random.normal(ks[2], (E, D, H), jnp.float32) * s, 'b1': jnp.zeros((E, H), jnp.float32), 'W2': jax.random.normal(ks[3], (E, H, D), jnp.float32) * s, 'b2': jnp.zeros((E, D), jnp.float32)}
    _L0_ffn_all = _L0_ffn_setup()
    _L0_ffn_in = {k: v for k, v in _L0_ffn_all.items() if k in ('Wg', 'bg', 'W1', 'b1', 'W2', 'b2')}
    del _L0_ffn_all
    return {'x': x, 'src': src, 'dst': dst, 'edge_type_3': edge_type_3, 'L0_gnn_conv_w': _L0_gnn_in['conv_w'], 'L0_gnn_gru_wih': _L0_gnn_in['gru_wih'], 'L0_gnn_gru_whh': _L0_gnn_in['gru_whh'], 'L0_gnn_gru_bih': _L0_gnn_in['gru_bih'], 'L0_gnn_gru_bhh': _L0_gnn_in['gru_bhh'], 'L0_gnn_ln_gamma': _L0_gnn_in['ln_gamma'], 'L0_gnn_ln_beta': _L0_gnn_in['ln_beta'], 'L0_mix_Wqkv': _L0_mix_in['Wqkv'], 'L0_mix_bqkv': _L0_mix_in['bqkv'], 'L0_mix_Wproj': _L0_mix_in['Wproj'], 'L0_mix_bproj': _L0_mix_in['bproj'], 'L0_mix_temperature': _L0_mix_in['temperature'], 'L0_ffn_Wg': _L0_ffn_in['Wg'], 'L0_ffn_bg': _L0_ffn_in['bg'], 'L0_ffn_W1': _L0_ffn_in['W1'], 'L0_ffn_b1': _L0_ffn_in['b1'], 'L0_ffn_W2': _L0_ffn_in['W2'], 'L0_ffn_b2': _L0_ffn_in['b2']}

def reference(x, src, dst, edge_type_3, L0_gnn_conv_w, L0_gnn_gru_wih, L0_gnn_gru_whh, L0_gnn_gru_bih, L0_gnn_gru_bhh, L0_gnn_ln_gamma, L0_gnn_ln_beta, L0_mix_Wqkv, L0_mix_bqkv, L0_mix_Wproj, L0_mix_bproj, L0_mix_temperature, L0_ffn_Wg, L0_ffn_bg, L0_ffn_W1, L0_ffn_b1, L0_ffn_W2, L0_ffn_b2):
    import jax
    import jax.numpy as jnp

    def _L0_gnn_ref(h, edge_index, edge_type, conv_w, gru_wih, gru_whh, gru_bih, gru_bhh, ln_gamma, ln_beta):
        import jax, jax.numpy as jnp
        import numpy as np
        N, C, E, STEPS, T = (3125, 256, 100000, 3, 3)
        LEAKY_SLOPE = 0.1
        LN_EPS = 1e-05

        def _gru_cell(m, h, wih, whh, bih, bhh):
            gi = m @ wih.T + bih
            gh = h @ whh.T + bhh
            i_r, i_z, i_n = jnp.split(gi, 3, axis=-1)
            h_r, h_z, h_n = jnp.split(gh, 3, axis=-1)
            r = jax.nn.sigmoid(i_r + h_r)
            z = jax.nn.sigmoid(i_z + h_z)
            n = jnp.tanh(i_n + r * h_n)
            return (1.0 - z) * n + z * h

        def _gated_graph_conv(x, src, dst, emask, W, wih, whh, bih, bhh):
            h = x
            for i in range(STEPS):
                m = h @ W[i]
                msg = m[src] * emask[:, None]
                agg = jax.ops.segment_sum(msg, dst, num_segments=N)
                h = _gru_cell(agg, h, wih, whh, bih, bhh)
            return h
        src, dst = (edge_index[0], edge_index[1])
        h_msg = jnp.zeros_like(h)
        for t in range(T):
            emask = (edge_type == t).astype(h.dtype)
            h_msg = h_msg + _gated_graph_conv(h, src, dst, emask, conv_w[t], gru_wih[t], gru_whh[t], gru_bih[t], gru_bhh[t])
        x = h + h_msg
        mu = jnp.mean(x, axis=-1, keepdims=True)
        var = jnp.var(x, axis=-1, keepdims=True)
        x = (x - mu) * jax.lax.rsqrt(var + LN_EPS) * ln_gamma + ln_beta
        return jnp.where(x >= 0, x, LEAKY_SLOPE * x)

    def _L0_mix_ref(x, Wqkv, bqkv, Wproj, bproj, temperature):
        import jax, jax.numpy as jnp
        import numpy as np
        A, Bc, Cc = (0.5, 1.0, 1.0)
        H = 8
        EPS = 1e-12

        def _normalize(t):
            n = jnp.linalg.norm(t, axis=-1, keepdims=True)
            return t / jnp.maximum(n, EPS)
        B, N, C = x.shape
        D = C // H
        scale = float(D) ** 0.25
        qkv = (x @ Wqkv.T + bqkv).reshape(B, N, 3, H, D)
        qkv = jnp.transpose(qkv, (2, 0, 3, 1, 4))
        q, k, v = (qkv[0], qkv[1], qkv[2])
        q = q * scale
        v1 = jnp.concatenate([jnp.ones((B, H, N, 1), dtype=v.dtype), v], axis=-1)
        qn = _normalize(q) * (scale * temperature)
        kn = _normalize(k) * scale
        vN = v1 / N
        kv_mod = jnp.einsum('bhni,bhnj,bhne->bhije', kn, kn, vN)
        kv = jnp.einsum('bhnd,bhne->bhde', kn, vN)
        vsum = jnp.sum(vN, axis=-2)[:, :, None, :]
        y = A * jnp.einsum('bhni,bhnj,bhije->bhne', qn, qn, kv_mod) + scale ** 2 * Bc * jnp.einsum('bhnd,bhde->bhne', qn, kv) + scale ** 4 * Cc * vsum
        y_norm, y = (y[..., :1], y[..., 1:])
        y = y / y_norm
        out = jnp.transpose(y, (0, 2, 1, 3)).reshape(B, N, H * D)
        return out @ Wproj.T + bproj

    def _L0_ffn_ref(x, Wg, bg, W1, b1, W2, b2):
        import jax, jax.numpy as jnp
        import numpy as np
        TOP_K = 2
        B, L, D = x.shape
        E = W1.shape[0]
        xf = x.reshape(-1, D)
        gate_logits = xf @ Wg + bg
        top_w, top_i = jax.lax.top_k(gate_logits, TOP_K)
        top_w = jax.nn.softmax(top_w, axis=-1)
        w_dense = jnp.sum(jax.nn.one_hot(top_i, E, dtype=xf.dtype) * top_w[..., None], axis=1)
        out = jnp.zeros_like(xf)
        for e in range(E):
            h = jax.nn.gelu(xf @ W1[e] + b1[e], approximate=False)
            out = out + w_dense[:, e:e + 1] * (h @ W2[e] + b2[e])
        return out.reshape(B, L, D)
    edge_index = jnp.stack([src, dst])
    xn = _layernorm(x, axis=-1)
    x = x + _L0_gnn_ref(xn, edge_index, edge_type_3, L0_gnn_conv_w, L0_gnn_gru_wih, L0_gnn_gru_whh, L0_gnn_gru_bih, L0_gnn_gru_bhh, L0_gnn_ln_gamma, L0_gnn_ln_beta) + _L0_mix_ref(xn[None], L0_mix_Wqkv, L0_mix_bqkv, L0_mix_Wproj, L0_mix_bproj, L0_mix_temperature)[0]
    x = x + _L0_ffn_ref(_layernorm(x, axis=-1)[None], L0_ffn_Wg, L0_ffn_bg, L0_ffn_W1, L0_ffn_b1, L0_ffn_W2, L0_ffn_b2)[0]
    return x

_drawn_inputs = setup_inputs


def setup_inputs(seed=0):
    import zlib

    import numpy as np

    out = dict(_drawn_inputs(seed))
    spreads = {'L0_gnn_ln_gamma': (1.0, 0.2),
     'L0_gnn_ln_beta': (0.0, 0.1),
     'L0_mix_bqkv': (0.0, 0.38),
     'L0_mix_bproj': (0.0, 0.1),
     'L0_mix_temperature': (1.0, 0.6),
     'L0_ffn_bg': (0.0, 0.1),
     'L0_ffn_b1': (0.0, 0.49),
     'L0_ffn_b2': (0.0, 0.1)}
    factors = {'L0_gnn_gru_bhh': 4.546, 'L0_mix_Wqkv': 8.0, 'L0_mix_Wproj': 2.792}
    for name, (base, spread) in spreads.items():
        noise = np.random.default_rng([zlib.crc32(name.encode()), seed]).standard_normal(out[name].shape)
        drawn = base * np.exp(spread * noise) if base else spread * noise
        out[name] = jnp.asarray(drawn.astype(out[name].dtype))
    for name, factor in factors.items():
        out[name] = (out[name] * factor).astype(out[name].dtype)
    return out
```

```python
import concourse.bass as bass
from concourse import mybir

F32 = mybir.dt.float32
I32 = mybir.dt.int32
ALU = mybir.AluOpType
ACT = mybir.ActivationFunctionType
AX = mybir.AxisListType

N, C, E = 3125, 256, 50000
STEPS, TYPES = 3, 3
P = 128
KC = C // P
PT = 112
TILES = 28
NP = PT * TILES
GW = 4 * PT
GROUPS = NP // GW
LAST = N - PT * (TILES - 1)
DT = 41
TG = 11
DTL = GW - DT * (TG - 1)
NT = GROUPS * TG
NKEY = TYPES * DT
TYPEKEY = 4096
NODST = 4000
EROWS = E // P
EREST = E - EROWS * P
EB = 4
NCH = EB * P
R = 4
HEADS, HD = 8, 32
ND = HD // 2 + 1
FEAT = ND * HD + HD + 1
FCH = (FEAT + P - 1) // P
FP = FCH * P
VD = HD + 1
SC = float(HD) ** 0.25
XPT, HID = 8, 1024
HC = HID // P


def counted(eng, sem, base):
    count = [0]

    def step(ins):
        count[0] += 1
        ins.then_inc(sem, 1)
        eng.wait_ge(sem, base + count[0])
        return count[0]
    return step


def hold(e, ticks):
    e.tensor_copy(ticks[0][0:1, 1:2], ticks[0][0:1, 0:1])


def hold_pool(e, ticks, held, n):
    e.wait_ge(held, n)
    t = ticks[1]
    e.tensor_tensor(t[0:1, 1:2], t[0:1, 0:1], t[0:1, 0:1], ALU.add).then_inc(held, 1)


def scoped(nc, ctx):
    mine = []

    def sem(name):
        mine.append(nc.alloc_semaphore(name))
        return mine[-1]

    def give_back():
        nc.clear_and_free_semaphores(mine)
        nc.all_engine_barrier()
    ctx.callback(give_back)
    return sem


def gps_layer_kernel(nc, A):
    def sb(name, shape, dt=F32):
        return nc.alloc_sbuf_tensor(name, shape, dt)

    sem = nc.alloc_semaphore
    out = A["out"]
    table0 = nc.dram_tensor("xn_rows", [NP, C], F32).ap()
    tables = [table0] + [nc.dram_tensor(f"h_rows{s}", [TYPES * NP, C], F32).ap() for s in (1, 2)]
    hT0 = nc.dram_tensor("xn_cols", [P, KC, NP], F32).ap()
    hTs = [nc.dram_tensor(f"h_cols{s}", [TYPES, P, KC, NP], F32).ap() for s in (1, 2)]

    acc = sb("acc", [PT, TILES, C])
    gm = sb("gm", [PT, TILES, C])
    xnT = sb("xnT", [P, KC, NP])
    ident = sb("ident", [P, P])
    ones = sb("ones", [1, 512])
    keys = sb("keys", [P, NCH])
    idx0 = sb("idx0", [P, NCH], I32)
    idx1 = sb("idx1", [P, NCH], I32)
    tab = sb("tab", [1, 160], I32)
    iota_keys = sb("iota_keys", [P, TYPES, DT])
    tile_keys = sb("tile_keys", [P, TYPES, DT])
    s_z = sem("const_zeroed")
    s_c = sem("const_ready")
    cdve = sem("const_dve")
    iota_i = sb("iota_i", [P, TYPES, DT], I32)
    nc_ticks = sb("tick_d", [1, 2]), sb("tick_p", [1, 2])
    with nc.Block() as block:
        @block.gpsimd
        def _(e):
            e.memset(ident[:, :], 0.0).then_inc(s_z, 1)
            e.wait_ge(s_z, 1)
            e.affine_select(out=ident[:, :], in_=ident[:, :], compare_op=ALU.not_equal, fill=1.0,
                            base=0, pattern=[[-1, P]], channel_multiplier=1).then_inc(s_c, 1)
            e.memset(ones[:, :], 1.0).then_inc(s_c, 1)
            e.iota(iota_i[:, :, :], [[TYPEKEY, TYPES], [1, DT]], base=0, channel_multiplier=0).then_inc(s_c, 1)

        @block.vector
        def _(e):
            for t in nc_ticks:
                e.memset(t[:, :], 0.0)
            e.wait_ge(s_c, 3)
            e.tensor_copy(iota_keys[:, :, :], iota_i[:, :, :]).then_inc(cdve, 1)
            e.wait_ge(cdve, 1)

    edge_tables(nc, sb, sem, A, ident, keys, idx0, idx1, tab)
    normalise(nc, sb, sem, "in", acc, gm, xnT, ident, load=A["x"], rows=table0, cols=hT0, ticks=nc_ticks)
    mix(nc, sem, A, acc, xnT, ident, ones)
    for s in range(STEPS):
        gnn_step(nc, sem, A, s, tables, [hT0] + hTs, idx0 if s == 0 else idx1, keys, tab,
                 iota_keys, tile_keys, ident, gm, xnT, nc_ticks)
    gnn_out(nc, sem, A, acc, gm, nc_ticks)
    normalise(nc, sb, sem, "ffn", acc, gm, xnT, ident, ticks=nc_ticks)
    ffn(nc, sem, A, acc, xnT, ident, ones, out, nc_ticks)


def edge_tables(nc, sb_, sem, A, ident, keys, idx0, idx1, tab):
    from contextlib import ExitStack
    with ExitStack() as ctx:
        sem = scoped(nc, ctx)
        def sb(name, shape, dt=F32):
            return ctx.enter_context(nc.sbuf_tensor(name, shape, dt))

        def ps(name, shape):
            return ctx.enter_context(nc.psum_tensor(name, shape, F32))
        ei = sb("ei", [P, 3, EB, P], I32)
        ef = sb("ef", [P, 3, EB, P])
        rows = sb("rows", [P, 3, EB, P])
        lim = sb("lim", [P, 2, EB])
        bcast = sb("lim_bcast", [P, 2, EB, NT])
        onesm = sb("onesm", [P, NT])
        base_i = sb("base_i", [1, NT], I32)
        base_r = sb("base_r", [1, NT])
        tlo = sb("tlo", [NT, 1])
        thi = sb("thi", [NT, 1])
        cio_i = sb("cio_i", [NT, NCH], I32)
        cio = sb("cio", [NT, NCH])
        member = sb("member", [NT, NCH])
        work = sb("work", [NT, NCH])
        col = sb("col", [NT, 8])
        col_i = sb("col_i", [NT, 1], I32)
        tri = sb("tri", [NT, NT + 1])
        pt = [ps(f"et{i}", [P, EB, P]) for i in range(3)]
        pl = [ps(f"el{i}", [NT, NCH]) for i in range(2)]
        pb = ps("eb", [NT, 1])
        pr = ps("er", [1, 256])
        e_set, e_in, e_io, e_d, e_row, e_t, e_lim, e_pl, e_n, e_r = (sem(f"edge_{n}") for n in (
            "set", "loaded", "iota", "dve", "rows", "turned", "limits", "limits_turned", "counts", "table"))
        with nc.Block() as block:
            @block.sync
            def _(e):
                e.wait_ge(e_set, 3)
                for k, name in enumerate(("src", "dst", "edge_type_3")):
                    a = A[name]
                    for b in range(3):
                        e.dma_start(ei[:, k, b, :], a[b * P * P:(b + 1) * P * P].rearrange("(r q) -> r q", q=P)).then_inc(e_in, 16)
                    n = EROWS - 3 * P
                    e.dma_start(ei[0:n, k, 3, :], a[3 * P * P:EROWS * P].rearrange("(r q) -> r q", q=P)).then_inc(e_in, 16)
                    e.dma_start(ei[n:n + 1, k, 3, 0:EREST], a[EROWS * P:E].rearrange("(r q) -> r q", r=1)).then_inc(e_in, 16)

            @block.gpsimd
            def _(e):
                e.iota(base_i[:, :], [[GW, GROUPS], [DT, TG]], base=0, channel_multiplier=0).then_inc(e_io, 1)
                e.iota(cio_i[:, :], [[1, NCH]], base=0, channel_multiplier=0).then_inc(e_io, 1)
                e.memset(tri[:, :], 1.0).then_inc(e_io, 1)
                e.wait_ge(e_io, 3)
                e.affine_select(out=tri[:, :], in_=tri[:, :], compare_op=ALU.is_gt, fill=0.0,
                                base=0, pattern=[[1, NT + 1]], channel_multiplier=-1).then_inc(e_io, 1)

            @block.vector
            def _(e):
                step = counted(e, e_d, 0)
                e.memset(ei[:, 0, 3, :], 0).then_inc(e_set, 1)
                e.memset(ei[:, 1, 3, :], NODST).then_inc(e_set, 1)
                e.memset(ei[:, 2, 3, :], 0).then_inc(e_set, 1)
                e.memset(onesm[:, :], 1.0)
                e.wait_ge(e_in, 16 * 15)
                step(e.tensor_copy(ef[:, :, :, :], ei[:, :, :, :]))
                e.tensor_copy(rows[:, 0, :, :], ef[:, 0, :, :]).then_inc(e_row, 1)
                e.scalar_tensor_tensor(out=rows[:, 1, :, :], in0=ef[:, 2, :, :], scalar=float(NP), in1=ef[:, 0, :, :], op0=ALU.mult, op1=ALU.add).then_inc(e_row, 1)
                e.scalar_tensor_tensor(out=rows[:, 2, :, :], in0=ef[:, 2, :, :], scalar=float(TYPEKEY), in1=ef[:, 1, :, :], op0=ALU.mult, op1=ALU.add).then_inc(e_row, 1)
                step(e.tensor_reduce(lim[:, 0, :], ef[:, 1, :, :], AX.X, ALU.min))
                step(e.tensor_reduce(lim[:, 1, :], ef[:, 1, :, :], AX.X, ALU.max))
                for k in range(2):
                    for b in range(EB):
                        e.tensor_scalar(bcast[:, k, b, :], onesm[:, :], lim[:, k, b:b + 1], None, ALU.mult).then_inc(e_lim, 1)
                e.wait_ge(e_io, 4)
                step(e.tensor_copy(base_r[:, :], base_i[:, :]))
                e.tensor_copy(cio[:, :], cio_i[:, :]).then_inc(e_lim, 1)
                e.wait_ge(e_t, 3)
                for k, t in enumerate((idx0, idx1, keys)):
                    e.tensor_copy(t[:, :], pt[k][:, :, :].rearrange("p a b -> p (a b)")).then_inc(e_row, 1)
                e.wait_ge(e_pl, 3)
                step(e.tensor_copy(tlo[:, :], pb[:, :]))
                step(e.tensor_scalar(thi[:, :], tlo[:, :], float(DT - 1), None, ALU.add))
                step(e.tensor_scalar(work[:, :], pl[0][:, :], thi[:, 0:1], None, ALU.is_le))
                step(e.scalar_tensor_tensor(out=member[:, :], in0=pl[1][:, :], scalar=tlo[:, 0:1], in1=work[:, :], op0=ALU.is_ge, op1=ALU.mult))
                step(e.scalar_tensor_tensor(out=work[:, :], in0=cio[:, :], scalar=-1024.0, in1=member[:, :], op0=ALU.add, op1=ALU.mult))
                step(e.tensor_reduce(col[:, 0:1], work[:, :], AX.X, ALU.min))
                step(e.scalar_tensor_tensor(out=work[:, :], in0=cio[:, :], scalar=1.0, in1=member[:, :], op0=ALU.add, op1=ALU.mult))
                step(e.tensor_reduce(col[:, 1:2], work[:, :], AX.X, ALU.max))
                step(e.tensor_scalar(col[:, 2:3], col[:, 1:2], 0.0, None, ALU.is_gt))
                step(e.scalar_tensor_tensor(out=col[:, 3:4], in0=col[:, 0:1], scalar=1024.0, in1=col[:, 2:3], op0=ALU.add, op1=ALU.mult))
                step(e.tensor_scalar(col[:, 4:5], col[:, 3:4], 1.0, None, ALU.add))
                step(e.tensor_tensor(col[:, 5:6], col[:, 4:5], col[:, 1:2], ALU.max))
                step(e.scalar_tensor_tensor(out=col[:, 6:7], in0=col[:, 5:6], scalar=float(R - 1), in1=col[:, 3:4], op0=ALU.add, op1=ALU.subtract))
                step(e.tensor_copy(col_i[:, :], col[:, 6:7]))
                step(e.tensor_scalar(col_i[:, :], col_i[:, :], R.bit_length() - 1, None, ALU.logical_shift_right))
                e.tensor_copy(col[:, 7:8], col_i[:, :]).then_inc(e_n, 1)
                e.wait_ge(e_r, 1)
                e.tensor_copy(tab[:, 0:NT + 1], pr[:, 0:NT + 1]).then_inc(e_n, 1)
                e.tensor_copy(tab[:, 80:80 + NT], pr[:, 80:80 + NT]).then_inc(e_n, 1)

            @block.tensor
            def _(e):
                e.wait_ge(e_row, 3)
                for k in range(3):
                    for b in range(EB):
                        last = e.transpose(pt[k][:, b, :], rows[:, k, b, :], ident[:, :])
                    last.then_inc(e_t, 1)
                e.wait_ge(e_lim, 9)
                for k in range(2):
                    for b in range(EB):
                        last = e.matmul(pl[k][:, b * P:(b + 1) * P], bcast[:, k, b, :], ident[:, :], start=True, stop=True)
                    last.then_inc(e_pl, 1)
                e.matmul(pb[:, :], base_r[:, :], ident[0:1, 0:1], start=True, stop=True).then_inc(e_pl, 1)
                e.wait_ge(e_n, 1)
                e.matmul(pr[:, 0:NT + 1], col[:, 7:8], tri[:, :], start=True, stop=True)
                e.matmul(pr[:, 80:80 + NT], col[:, 3:4], ident[0:NT, 0:NT], start=True, stop=True).then_inc(e_r, 1)


def normalise(nc, sb_, sem, tag, acc, gm, xnT, ident, load=None, rows=None, cols=None, ticks=None):
    from contextlib import ExitStack
    with ExitStack() as ctx:
        sem = scoped(nc, ctx)
        stats = ctx.enter_context(nc.sbuf_tensor(f"{tag}_stats", [PT, 2, 6], F32))
        mv = ctx.enter_context(nc.sbuf_tensor(f"{tag}_mv", [PT, TILES, 2], F32))
        rstd = ctx.enter_context(nc.sbuf_tensor(f"{tag}_rstd", [PT, TILES], F32))
        std = ctx.enter_context(nc.sbuf_tensor(f"{tag}_std", [PT, TILES], F32))
        mv1 = ctx.enter_context(nc.sbuf_tensor(f"{tag}_mv1", [PT, 2], F32))
        xr = ctx.enter_context(nc.sbuf_tensor(f"{tag}_xr", [PT, 2, C], F32))
        pt = [ctx.enter_context(nc.psum_tensor(f"{tag}_pt{i}", [P, KC, 256], F32)) for i in range(2)]
        n_z, n_in, n_d, n_v, n_s, n_x, n_t, n_c, n_o, n_g = (sem(f"norm_{tag}_{n}") for n in (
            "zeroed", "loaded", "dve", "var", "std", "rows", "turned", "copied", "stored", "kept"))
        with nc.Block() as block:
            @block.vector
            def _(e):
                if load is not None:
                    e.memset(acc[:, TILES - 1, :], 0.0).then_inc(n_z, 1)
                    e.wait_ge(n_in, 32)
                with e.Fori(0, TILES) as i:
                    step = counted(e, n_d, 3 * i)
                    step(e.bn_stats(stats[:, 0, :], acc[:, bass.ds(i, 1), :].rearrange("p a c -> p (a c)")))
                    hold(e, ticks)
                    step(e.bn_aggr(mv1[:, :], stats[:, 0, :]))
                    step(e.tensor_copy(mv[:, bass.ds(i, 1), :].rearrange("p a c -> p (a c)"), mv1[:, :]))
                step = counted(e, n_d, 3 * TILES)
                step(e.tensor_scalar(rstd[:, :], mv[:, :, 1], 1e-5, None, ALU.add))
                e.sem_inc(n_v, 1)
                e.wait_ge(n_s, 1)
                step(e.reciprocal(rstd[:, :], std[:, :]))
                with e.Fori(0, TILES // 2) as pair:
                    i = pair * 2
                    for b in range(2):
                        e.wait_ge(n_t, i + b)
                        e.wait_ge(n_g, i + b)
                        e.tensor_scalar(xr[:, b, :], acc[:, bass.ds(i + b, 1), :].rearrange("p a c -> p (a c)"),
                                        mv[:, bass.ds(i + b, 1), 0], rstd[:, bass.ds(i + b, 1)],
                                        ALU.subtract, ALU.mult).then_inc(n_x, 1)

            @block.scalar
            def _(e):
                e.wait_ge(n_v, 1)
                e.activation(std[:, :], rstd[:, :], ACT.Sqrt).then_inc(n_s, 1)
                with e.Fori(0, TILES // 2) as pair:
                    i = pair * 2
                    for b in range(2):
                        e.wait_ge(n_x, i + b + 1)
                        e.activation(gm[:, bass.ds(i + b, 1), :].rearrange("p a c -> p (a c)"), xr[:, b, :], ACT.Copy).then_inc(n_g, 1)
                        e.wait_ge(n_t, i + b + 1)
                        e.activation(xnT[:, :, bass.ds((i + b) * PT, PT)], pt[b][:, :, 0:PT], ACT.Copy).then_inc(n_c, 1)

            @block.tensor
            def _(e):
                e.sem_inc(n_c, 2)
                with e.Fori(0, TILES // 2) as pair:
                    i = pair * 2
                    for b in range(2):
                        e.wait_ge(n_x, i + b + 1)
                        e.wait_ge(n_c, i + b + 1)
                        for k in range(KC):
                            last = e.transpose(pt[b][:, k, 0:PT], xr[:, b, k * P:(k + 1) * P], ident[0:PT, 0:PT])
                        last.then_inc(n_t, 1)

            @block.sync
            def _(e):
                if load is not None:
                    n = PT * (TILES - 1)
                    e.dma_start(acc[:, 0:TILES - 1, :], load[0:n, :].rearrange("(i p) c -> p i c", p=PT)).then_inc(n_in, 16)
                    e.wait_ge(n_z, 1)
                    e.dma_start(acc[0:LAST, TILES - 1, :], load[n:N, :]).then_inc(n_in, 16)
                    e.wait_ge(n_g, TILES)
                    e.dma_start(rows.rearrange("(i p) c -> p i c", p=PT), gm[:, :, :]).then_inc(n_o, 16)
                    e.wait_ge(n_c, TILES + 2)
                    e.dma_start(cols, xnT[:, :, :]).then_inc(n_o, 16)
                    e.wait_ge(n_o, 32)


def mix(nc, sem, A, acc, xnT, ident, ones):
    from contextlib import ExitStack
    for part in ("k", "q"):
        if part == "k":
            mctx = ExitStack()
            M = mctx.enter_context(nc.sbuf_tensor("moments", [P, HEADS * FCH, VD], F32))
            wts = mctx.enter_context(nc.sbuf_tensor("moment_weights", [P, FCH], F32))
            mask = mctx.enter_context(nc.sbuf_tensor("row_weight", [PT, TILES], F32))
        with ExitStack() as ctx:
            sem = scoped(nc, ctx)
            def sb(name, shape, dt=F32):
                return ctx.enter_context(nc.sbuf_tensor(f"mix{part}_{name}", shape, dt))

            def ps(name, shape):
                return ctx.enter_context(nc.psum_tensor(f"mix{part}_{name}", shape, F32))
            WN = 512 if part == "k" else 256
            col0 = 256 if part == "k" else 0
            w = sb("w", [P, KC, WN])
            wb = sb("wb", [1, WN])
            sq = sb("sq", [PT, C])
            ss = sb("ss", [PT, 4, HEADS])
            ext = sb("ext", [PT, HEADS, HD + HD // 2])
            F = sb("F", [PT, HEADS, FP])
            xs = sb("xs", [P, KC, PT])
            zero = sb("zero", [P, 512])
            pa = ps("proj", [PT, 512])
            S = {n: sem(f"mix{part}_{n}") for n in ("in", "set", "dve", "proj", "sq", "ss", "sqrt", "feat", "mm", "pfree", 
                                                    "turned", "evac", "y", "yo", "yt", "ytc", "o", "odone", "vset", "xs")}
            if part == "k":
                v1 = sb("v1", [PT, HEADS, VD])
                pm = [ps(f"pm{i}", [P, 15 * VD]) for i in range(3)]
            else:
                wp = sb("wp", [P, KC, C])
                bp = sb("bp", [1, C])
                temp = sb("temp", [PT, HEADS])
                FT = sb("FT", [P, HEADS * FCH, PT])
                yo = sb("yo", [PT, C])
                yr = sb("yr", [PT, HEADS])
                yT = sb("yT", [P, KC, PT])
                pt = [ps(f"pt{i}", [P, 4, PT]) for i in range(2)]
                py = ps("py", [PT, HEADS, VD])
                pyt = ps("pyt", [P, KC, PT])
                po = ps("po", [PT, C])

            def ext_window(ext):
                a = ext[:, :, :].ap
                return bass.AP(ext[:, :, :].tensor, ext[:, :, :].offset,
                               [list(a[0]), [HD + HD // 2, HEADS], [1, ND], [1, HD]])

            with nc.Block() as block:
                @block.gpsimd
                def _(e):
                    if part == "k":
                        e.memset(mask[:, :], 1.0 / N).then_inc(S["set"], 1)
                        e.wait_ge(S["set"], 1)
                        m = mask[:, TILES - 1:TILES]
                        e.affine_select(out=m, in_=m, compare_op=ALU.is_ge, fill=0.0, base=LAST - 1,
                                        pattern=[[0, 1]], channel_multiplier=-1).then_inc(S["set"], 1)

                @block.sync
                def _(e):
                    e.dma_start(w[:, :, :], A["WqkvT"].rearrange("(k p) n -> p k n", p=P)[:, :, col0:col0 + WN]).then_inc(S["in"], 16)
                    e.dma_start(wb[:, :], A["L0_mix_bqkv"].rearrange("(a n) -> a n", a=1)[:, col0:col0 + WN]).then_inc(S["in"], 16)
                    if part == "q":
                        e.dma_start(wp[:, :, :], A["WprojT"].rearrange("(k p) n -> p k n", p=P)).then_inc(S["in"], 16)
                        e.dma_start(bp[:, :], A["L0_mix_bproj"].rearrange("(a n) -> a n", a=1)).then_inc(S["in"], 16)
                        e.dma_start(temp[:, :], A["L0_mix_temperature"].rearrange("a h b c -> (a b c) h").to_broadcast([PT, HEADS])).then_inc(S["in"], 16)

                @block.scalar
                def _(e):
                    with e.Fori(0, TILES) as i:
                        e.wait_ge(S["proj"], i)
                        e.activation(xs[:, :, :], xnT[:, :, bass.ds(i * PT, PT)], ACT.Copy).then_inc(S["xs"], 1)
                        e.wait_ge(S["proj"], i + 1)
                        e.activation(sq[:, :], pa[:, 0:C], ACT.Square).then_inc(S["sq"], 1)
                        e.wait_ge(S["ss"], i + 1)
                        e.activation(ss[:, 1, :], ss[:, 0, :], ACT.Sqrt).then_inc(S["sqrt"], 1)
                        if part == "q":
                            for t in range(HEADS * FCH // 4):
                                e.wait_ge(S["turned"], i * (HEADS * FCH // 4) + t + 1)
                                if t == 0:
                                    e.wait_ge(S["y"], i)
                                e.activation(FT[:, 4 * t:4 * t + 4, :], pt[t % 2][:, :, :], ACT.Copy).then_inc(S["evac"], 1)
                            e.wait_ge(S["yt"], i + 1)
                            e.activation(yT[:, :, :], pyt[:, :, :], ACT.Copy).then_inc(S["ytc"], 1)

                @block.vector
                def _(e):
                    step = counted(e, S["vset"], 0)
                    step(e.memset(zero[:, :], 0.0))
                    step(e.memset(F[:, :, :], 0.0))
                    step(e.memset(F[:, :, FEAT - 1:FEAT], 1.0))
                    if part == "k":
                        e.wait_ge(S["set"], 2)
                        step(e.memset(ss[:, 3, :], 1.0))
                        step(e.memset(wts[:, 0:4], 1.0))
                        step(e.memset(wts[:, 4:5], SC ** 2))
                        step(e.memset(wts[0:32, 0:1], 0.5))
                        step(e.memset(wts[0:32, 4:5], 0.5))
                        step(e.memset(wts[64:96, 4:5], SC ** 4))
                    else:
                        e.wait_ge(S["in"], 16 * 5)
                        step(e.tensor_scalar(temp[:, :], temp[:, :], SC * SC, None, ALU.mult))
                    KS = 9 if part == "k" else 10
                    with e.Fori(0, TILES) as i:
                        step = counted(e, S["dve"], KS * i)
                        e.wait_ge(S["sq"], i + 1)
                        e.tensor_reduce(ss[:, 0, :], sq[:, :].rearrange("p (h d) -> p h d", h=HEADS), AX.X, ALU.add).then_inc(S["ss"], 1)
                        e.wait_ge(S["sqrt"], i + 1)
                        step(e.tensor_scalar(ss[:, 2, :], ss[:, 1, :], 1.0 if part == "k" else SC, 1e-12, ALU.mult, ALU.max))
                        step(e.reciprocal(ss[:, 2, :], ss[:, 2, :]))
                        if part == "k":
                            step(e.tensor_scalar(ss[:, 2, :], ss[:, 2, :], SC, None, ALU.mult))
                        else:
                            step(e.tensor_tensor(ss[:, 2, :], ss[:, 2, :], temp[:, :], ALU.mult))
                        kk = pa[:, 0:C].rearrange("p (h d) -> p h d", h=HEADS)
                        step(e.tensor_tensor(ext[:, :, 0:HD], kk, ss[:, 2, :].unsqueeze(2).to_broadcast([PT, HEADS, HD]), ALU.mult))
                        if part == "k":
                            e.wait_ge(S["mm"], i)
                            step(e.tensor_scalar(v1[:, :, 1:VD], pa[:, C:2 * C].rearrange("p (h d) -> p h d", h=HEADS), mask[:, bass.ds(i, 1)], None, ALU.mult))
                            step(e.tensor_scalar(v1[:, :, 0:1], ss[:, 3, :].unsqueeze(2), mask[:, bass.ds(i, 1)], None, ALU.mult))
                        else:
                            e.wait_ge(S["turned"], i * (HEADS * FCH // 4))
                        e.sem_inc(S["pfree"], 1)
                        step(e.tensor_copy(ext[:, :, HD:HD + HD // 2], ext[:, :, 0:HD // 2]))
                        step(e.tensor_copy(F[:, :, ND * HD:ND * HD + HD], ext[:, :, 0:HD]))
                        win = ext_window(ext)
                        for h in range(HEADS):
                            ins = e.tensor_tensor(F[:, h, 0:ND * HD].rearrange("p (d j) -> p d j", d=ND),
                                                  ext[:, h, 0:HD].unsqueeze(1).to_broadcast([PT, ND, HD]), win[:, h, :, :], ALU.mult)
                            if h < HEADS - 1:
                                continue
                            step(ins)
                        e.sem_inc(S["feat"], 1)
                        if part == "q":
                            e.wait_ge(S["y"], i + 1)
                            step(e.reciprocal(yr[:, :], py[:, :, 0]))
                            step(e.tensor_tensor(yo[:, :].rearrange("p (h d) -> p h d", h=HEADS), py[:, :, 1:VD],
                                                 yr[:, :].unsqueeze(2).to_broadcast([PT, HEADS, HD]), ALU.mult))
                            e.sem_inc(S["yo"], 1)
                            e.wait_ge(S["o"], i + 1)
                            a = acc[:, bass.ds(i, 1), :].rearrange("p a c -> p (a c)")
                            step(e.tensor_tensor(a, a, po[:, :], ALU.add))
                            e.sem_inc(S["odone"], 1)
                    if part == "k":
                        e.wait_ge(S["mm"], TILES)
                        for m in range(3):
                            n = min(15, HEADS * FCH - 15 * m)
                            ins = e.tensor_copy(M[:, 15 * m:15 * m + n, :], pm[m][:, 0:n * VD].rearrange("p (u e) -> p u e", e=VD))
                            ins.then_inc(S["odone"], 1)
                        e.wait_ge(S["odone"], 3)
                        for c in range(FCH):
                            v = M[:, c:HEADS * FCH:FCH, :]
                            e.tensor_scalar(v, v, wts[:, c:c + 1], None, ALU.mult).then_inc(S["odone"], 1)

                @block.tensor
                def _(e):
                    e.wait_ge(S["in"], 16 * (2 if part == "k" else 5))
                    e.wait_ge(S["vset"], 1)
                    if part == "k":
                        for m in range(3):
                            e.matmul(pm[m][:, :], zero[:, 0:P], zero[:, 0:15 * VD], start=True, stop=False, skip_group_check=True)
                    with e.Fori(0, TILES) as i:
                        e.wait_ge(S["pfree"], i)
                        e.wait_ge(S["xs"], i + 1)
                        for k in range(KC):
                            e.matmul(pa[:, 0:WN], xs[:, k, :], w[:, k, :], start=(k == 0), stop=False)
                        e.matmul(pa[:, 0:WN], ones[0:1, 0:PT], wb[:, :], start=False, stop=True).then_inc(S["proj"], 1)
                        e.wait_ge(S["feat"], i + 1)
                        if part == "k":
                            for u in range(HEADS * FCH):
                                h, c, j = u // FCH, u % FCH, u % 15
                                last = e.matmul(pm[u // 15][:, j * VD:(j + 1) * VD], F[:, h, c * P:(c + 1) * P], v1[:, h, :],
                                                start=False, stop=False, skip_group_check=True)
                            last.then_inc(S["mm"], 1)
                        else:
                            NTR = HEADS * FCH // 4
                            for t in range(NTR):
                                e.wait_ge(S["evac"], i * NTR + max(t - 1, 0))
                                for j in range(4):
                                    u = 4 * t + j
                                    last = e.transpose(pt[t % 2][:, j, :], F[:, u // FCH, (u % FCH) * P:(u % FCH + 1) * P], ident[0:PT, 0:PT])
                                last.then_inc(S["turned"], 1)
                            e.wait_ge(S["evac"], (i + 1) * NTR)
                            for h in range(HEADS):
                                for c in range(FCH):
                                    last = e.matmul(py[:, h, :], FT[:, h * FCH + c, :], M[:, h * FCH + c, :], start=(c == 0), stop=(c == FCH - 1))
                            last.then_inc(S["y"], 1)
                            e.wait_ge(S["yo"], i + 1)
                            for k in range(KC):
                                last = e.transpose(pyt[:, k, :], yo[:, k * P:(k + 1) * P], ident[0:PT, 0:PT])
                            last.then_inc(S["yt"], 1)
                            e.wait_ge(S["ytc"], i + 1)
                            for k in range(KC):
                                e.matmul(po[:, :], yT[:, k, :], wp[:, k, :], start=(k == 0), stop=False)
                            e.matmul(po[:, :], ones[0:1, 0:PT], bp[:, :], start=False, stop=True).then_inc(S["o"], 1)
    mctx.close()


def gnn_step(nc, sem, A, s, tables, cols, idx, keys, tab, iota_keys, tile_keys, ident, gm, xnT, ticks):
    from contextlib import ExitStack
    last_step = s == STEPS - 1
    with ExitStack() as ctx:
        sem = scoped(nc, ctx)
        def sb(name, shape, dt=F32):
            return ctx.enter_context(nc.sbuf_tensor(f"g{s}_{name}", shape, dt))

        def ps(name, shape):
            return ctx.enter_context(nc.psum_tensor(f"g{s}_{name}", shape, F32))
        names = ("w_in", "w_mm", "w_cp", "idx_ready", "onehot", "used", "tile_done", "tile_out", "keyed", "set",
                 "h_in", "h_free", "held", "pr", "pz", "pi", "ph", "r", "z", "t1", "t2", "n", "d", "hnew", "turn", "rows", "hsum",
                 "stored", "row_store", "col_store")
        S = {n: sem(f"g{s}_{n}") for n in names}
        landed = [nc.alloc_semaphore(f"g{s}_landed{r}") for r in range(R)]
        wc = sb("wc", [P, TYPES, KC, 3 * C])
        wh = sb("wh", [P, TYPES, KC, 3 * C])
        bi = sb("bi", [P, TYPES, 6])
        bh = sb("bh", [P, TYPES, 6])
        brz = sb("brz", [P, TYPES, 6])
        with ExitStack() as wctx:
            wm = wctx.enter_context(nc.sbuf_tensor(f"g{s}_wm", [P, TYPES, KC, C], F32))
            wi = wctx.enter_context(nc.sbuf_tensor(f"g{s}_wi", [P, TYPES, KC, 3 * C], F32))
            pw = [wctx.enter_context(nc.psum_tensor(f"g{s}_pw{i}", [P, 384], F32)) for i in range(2)]
            with nc.Block() as block:
                @block.sync
                def _(e):
                    for t in range(TYPES):
                        e.dma_start(wm[:, t, :, :], A["convT"][t, s].rearrange("(k p) n -> p k n", p=P)).then_inc(S["w_in"], 16)
                        e.dma_start(wi[:, t, :, :], A["wihT"][t].rearrange("(k p) n -> p k n", p=P)).then_inc(S["w_in"], 16)
                        e.dma_start(wh[:, t, :, :], A["whhT"][t].rearrange("(k p) n -> p k n", p=P)).then_inc(S["w_in"], 16)
                        e.dma_start(bi[:, t, :], A["bihT"][:, t, :]).then_inc(S["w_in"], 16)
                        e.dma_start(bh[:, t, :], A["bhhT"][:, t, :]).then_inc(S["w_in"], 16)

                @block.tensor
                def _(e):
                    e.wait_ge(S["w_in"], 16 * 15)
                    n = 0
                    for t in range(TYPES):
                        for m in range(KC):
                            for q in range(2):
                                if n >= 2:
                                    e.wait_ge(S["w_cp"], n - 1)
                                for k in range(KC):
                                    last = e.matmul(pw[n % 2][:, :], wm[:, t, k, m * P:(m + 1) * P], wi[:, t, k, q * 384:(q + 1) * 384], start=(k == 0), stop=(k == KC - 1))
                                last.then_inc(S["w_mm"], 1)
                                n += 1

                @block.vector
                def _(e):
                    e.wait_ge(S["w_in"], 16 * 15)
                    n = 0
                    for t in range(TYPES):
                        for m in range(KC):
                            for q in range(2):
                                n += 1
                                e.wait_ge(S["w_mm"], n)
                                e.tensor_copy(wc[:, t, m, q * 384:(q + 1) * 384], pw[(n - 1) % 2][:, :]).then_inc(S["w_cp"], 1)
                    e.tensor_tensor(brz[:, :, :], bi[:, :, :], bh[:, :, :], ALU.add)
        ring = sb("ring", [P, R, C])
        islot = [sb(f"islot{r}", [P, 1], I32) for r in range(R)]
        onehot = sb("onehot", [P, R, NKEY])
        zero = sb("zero", [1, 512])
        ah = sb("ah", [P, TYPES, KC, GW])
        hT = sb("hT", [P, TYPES, KC, GW])
        hn = sb("hn", [P, TYPES, KC, GW])
        rT = sb("rT", [P, GW])
        zT = sb("zT", [P, GW])
        t1 = sb("t1", [P, GW])
        nT = sb("nT", [P, GW])
        dT = sb("dT", [P, GW])
        hsum = sb("hsum", [P, KC, GW]) if last_step else None
        rowb = sb("rowb", [PT, 4, C])
        pagg = [ps(f"pagg{i}", [P, KC, TYPES, DT]) for i in range(2)]
        pr, pz, pi, ph = (ps(n, [P, GW]) for n in ("pr", "pz", "pi", "ph"))
        ptr = [ps(f"ptr{i}", [PT, 2, C]) for i in range(2)]
        NU = TYPES * KC
        TU = 1 if last_step else TYPES

        def tile_range(e, g, j):
            a = e.value_load(tab[0:1, bass.ds(g * TG + j, 1)], min_val=0, max_val=32000)
            b = e.value_load(tab[0:1, bass.ds(g * TG + j + 1, 1)], min_val=1, max_val=32000)
            return a, b

        def turn(e, g, t, src, ready, value, n):
            e.wait_ge(S[ready], value)
            for b in range(2):
                e.wait_ge(S["rows"], 2 * n)
                for c in range(2):
                    for k in range(KC):
                        mm = e.transpose(ptr[b][:, c, k * P:(k + 1) * P], src[:, k, (2 * b + c) * PT:(2 * b + c + 1) * PT], ident[:, :])
                mm.then_inc(S["turn"], 1)

        def rows_out(e, g, n):
            if not last_step:
                e.wait_ge(S["row_store"], 16 * n)
            for b in range(2):
                e.wait_ge(S["turn"], 2 * n + b + 1)
                if last_step:
                    e.activation(gm[:, bass.ds(g * 4 + 2 * b, 2), :], ptr[b][:, :, :], ACT.Copy).then_inc(S["rows"], 1)
                else:
                    e.activation(rowb[:, 2 * b:2 * b + 2, :], ptr[b][:, :, :], ACT.Copy).then_inc(S["rows"], 1)

        with nc.Block() as block:
            @block.gpsimd
            def _(e):
                with e.Fori(0, GROUPS) as g:
                    for j in range(TG):
                        q0, q1 = tile_range(e, g, j)
                        with e.Fori(q0, q1) as q:
                            for r in range(R):
                                e.wait_ge(S["idx_ready"], q * R + r + 1)
                                hold_pool(e, ticks, S["held"], q * R + r)
                                e.indirect_dma_start(ring[:, r, :], None, tables[s], bass.IndirectOffsetOnAxis(ap=islot[r][:, 0:1], axis=0)).then_inc(landed[r], 16)

            @block.sync
            def _(e):
                with e.Fori(0, GROUPS) as g:
                    e.wait_ge(S["h_free"], g * NU)
                    for t in range(TYPES):
                        src = cols[0] if s == 0 else cols[s][t]
                        e.dma_start(hT[:, t, :, :], src[:, :, bass.ds(g * GW, GW)]).then_inc(S["h_in"], 16)
                    if not last_step:
                        for t in range(TYPES):
                            e.wait_ge(S["hnew"], g * NU + KC * (t + 1))
                            e.dma_start(cols[s + 1][t][:, :, bass.ds(g * GW, GW)], hn[:, t, :, :]).then_inc(S["col_store"], 16)
                            e.wait_ge(S["rows"], 2 * (g * TYPES + t + 1))
                            e.dma_start(tables[s + 1][bass.ds(g * GW + t * NP, GW), :].rearrange("(a p) c -> p a c", p=PT), rowb[:, :, :]).then_inc(S["row_store"], 16)
                if not last_step:
                    e.wait_ge(S["row_store"], 16 * TYPES * GROUPS)
                    e.wait_ge(S["col_store"], 16 * TYPES * GROUPS)

            @block.tensor
            def _(e):
                e.sem_inc(S["used"], R)
                e.sem_inc(S["tile_out"], 2)
                e.wait_ge(S["set"], 1)
                with e.Fori(0, GROUPS) as g:
                    for j in range(TG):
                        q0, q1 = tile_range(e, g, j)
                        pg = pagg[j % 2]
                        e.wait_ge(S["tile_out"], (g * TG + j + 1) if j != 0 else (g * TG + 2))
                        e.matmul(pg[:, :, :, :].rearrange("p k t d -> p (k t d)"), zero[0:1, 0:P], zero[0:1, 0:KC * NKEY], start=True, stop=False, skip_group_check=True)
                        with e.Fori(q0, q1) as q:
                            for r in range(R):
                                e.wait_ge(landed[r], q * 16 + 16)
                                e.wait_ge(S["onehot"], q * R + r + 1)
                                for k in range(KC):
                                    mm = e.matmul(pg[:, k, :, :].rearrange("p t d -> p (t d)"), ring[:, r, k * P:(k + 1) * P], onehot[:, r, :], start=False, stop=False, skip_group_check=True)
                                mm.then_inc(S["used"], 1)
                        e.matmul(pg[:, :, :, :].rearrange("p k t d -> p (k t d)"), zero[0:1, 0:P], zero[0:1, 0:KC * NKEY], start=False, stop=True, skip_group_check=True).then_inc(S["tile_done"], 1)
                    e.wait_ge(S["tile_out"], (g + 1) * TG + 2)
                    e.wait_ge(S["h_in"], (g + 1) * 16 * TYPES)
                    for t in range(TYPES):
                        for m in range(KC):
                            u = t * KC + m

                            def product(p, gate, parts, done, free):
                                e.wait_ge(S[free], g * NU + u)
                                o = gate * C + m * P
                                steps = [(w, x, k) for w, x in parts for k in range(KC)]
                                for n, (w, x, k) in enumerate(steps):
                                    mm = e.matmul(p[:, :], w[:, t, k, o:o + P], x[:, t, k, :], start=(n == 0), stop=(n == len(steps) - 1))
                                mm.then_inc(S[done], 1)
                            product(pr, 0, [(wc, ah), (wh, hT)], "pr", "r")
                            product(ph, 2, [(wh, hT)], "ph", "t1")
                            product(pi, 2, [(wc, ah)], "pi", "t2")
                            product(pz, 1, [(wc, ah), (wh, hT)], "pz", "z")
                        if not last_step:
                            turn(e, g, t, hn[:, t, :, :], "hnew", g * NU + KC * (t + 1), g * TYPES + t)
                    if last_step:
                        turn(e, g, 0, hsum[:, :, :], "hsum", (g + 1) * NU, g)

            @block.scalar
            def _(e):
                with e.Fori(0, GROUPS) as g:
                    for j in range(TG):
                        w = DT if j < TG - 1 else DTL
                        if j == 0:
                            e.wait_ge(S["pz"], g * NU)
                        e.wait_ge(S["tile_done"], g * TG + j + 1)
                        e.activation(ah[:, :, :, j * DT:j * DT + w], pagg[j % 2][:, :, :, 0:w].rearrange("p k t d -> p t k d"), ACT.Copy).then_inc(S["tile_out"], 1)
                    for t in range(TYPES):
                        for m in range(KC):
                            u = t * KC + m
                            U = g * NU + u
                            e.wait_ge(S["pr"], U + 1)
                            e.wait_ge(S["t1"], U)
                            e.activation(rT[:, :], pr[:, :], ACT.Sigmoid, bias=brz[:, t, m:m + 1]).then_inc(S["r"], 1)
                            e.wait_ge(S["t2"], U + 1)
                            e.wait_ge(S["hnew"], U)
                            e.activation(nT[:, :], t1[:, :], ACT.Tanh, bias=bi[:, t, 4 + m:5 + m]).then_inc(S["n"], 1)
                            e.wait_ge(S["pz"], U + 1)
                            e.activation(zT[:, :], pz[:, :], ACT.Sigmoid, bias=brz[:, t, 2 + m:3 + m]).then_inc(S["z"], 1)
                        if not last_step:
                            rows_out(e, g, g * TYPES + t)
                    if last_step:
                        rows_out(e, g, g)

            @block.vector
            def _(e):
                e.memset(zero[:, :], 0.0).then_inc(S["set"], 1)
                e.tensor_scalar(tile_keys[:, :, :], iota_keys[:, :, :], -float(DTL), None, ALU.add).then_inc(S["keyed"], 1)
                with e.Fori(0, GROUPS) as g:
                    for j in range(TG):
                        q0, q1 = tile_range(e, g, j)
                        first = e.value_load(tab[0:1, bass.ds(g * TG + j + 80, 1)], min_val=0, max_val=400)
                        e.wait_ge(S["keyed"], g * TG + j + 1)
                        e.tensor_scalar(tile_keys[:, :, :], tile_keys[:, :, :], float(DT if j else DTL), None, ALU.add).then_inc(S["keyed"], 1)
                        e.wait_ge(S["keyed"], g * TG + j + 2)
                        hold(e, ticks)
                        with e.Fori(q0, q1) as q:
                            for r in range(R):
                                c = nc.s_assert_within((q - q0) * R + first + r, 0, NCH - 1, skip_runtime_bounds_check_because="a tile has at most all the chunks, and R - 1 more")
                                e.wait_ge(S["used"], q * R + r + 1)
                                e.tensor_copy(islot[r][:, :], idx[:, bass.ds(c, 1)]).then_inc(S["idx_ready"], 1)
                                e.tensor_scalar(onehot[:, r, :], tile_keys[:, :, :].rearrange("p t d -> p (t d)"), keys[:, bass.ds(c, 1)], None, ALU.is_equal).then_inc(S["onehot"], 1)
                    for t in range(TYPES):
                        for m in range(KC):
                            u = t * KC + m
                            U = g * NU + u
                            e.wait_ge(S["ph"], U + 1)
                            e.wait_ge(S["r"], U + 1)
                            e.wait_ge(S["n"], U)
                            e.scalar_tensor_tensor(out=t1[:, :], in0=ph[:, :], scalar=bh[:, t, 4 + m:5 + m], in1=rT[:, :], op0=ALU.add, op1=ALU.mult).then_inc(S["t1"], 1)
                            e.wait_ge(S["t1"], U + 1)
                            e.wait_ge(S["pi"], U + 1)
                            e.tensor_tensor(t1[:, :], t1[:, :], pi[:, :], ALU.add).then_inc(S["t2"], 1)
                            e.wait_ge(S["n"], U + 1)
                            e.wait_ge(S["h_in"], (g + 1) * 16 * TYPES)
                            e.tensor_tensor(dT[:, :], hT[:, t, m, :], nT[:, :], ALU.subtract).then_inc(S["d"], 1)
                            e.wait_ge(S["d"], 2 * U + 1)
                            e.wait_ge(S["z"], U + 1)
                            e.tensor_tensor(dT[:, :], dT[:, :], zT[:, :], ALU.mult).then_inc(S["d"], 1)
                            e.wait_ge(S["d"], 2 * U + 2)
                            if not last_step:
                                if u == 0:
                                    e.wait_ge(S["col_store"], g * 16 * TYPES)
                                    e.wait_ge(S["turn"], g * 2 * TYPES)
                                e.tensor_tensor(hn[:, t, m, :], dT[:, :], nT[:, :], ALU.add).then_inc(S["hnew"], 1)
                            else:
                                e.tensor_tensor(hn[:, t, m, :], dT[:, :], nT[:, :], ALU.add).then_inc(S["hnew"], 1)
                                e.wait_ge(S["hnew"], U + 1)
                                if u == 0:
                                    e.wait_ge(S["turn"], 2 * g)
                                prev = xnT[:, m, bass.ds(g * GW, GW)] if t == 0 else hsum[:, m, :]
                                e.tensor_tensor(hsum[:, m, :], prev, hn[:, t, m, :], ALU.add).then_inc(S["hsum"], 1)
                                e.wait_ge(S["hsum"], U + 1)
                            if u == NU - 1:
                                e.wait_ge(S["pz"], U + 1)
                            e.sem_inc(S["h_free"], 1)


def gnn_out(nc, sem, A, acc, gm, ticks):
    from contextlib import ExitStack
    with ExitStack() as ctx:
        sem = scoped(nc, ctx)
        def sb(name, shape, dt=F32):
            return ctx.enter_context(nc.sbuf_tensor(f"go_{name}", shape, dt))
        gam = sb("gamma", [PT, C])
        bet = sb("beta", [PT, C])
        stats = sb("stats", [PT, 6])
        mv = sb("mv", [PT, TILES, 2])
        mv1 = sb("mv1", [PT, 2])
        std = sb("std", [PT, TILES])
        rstd = sb("rstd", [PT, TILES])
        w = sb("work", [PT, C])
        o_in, o_d, o_v, o_s = (sem(f"go_{n}") for n in ("loaded", "dve", "var", "std"))

        def row(t, i):
            return t[:, bass.ds(i, 1), :].rearrange("p a c -> p (a c)")
        with nc.Block() as block:
            @block.sync
            def _(e):
                e.dma_start(gam[:, :], A["L0_gnn_ln_gamma"].rearrange("(a c) -> a c", a=1).to_broadcast([PT, C])).then_inc(o_in, 16)
                e.dma_start(bet[:, :], A["L0_gnn_ln_beta"].rearrange("(a c) -> a c", a=1).to_broadcast([PT, C])).then_inc(o_in, 16)

            @block.scalar
            def _(e):
                e.wait_ge(o_v, 1)
                e.activation(std[:, :], rstd[:, :], ACT.Sqrt).then_inc(o_s, 1)

            @block.vector
            def _(e):
                with e.Fori(0, TILES) as i:
                    step = counted(e, o_d, 3 * i)
                    step(e.bn_stats(stats[:, :], row(gm, i)))
                    hold(e, ticks)
                    step(e.bn_aggr(mv1[:, :], stats[:, :]))
                    step(e.tensor_copy(row(mv, i), mv1[:, :]))
                step = counted(e, o_d, 3 * TILES)
                step(e.tensor_scalar(rstd[:, :], mv[:, :, 1], 1e-5, None, ALU.add))
                e.sem_inc(o_v, 1)
                e.wait_ge(o_s, 1)
                step(e.reciprocal(rstd[:, :], std[:, :]))
                e.wait_ge(o_in, 32)
                with e.Fori(0, TILES) as i:
                    step = counted(e, o_d, 3 * TILES + 2 + 5 * i)
                    step(e.tensor_scalar(w[:, :], row(gm, i), mv[:, bass.ds(i, 1), 0], rstd[:, bass.ds(i, 1)], ALU.subtract, ALU.mult))
                    step(e.tensor_tensor(w[:, :], w[:, :], gam[:, :], ALU.mult))
                    step(e.tensor_tensor(w[:, :], w[:, :], bet[:, :], ALU.add))
                    step(e.scalar_tensor_tensor(out=w[:, :], in0=w[:, :], scalar=0.1, in1=w[:, :], op0=ALU.mult, op1=ALU.max))
                    step(e.tensor_tensor(row(acc, i), row(acc, i), w[:, :], ALU.add))


def ffn(nc, sem, A, acc, xnT, ident, ones, out, ticks):
    from contextlib import ExitStack
    with ExitStack() as ctx:
        sem = scoped(nc, ctx)
        def sb(name, shape, dt=F32):
            return ctx.enter_context(nc.sbuf_tensor(f"f_{name}", shape, dt))
        gate = sb("gate", [PT, TILES, XPT])
        b1 = sb("b1", [P, XPT, HC])
        with ExitStack() as gctx:
            def gsb(name, shape, dt=F32):
                return gctx.enter_context(nc.sbuf_tensor(f"fg_{name}", shape, dt))

            def gps(name, shape):
                return gctx.enter_context(nc.psum_tensor(f"fg_{name}", shape, F32))
            wg, bg, b2 = gsb("wg", [P, KC, XPT]), gsb("bg", [1, XPT]), gsb("b2", [XPT, C])
            xs, gT = gsb("xs", [P, KC, PT]), gsb("gT", [XPT, PT])
            lg, top = gsb("lg", [PT, XPT]), gsb("top", [PT, 8])
            at = gsb("at", [PT, 8], mybir.dt.uint32)
            atf, ew = gsb("atf", [PT, 8]), gsb("ew", [PT, 4])
            io_i, io = gsb("io_i", [PT, XPT], I32), gsb("io", [PT, XPT])
            g1, g2 = gsb("g1", [PT, XPT]), gsb("g2", [PT, XPT])
            pl, pg, pb = gps("pl", [PT, XPT]), gps("pg", [XPT, PT]), gps("pb", [PT, C])
            f_in, f_xs, f_l, f_d, f_g, f_t, f_tc, f_b, f_e, f_io, f_df = (sem(f"gate_{n}") for n in (
                "loaded", "x", "logits", "dve", "weights", "turned", "copied", "bias", "exp", "iota", "diff"))
            KS = 10
            with nc.Block() as block:
                @block.sync
                def _(e):
                    e.dma_start(wg[:, :, :], A["L0_ffn_Wg"].rearrange("(k p) n -> p k n", p=P)).then_inc(f_in, 16)
                    e.dma_start(bg[:, :], A["L0_ffn_bg"].rearrange("(a n) -> a n", a=1)).then_inc(f_in, 16)
                    e.dma_start(b2[:, :], A["L0_ffn_b2"]).then_inc(f_in, 16)
                    e.dma_start(b1[:, :, :], A["b1T"]).then_inc(f_in, 16)
                    e.wait_ge(f_in, 64)

                @block.gpsimd
                def _(e):
                    e.iota(io_i[:, :], [[1, XPT]], base=0, channel_multiplier=0).then_inc(f_io, 1)

                @block.scalar
                def _(e):
                    with e.Fori(0, TILES) as i:
                        e.wait_ge(f_l, i)
                        e.activation(xs[:, :, :], xnT[:, :, bass.ds(i * PT, PT)], ACT.Copy).then_inc(f_xs, 1)
                        e.wait_ge(f_df, i + 1)
                        e.activation(ew[:, 1:2], ew[:, 0:1], ACT.Exp).then_inc(f_e, 1)
                        e.wait_ge(f_t, i + 1)
                        e.activation(gT[:, :], pg[:, :], ACT.Copy).then_inc(f_tc, 1)

                @block.tensor
                def _(e):
                    e.wait_ge(f_in, 64)
                    with e.Fori(0, TILES) as i:
                        e.wait_ge(f_xs, i + 1)
                        e.wait_ge(f_d, i * KS)
                        for k in range(KC):
                            e.matmul(pl[:, :], xs[:, k, :], wg[:, k, :], start=(k == 0), stop=False)
                        e.matmul(pl[:, :], ones[0:1, 0:PT], bg[:, :], start=False, stop=True).then_inc(f_l, 1)
                        e.wait_ge(f_g, i + 1)
                        e.transpose(pg[:, :], g1[:, :], ident[0:PT, 0:PT]).then_inc(f_t, 1)
                        e.wait_ge(f_tc, i + 1)
                        e.matmul(pb[:, :], gT[:, :], b2[:, :], start=True, stop=True).then_inc(f_b, 1)

                @block.vector
                def _(e):
                    e.wait_ge(f_io, 1)
                    e.tensor_copy(io[:, :], io_i[:, :]).then_inc(f_io, 1)
                    e.wait_ge(f_io, 2)
                    with e.Fori(0, TILES) as i:
                        step = counted(e, f_d, i * KS)
                        e.wait_ge(f_l, i + 1)
                        step(e.tensor_copy(lg[:, :], pl[:, :]))
                        hold(e, ticks)
                        step(e.max(top[:, :], lg[:, :]))
                        hold(e, ticks)
                        step(e.max_index(at[:, :], top[:, :], lg[:, :]))
                        step(e.tensor_copy(atf[:, :], at[:, :]))
                        e.tensor_tensor(ew[:, 0:1], top[:, 1:2], top[:, 0:1], ALU.subtract).then_inc(f_df, 1)
                        e.wait_ge(f_e, i + 1)
                        step(e.tensor_scalar(ew[:, 2:3], ew[:, 1:2], 1.0, None, ALU.add))
                        step(e.reciprocal(ew[:, 2:3], ew[:, 2:3]))
                        step(e.tensor_tensor(ew[:, 3:4], ew[:, 1:2], ew[:, 2:3], ALU.mult))
                        step(e.tensor_scalar(g1[:, :], io[:, :], atf[:, 0:1], ew[:, 2:3], ALU.is_equal, ALU.mult))
                        step(e.tensor_scalar(g2[:, :], io[:, :], atf[:, 1:2], ew[:, 3:4], ALU.is_equal, ALU.mult))
                        e.tensor_tensor(g1[:, :], g1[:, :], g2[:, :], ALU.add).then_inc(f_g, 1)
                        e.wait_ge(f_g, i + 1)
                        e.tensor_copy(gate[:, bass.ds(i, 1), :].rearrange("p a x -> p (a x)"), g1[:, :])
                        e.wait_ge(f_b, i + 1)
                        a = acc[:, bass.ds(i, 1), :].rearrange("p a c -> p (a c)")
                        step(e.tensor_tensor(a, a, pb[:, :], ALU.add))
        w1 = sb("w1", [P, 2, KC, HID])
        w2 = sb("w2", [P, 2, HC, C])
        hid = sb("hid", [P, HC, GW])
        p1 = [ctx.enter_context(nc.psum_tensor(f"f_p1{i}", [P, GW], F32)) for i in range(4)]
        p2 = [ctx.enter_context(nc.psum_tensor(f"f_p2{i}", [PT, C], F32)) for i in range(4)]
        x_in = [sem(f"ffn_weights{i}") for i in range(2)]
        x_p1, x_h, x_p2, x_a, x_o = (sem(f"ffn_{n}") for n in ("hidden_sum", "hidden", "expert_sum", "added", "stored"))
        with nc.Block() as block:
            @block.sync
            def _(e):
                for x in range(XPT):
                    if x >= 2:
                        e.wait_ge(x_p2, (x - 1) * TILES)
                    e.dma_start(w1[:, x % 2, :, :], A["L0_ffn_W1"][x].rearrange("(k p) n -> p k n", p=P)).then_inc(x_in[x % 2], 16)
                    e.dma_start(w2[:, x % 2, :, :], A["L0_ffn_W2"][x].rearrange("(k p) n -> p k n", p=P)).then_inc(x_in[x % 2], 16)
                e.wait_ge(x_a, XPT * TILES + 4)
                n = PT * (TILES - 1)
                e.dma_start(out[0:n, :].rearrange("(i p) c -> p i c", p=PT), acc[:, 0:TILES - 1, :]).then_inc(x_o, 16)
                e.dma_start(out[n:N, :], acc[0:LAST, TILES - 1, :]).then_inc(x_o, 16)
                e.wait_ge(x_o, 32)

            @block.tensor
            def _(e):
                e.sem_inc(x_h, 4)
                e.sem_inc(x_a, 4)
                for x in range(XPT):
                    e.wait_ge(x_in[x % 2], 32 * (x // 2 + 1))
                    with e.Fori(0, GROUPS) as g:
                        for m in range(HC):
                            e.wait_ge(x_h, (x * GROUPS + g) * HC + m + 1)
                            for k in range(KC):
                                mm = e.matmul(p1[m % 4][:, :], w1[:, x % 2, k, m * P:(m + 1) * P], xnT[:, k, bass.ds(g * GW, GW)], start=(k == 0), stop=(k == KC - 1))
                            mm.then_inc(x_p1, 1)
                        e.wait_ge(x_h, (x * GROUPS + g + 1) * HC + 4)
                        for c in range(4):
                            e.wait_ge(x_a, (x * GROUPS + g) * 4 + c + 1)
                            for m in range(HC):
                                mm = e.matmul(p2[c][:, :], hid[:, m, c * PT:(c + 1) * PT], w2[:, x % 2, m, :], start=(m == 0), stop=(m == HC - 1))
                            mm.then_inc(x_p2, 1)

            @block.scalar
            def _(e):
                for x in range(XPT):
                    with e.Fori(0, GROUPS) as g:
                        for m in range(HC):
                            e.wait_ge(x_p1, (x * GROUPS + g) * HC + m + 1)
                            if m == 0:
                                e.wait_ge(x_p2, (x * GROUPS + g) * 4)
                            e.activation(hid[:, m, :], p1[m % 4][:, :], ACT.Gelu, bias=b1[:, x, m:m + 1]).then_inc(x_h, 1)

            @block.vector
            def _(e):
                for x in range(XPT):
                    with e.Fori(0, GROUPS) as g:
                        for c in range(4):
                            e.wait_ge(x_p2, (x * GROUPS + g) * 4 + c + 1)
                            a = acc[:, bass.ds(g * 4 + c, 1), :].rearrange("p a c -> p (a c)")
                            e.scalar_tensor_tensor(out=a, in0=p2[c][:, :], scalar=gate[:, bass.ds(g * 4 + c, 1), x], in1=a, op0=ALU.mult, op1=ALU.add).then_inc(x_a, 1)


def kernel(**inputs):
    import numpy as _np
    import concourse.bacc as _bacc
    from concourse import mybir as _mybir
    from concourse.bass_utils import run_bass_kernel_spmd as _run

    i = {k: _np.asarray(v) for k, v in inputs.items()}
    laid = {n: i[n] for n in ("x", "src", "dst", "edge_type_3", "L0_gnn_ln_gamma", "L0_gnn_ln_beta", "L0_mix_bqkv",
                              "L0_mix_bproj", "L0_mix_temperature", "L0_ffn_Wg", "L0_ffn_bg", "L0_ffn_W1",
                              "L0_ffn_W2", "L0_ffn_b2")}
    laid["convT"] = i["L0_gnn_conv_w"].transpose(0, 1, 3, 2)
    laid["wihT"] = i["L0_gnn_gru_wih"].transpose(0, 2, 1)
    laid["whhT"] = i["L0_gnn_gru_whh"].transpose(0, 2, 1)
    laid["bihT"] = i["L0_gnn_gru_bih"].reshape(3, 6, 128).transpose(2, 0, 1)
    laid["bhhT"] = i["L0_gnn_gru_bhh"].reshape(3, 6, 128).transpose(2, 0, 1)
    laid["WqkvT"] = i["L0_mix_Wqkv"].T
    laid["WprojT"] = i["L0_mix_Wproj"].T
    laid["b1T"] = i["L0_ffn_b1"].reshape(8, 8, 128).transpose(2, 0, 1)
    nc = _bacc.Bacc("TRN2", target_bir_lowering=False, num_devices=1)
    arrays, A = {}, {}
    for name, a in laid.items():
        a = _np.ascontiguousarray(a)
        arrays[f"in_{name}"] = a
        A[name] = nc.dram_tensor(f"in_{name}", a.shape, _mybir.dt.from_np(a.dtype), kind="ExternalInput").ap()
    A["out"] = nc.dram_tensor("out_0", (3125, 256), F32, kind="ExternalOutput").ap()
    gps_layer_kernel(nc, A)
    r = _run(nc, [arrays], core_ids=[0])
    return r.results[0]["out_0"]
```

```python
import concourse.bass as bass
from concourse import mybir
from contextlib import ExitStack

F32 = mybir.dt.float32
F16 = mybir.dt.float16
BF16 = mybir.dt.bfloat16
I16 = mybir.dt.int16
I32 = mybir.dt.int32
ALU = mybir.AluOpType
ACT = mybir.ActivationFunctionType
AX = mybir.AxisListType

N, C, E = 3125, 256, 50000
STEPS, TYPES = 3, 3
P = 128
KC = C // P
PT = 112
TILES = 28
NP = PT * TILES
GW = 4 * PT
GROUPS = NP // GW
LAST = N - PT * (TILES - 1)
DT = 64
TG = GW // DT
NT = GROUPS * TG
NKEY = TYPES * DT
TYPEKEY = 4096
NODST = 4000
EROWS = E // P
EREST = E - EROWS * P
EB = 4
NCH = EB * P
DEEP = 32
R = 8
HEADS, HD = 8, 32
ND = HD // 2 + 1
FEAT = ND * HD + HD + 1
FCH = (FEAT + P - 1) // P
FP = FCH * P
VD = HD + 1
SC = float(HD) ** 0.25
XPT, HID = 8, 1024
HC = HID // P


def counted(eng, sem, base):
    count = [0]

    def step(ins):
        count[0] += 1
        ins.then_inc(sem, 1)
        eng.wait_ge(sem, base + count[0])
        return count[0]
    return step


def hold(e, ticks):
    e.tensor_copy(ticks[0][0:1, 1:2], ticks[0][0:1, 0:1])


def hold_pool(e, ticks, held, n):
    e.wait_ge(held, n)
    t = ticks[1]
    e.tensor_tensor(t[0:1, 1:2], t[0:1, 0:1], t[0:1, 0:1], ALU.add).then_inc(held, 1)


def scoped(nc, ctx):
    mine = []

    def sem(name):
        mine.append(nc.alloc_semaphore(name))
        return mine[-1]

    def give_back():
        nc.clear_and_free_semaphores(mine)
        nc.all_engine_barrier()
    ctx.callback(give_back)
    return sem


def gps_layer_kernel(nc, A):
    def sb(name, shape, dt=F32):
        return nc.alloc_sbuf_tensor(name, shape, dt)

    sem = nc.alloc_semaphore
    out = A["out"]
    table0 = nc.dram_tensor("xn_rows", [NP, 2 * C], F16).ap()
    tables = [table0] + [nc.dram_tensor(f"h_rows{s}", [TYPES * NP, 2 * C], F16).ap() for s in (1, 2)]
    hT0 = nc.dram_tensor("xn_cols", [P, KC, NP], F32).ap()
    hTs = [nc.dram_tensor(f"h_cols{s}", [TYPES, P, KC, NP], F32).ap() for s in (1, 2)]

    sums = nc.dram_tensor("h_sums", [NP, C], F32).ap()
    acc = sb("acc", [PT, TILES, C])
    ident = sb("ident", [P, P])
    ones = sb("ones", [1, 512])
    keys = sb("keys", [P, NCH])
    idx0 = sb("idx0", [P, NCH], I32)
    idx1 = sb("idx1", [P, NCH], I32)
    tab = sb("tab", [1, 160], I32)
    iota_keys = sb("iota_keys", [P, TYPES, DT], I16)
    tile_keys = sb("tile_keys", [P, TYPES, DT], I16)
    s_z = sem("const_zeroed")
    s_c = sem("const_ready")
    cdve = sem("const_dve")
    iota_i = sb("iota_i", [P, TYPES, DT], I32)
    nc_ticks = sb("tick_d", [1, 2]), sb("tick_p", [1, 2])
    with nc.Block() as block:
        @block.gpsimd
        def _(e):
            e.memset(ident[:, :], 0.0).then_inc(s_z, 1)
            e.wait_ge(s_z, 1)
            e.affine_select(out=ident[:, :], in_=ident[:, :], compare_op=ALU.not_equal, fill=1.0,
                            base=0, pattern=[[-1, P]], channel_multiplier=1).then_inc(s_c, 1)
            e.memset(ones[:, :], 1.0).then_inc(s_c, 1)
            e.iota(iota_i[:, :, :], [[TYPEKEY, TYPES], [1, DT]], base=0, channel_multiplier=0).then_inc(s_c, 1)

        @block.vector
        def _(e):
            for t in nc_ticks:
                e.memset(t[:, :], 0.0)
            e.wait_ge(s_c, 3)
            e.tensor_copy(iota_keys[:, :, :], iota_i[:, :, :]).then_inc(cdve, 1)
            e.wait_ge(cdve, 1)

    edge_tables(nc, A, ident, keys, idx0, idx1, tab)
    with nc.sbuf_tensor("xnT", [P, KC, NP], F32) as xnT:
        normalise(nc, "in", acc, xnT, ident, nc_ticks, load=A["x"], rows=table0, cols=hT0)
        mix(nc, A, acc, xnT, ident, ones)
    for s in range(STEPS):
        gnn_step(nc, A, s, tables, [hT0] + hTs, idx0 if s == 0 else idx1, keys, tab,
                 iota_keys, tile_keys, ident, sums, nc_ticks)
    gnn_out(nc, A, acc, sums, nc_ticks)
    with nc.sbuf_tensor("xfT", [P, KC, NP], F32) as xfT:
        normalise(nc, "ffn", acc, xfT, ident, nc_ticks)
        ffn(nc, A, acc, xfT, ident, ones, out, nc_ticks)


def edge_tables(nc, A, ident, keys, idx0, idx1, tab):
    with ExitStack() as ctx:
        sem = scoped(nc, ctx)
        def sb(name, shape, dt=F32):
            return ctx.enter_context(nc.sbuf_tensor(name, shape, dt))

        def ps(name, shape):
            return ctx.enter_context(nc.psum_tensor(name, shape, F32))
        ei = sb("ei", [P, 3, EB, P], I32)
        ef = sb("ef", [P, 3, EB, P])
        rows = sb("rows", [P, 3, EB, P])
        lim = sb("lim", [P, 2, EB])
        bcast = sb("lim_bcast", [P, 2, EB, NT])
        onesm = sb("onesm", [P, NT])
        base_i = sb("base_i", [1, NT], I32)
        base_r = sb("base_r", [1, NT])
        tlo = sb("tlo", [NT, 1])
        thi = sb("thi", [NT, 1])
        cio_i = sb("cio_i", [NT, NCH], I32)
        cio = sb("cio", [NT, NCH])
        member = sb("member", [NT, NCH])
        work = sb("work", [NT, NCH])
        col = sb("col", [NT, 8])
        col_i = sb("col_i", [NT, 1], I32)
        tri = sb("tri", [NT, NT + 1])
        pt = [ps(f"et{i}", [P, EB, P]) for i in range(3)]
        pl = [ps(f"el{i}", [NT, NCH]) for i in range(2)]
        pb = ps("eb", [NT, 1])
        pr = ps("er", [1, 256])
        e_set, e_in, e_io, e_d, e_row, e_t, e_lim, e_pl, e_n, e_r = (sem(f"edge_{n}") for n in (
            "set", "loaded", "iota", "dve", "rows", "turned", "limits", "limits_turned", "counts", "table"))
        with nc.Block() as block:
            @block.sync
            def _(e):
                e.wait_ge(e_set, 3)
                for k, name in enumerate(("src", "dst", "edge_type_3")):
                    a = A[name]
                    for b in range(3):
                        e.dma_start(ei[:, k, b, :], a[b * P * P:(b + 1) * P * P].rearrange("(r q) -> r q", q=P)).then_inc(e_in, 16)
                    n = EROWS - 3 * P
                    e.dma_start(ei[0:n, k, 3, :], a[3 * P * P:EROWS * P].rearrange("(r q) -> r q", q=P)).then_inc(e_in, 16)
                    e.dma_start(ei[n:n + 1, k, 3, 0:EREST], a[EROWS * P:E].rearrange("(r q) -> r q", r=1)).then_inc(e_in, 16)

            @block.gpsimd
            def _(e):
                e.iota(base_i[:, :], [[DT, NT]], base=0, channel_multiplier=0).then_inc(e_io, 1)
                e.iota(cio_i[:, :], [[1, NCH]], base=0, channel_multiplier=0).then_inc(e_io, 1)
                e.memset(tri[:, :], 1.0).then_inc(e_io, 1)
                e.wait_ge(e_io, 3)
                e.affine_select(out=tri[:, :], in_=tri[:, :], compare_op=ALU.is_gt, fill=0.0,
                                base=0, pattern=[[1, NT + 1]], channel_multiplier=-1).then_inc(e_io, 1)

            @block.vector
            def _(e):
                step = counted(e, e_d, 0)
                e.memset(ei[:, 0, 3, :], 0).then_inc(e_set, 1)
                e.memset(ei[:, 1, 3, :], NODST).then_inc(e_set, 1)
                e.memset(ei[:, 2, 3, :], 0).then_inc(e_set, 1)
                e.memset(onesm[:, :], 1.0)
                e.wait_ge(e_in, 16 * 15)
                step(e.tensor_copy(ef[:, :, :, :], ei[:, :, :, :]))
                e.tensor_copy(rows[:, 0, :, :], ef[:, 0, :, :]).then_inc(e_row, 1)
                e.scalar_tensor_tensor(out=rows[:, 1, :, :], in0=ef[:, 2, :, :], scalar=float(NP), in1=ef[:, 0, :, :], op0=ALU.mult, op1=ALU.add).then_inc(e_row, 1)
                e.scalar_tensor_tensor(out=rows[:, 2, :, :], in0=ef[:, 2, :, :], scalar=float(TYPEKEY), in1=ef[:, 1, :, :], op0=ALU.mult, op1=ALU.add).then_inc(e_row, 1)
                step(e.tensor_reduce(lim[:, 0, :], ef[:, 1, :, :], AX.X, ALU.min))
                step(e.tensor_reduce(lim[:, 1, :], ef[:, 1, :, :], AX.X, ALU.max))
                for k in range(2):
                    for b in range(EB):
                        e.tensor_scalar(bcast[:, k, b, :], onesm[:, :], lim[:, k, b:b + 1], None, ALU.mult).then_inc(e_lim, 1)
                e.wait_ge(e_io, 4)
                step(e.tensor_copy(base_r[:, :], base_i[:, :]))
                e.tensor_copy(cio[:, :], cio_i[:, :]).then_inc(e_lim, 1)
                e.wait_ge(e_t, 3)
                for k, t in enumerate((idx0, idx1, keys)):
                    e.tensor_copy(t[:, :], pt[k][:, :, :].rearrange("p a b -> p (a b)")).then_inc(e_row, 1)
                e.wait_ge(e_pl, 3)
                step(e.tensor_copy(tlo[:, :], pb[:, :]))
                step(e.tensor_scalar(thi[:, :], tlo[:, :], float(DT - 1), None, ALU.add))
                step(e.tensor_scalar(work[:, :], pl[0][:, :], thi[:, 0:1], None, ALU.is_le))
                step(e.scalar_tensor_tensor(out=member[:, :], in0=pl[1][:, :], scalar=tlo[:, 0:1], in1=work[:, :], op0=ALU.is_ge, op1=ALU.mult))
                step(e.scalar_tensor_tensor(out=work[:, :], in0=cio[:, :], scalar=-1024.0, in1=member[:, :], op0=ALU.add, op1=ALU.mult))
                step(e.tensor_reduce(col[:, 0:1], work[:, :], AX.X, ALU.min))
                step(e.scalar_tensor_tensor(out=work[:, :], in0=cio[:, :], scalar=1.0, in1=member[:, :], op0=ALU.add, op1=ALU.mult))
                step(e.tensor_reduce(col[:, 1:2], work[:, :], AX.X, ALU.max))
                step(e.tensor_scalar(col[:, 2:3], col[:, 1:2], 0.0, None, ALU.is_gt))
                step(e.scalar_tensor_tensor(out=col[:, 3:4], in0=col[:, 0:1], scalar=1024.0, in1=col[:, 2:3], op0=ALU.add, op1=ALU.mult))
                step(e.tensor_scalar(col[:, 4:5], col[:, 3:4], 1.0, None, ALU.add))
                step(e.tensor_tensor(col[:, 5:6], col[:, 4:5], col[:, 1:2], ALU.max))
                step(e.scalar_tensor_tensor(out=col[:, 6:7], in0=col[:, 5:6], scalar=float(R - 1), in1=col[:, 3:4], op0=ALU.add, op1=ALU.subtract))
                step(e.tensor_copy(col_i[:, :], col[:, 6:7]))
                step(e.tensor_scalar(col_i[:, :], col_i[:, :], R.bit_length() - 1, None, ALU.logical_shift_right))
                e.tensor_copy(col[:, 7:8], col_i[:, :]).then_inc(e_n, 1)
                e.wait_ge(e_r, 1)
                e.tensor_copy(tab[:, 0:NT + 1], pr[:, 0:NT + 1]).then_inc(e_n, 1)
                e.tensor_copy(tab[:, 80:80 + NT], pr[:, 80:80 + NT]).then_inc(e_n, 1)

            @block.tensor
            def _(e):
                e.wait_ge(e_row, 3)
                for k in range(3):
                    for b in range(EB):
                        last = e.transpose(pt[k][:, b, :], rows[:, k, b, :], ident[:, :])
                    last.then_inc(e_t, 1)
                e.wait_ge(e_lim, 9)
                for k in range(2):
                    for b in range(EB):
                        last = e.matmul(pl[k][:, b * P:(b + 1) * P], bcast[:, k, b, :], ident[:, :], start=True, stop=True)
                    last.then_inc(e_pl, 1)
                e.matmul(pb[:, :], base_r[:, :], ident[0:1, 0:1], start=True, stop=True).then_inc(e_pl, 1)
                e.wait_ge(e_n, 1)
                e.matmul(pr[:, 0:NT + 1], col[:, 7:8], tri[:, :], start=True, stop=True)
                e.matmul(pr[:, 80:80 + NT], col[:, 3:4], ident[0:NT, 0:NT], start=True, stop=True).then_inc(e_r, 1)


def normalise(nc, tag, acc, xnT, ident, ticks, load=None, rows=None, cols=None):
    with ExitStack() as ctx:
        sem = scoped(nc, ctx)
        stats = ctx.enter_context(nc.sbuf_tensor(f"{tag}_stats", [PT, 2, 6], F32))
        mv = ctx.enter_context(nc.sbuf_tensor(f"{tag}_mv", [PT, TILES, 2], F32))
        rstd = ctx.enter_context(nc.sbuf_tensor(f"{tag}_rstd", [PT, TILES], F32))
        std = ctx.enter_context(nc.sbuf_tensor(f"{tag}_std", [PT, TILES], F32))
        gm = ctx.enter_context(nc.sbuf_tensor(f"{tag}_gm", [PT, TILES, 2 * C], F16)) if rows is not None else None
        mv1 = ctx.enter_context(nc.sbuf_tensor(f"{tag}_mv1", [PT, 2], F32))
        xr = ctx.enter_context(nc.sbuf_tensor(f"{tag}_xr", [PT, 2, C], F32))
        pt = [ctx.enter_context(nc.psum_tensor(f"{tag}_pt{i}", [P, KC, 256], F32)) for i in range(2)]
        n_z, n_in, n_d, n_v, n_s, n_x, n_t, n_c, n_o, n_g, n_l = (sem(f"norm_{tag}_{n}") for n in (
            "zeroed", "loaded", "dve", "var", "std", "rows", "turned", "copied", "stored", "high", "low"))
        with nc.Block() as block:
            @block.vector
            def _(e):
                if load is not None:
                    e.memset(acc[:, TILES - 1, :], 0.0).then_inc(n_z, 1)
                    e.wait_ge(n_in, 32)
                with e.Fori(0, TILES) as i:
                    step = counted(e, n_d, 3 * i)
                    step(e.bn_stats(stats[:, 0, :], acc[:, bass.ds(i, 1), :].rearrange("p a c -> p (a c)")))
                    hold(e, ticks)
                    step(e.bn_aggr(mv1[:, :], stats[:, 0, :]))
                    step(e.tensor_copy(mv[:, bass.ds(i, 1), :].rearrange("p a c -> p (a c)"), mv1[:, :]))
                step = counted(e, n_d, 3 * TILES)
                step(e.tensor_scalar(rstd[:, :], mv[:, :, 1], 1e-5, None, ALU.add))
                e.sem_inc(n_v, 1)
                e.wait_ge(n_s, 1)
                step(e.reciprocal(rstd[:, :], std[:, :]))
                with e.Fori(0, TILES // 2) as pair:
                    i = pair * 2
                    for b in range(2):
                        e.wait_ge(n_t, i + b)
                        e.tensor_scalar(xr[:, b, :], acc[:, bass.ds(i + b, 1), :].rearrange("p a c -> p (a c)"),
                                        mv[:, bass.ds(i + b, 1), 0], rstd[:, bass.ds(i + b, 1)],
                                        ALU.subtract, ALU.mult).then_inc(n_x, 1)
                        if rows is not None:
                            e.wait_ge(n_g, i + b + 1)
                            e.tensor_tensor(gm[:, bass.ds(i + b, 1), C:2 * C].rearrange("p a c -> p (a c)"), xr[:, b, :],
                                            gm[:, bass.ds(i + b, 1), 0:C].rearrange("p a c -> p (a c)"), ALU.subtract).then_inc(n_l, 1)

            @block.scalar
            def _(e):
                e.wait_ge(n_v, 1)
                e.activation(std[:, :], rstd[:, :], ACT.Sqrt).then_inc(n_s, 1)
                with e.Fori(0, TILES // 2) as pair:
                    i = pair * 2
                    for b in range(2):
                        e.wait_ge(n_x, i + b + 1)
                        if rows is not None:
                            e.activation(gm[:, bass.ds(i + b, 1), 0:C].rearrange("p a c -> p (a c)"), xr[:, b, :], ACT.Copy).then_inc(n_g, 1)
                        e.wait_ge(n_t, i + b + 1)
                        e.activation(xnT[:, :, bass.ds((i + b) * PT, PT)], pt[b][:, :, 0:PT], ACT.Copy).then_inc(n_c, 1)

            @block.tensor
            def _(e):
                e.sem_inc(n_c, 2)
                with e.Fori(0, TILES // 2) as pair:
                    i = pair * 2
                    for b in range(2):
                        e.wait_ge(n_x, i + b + 1)
                        e.wait_ge(n_c, i + b + 1)
                        for k in range(KC):
                            last = e.transpose(pt[b][:, k, 0:PT], xr[:, b, k * P:(k + 1) * P], ident[0:PT, 0:PT])
                        last.then_inc(n_t, 1)

            @block.sync
            def _(e):
                if load is not None:
                    n = PT * (TILES - 1)
                    e.dma_start(acc[:, 0:TILES - 1, :], load[0:n, :].rearrange("(i p) c -> p i c", p=PT)).then_inc(n_in, 16)
                    e.wait_ge(n_z, 1)
                    e.dma_start(acc[0:LAST, TILES - 1, :], load[n:N, :]).then_inc(n_in, 16)
                    e.wait_ge(n_l, TILES)
                    e.dma_start(rows.rearrange("(i p) c -> p i c", p=PT), gm[:, :, :]).then_inc(n_o, 16)
                    e.wait_ge(n_c, TILES + 2)
                    e.dma_start(cols, xnT[:, :, :]).then_inc(n_o, 16)
                    e.wait_ge(n_o, 32)


def mix(nc, A, acc, xnT, ident, ones):
    with ExitStack() as ctx:
        m_parts = [ctx.enter_context(nc.sbuf_tensor(f"moments{i}", [P, HEADS * FCH, VD], BF16)) for i in range(3)]
        qT = [ctx.enter_context(nc.sbuf_tensor(f"q_cols{i}", [P, KC, NP], F16)) for i in range(2)]
        mix_moments(nc, A, xnT, ident, ones, m_parts, qT)
        yo = ctx.enter_context(nc.sbuf_tensor("mix_y", [PT, TILES, C], F32))
        mix_queries(nc, ident, m_parts, qT, yo)
        mix_project(nc, A, acc, ident, ones, yo)


def mix_moments(nc, A, xnT, ident, ones, m_parts, qT):
    with ExitStack() as ctx:
        sem = scoped(nc, ctx)

        def sb(name, shape, dt=F32):
            return ctx.enter_context(nc.sbuf_tensor(f"mk_{name}", shape, dt))

        def ps(name, shape):
            return ctx.enter_context(nc.psum_tensor(f"mk_{name}", shape, F32))
        w = sb("w", [P, KC, 3 * C])
        wb = sb("wb", [1, 3 * C])
        temp = sb("temp", [P, HEADS])
        tsq = sb("tsq", [P, HEADS])
        factor = sb("factor", [P, HEADS, FCH])
        M = sb("M", [P, HEADS * FCH, VD])
        mask = sb("mask", [PT, TILES])
        xs = [sb(f"xs{b}", [P, KC, PT]) for b in range(2)]
        sq = sb("sq", [PT, 2 * C])
        ss = sb("ss", [PT, 3, 2 * HEADS])
        one = sb("one", [PT, HEADS])
        ext = sb("ext", [PT, HEADS, HD + HD // 2])
        qn = sb("qn", [PT, C])
        F = sb("F", [PT, HEADS, ND * HD + HD])
        Fh, Fl = ([sb(f"F{n}{b}", [PT, HEADS, FP], F16) for b in range(2)] for n in "hl")
        vf, vr = sb("vf", [PT, HEADS, VD]), sb("vr", [PT, HEADS, VD])
        v = [[sb(f"v{b}{i}", [PT, HEADS, VD], BF16) for i in range(3)] for b in range(2)]
        zero = sb("zero", [P, 15 * VD])
        pqk = [ps(f"pqk{b}", [PT, 2 * C]) for b in range(2)]
        pv = [ps(f"pv{b}", [PT, C]) for b in range(2)]
        pm = [ps(f"pm{i}", [P, 15 * VD]) for i in range(3)]
        pqt = ps("pqt", [P, KC, PT])
        S = {n: sem(f"mk_{n}") for n in ("in", "set", "vset", "dve", "pool", "xs", "proj", "pfree", "sq", "ss", "sqrt", "qn", "qt",
                                         "q_hi", "q_lo", "feat", "f_hi", "f_lo", "f_lo_pool", "vf", "v_parts", "mm", "out")}
        NF = ND * HD + HD
        H2 = HEADS // 2
        PAIRS = TILES // 2

        def tiles(body):
            def run(e):
                with e.Fori(0, PAIRS - 1) as p:
                    for b in range(2):
                        body(e, p * 2 + b, b, True)
                body(e, TILES - 2, 0, True)
                body(e, TILES - 1, 1, False)
            return run

        def ext_window():
            a = ext[:, :, :].ap
            return bass.AP(ext[:, :, :].tensor, ext[:, :, :].offset, [list(a[0]), [HD + HD // 2, HEADS], [1, ND], [1, HD]])

        with nc.Block() as block:
            @block.sync
            def _(e):
                e.dma_start(w[:, :, :], A["WqkvT"].rearrange("(k p) n -> p k n", p=P)).then_inc(S["in"], 16)
                e.dma_start(wb[:, :], A["L0_mix_bqkv"].rearrange("(a n) -> a n", a=1)).then_inc(S["in"], 16)
                e.dma_start(temp[:, :], A["L0_mix_temperature"].rearrange("a h b c -> (a b c) h").to_broadcast([P, HEADS])).then_inc(S["in"], 16)

            @block.gpsimd
            def _(e):
                e.memset(mask[:, :], 1.0 / N).then_inc(S["set"], 1)
                e.wait_ge(S["set"], 1)
                m = mask[:, TILES - 1:TILES]
                e.affine_select(out=m, in_=m, compare_op=ALU.is_ge, fill=0.0, base=LAST - 1,
                                pattern=[[0, 1]], channel_multiplier=-1).then_inc(S["set"], 1)
                e.sem_inc(S["v_parts"], 1)
                e.wait_ge(S["vset"], 1)
                none = zero[0:PT, 0:HEADS * VD].rearrange("p (h e) -> p h e", h=HEADS)
                e.sem_inc(S["f_lo_pool"], 1)

                def body(e, i, b, more):
                    n = 3 * i
                    e.wait_ge(S["vf"], i + 1)
                    e.wait_ge(S["mm"], i + 1)
                    e.tensor_tensor(v[b][0][:, :, :], vf[:, :, :], none, ALU.subtract).then_inc(S["pool"], 1)
                    e.wait_ge(S["pool"], n + 1)
                    e.tensor_tensor(vr[:, :, :], vf[:, :, :], v[b][0][:, :, :], ALU.subtract).then_inc(S["pool"], 1)
                    e.wait_ge(S["pool"], n + 2)
                    e.tensor_tensor(v[b][1][:, :, :], vr[:, :, :], none, ALU.subtract).then_inc(S["pool"], 1)
                    e.wait_ge(S["pool"], n + 3)
                    e.tensor_tensor(v[b][2][:, :, :], vr[:, :, :], v[b][1][:, :, :], ALU.subtract).then_inc(S["v_parts"], 1)
                    e.wait_ge(S["f_hi"], 2 * i + 2)
                    e.tensor_tensor(Fl[b][:, H2:HEADS, 0:NF], F[:, H2:HEADS, :], Fh[b][:, H2:HEADS, 0:NF], ALU.subtract).then_inc(S["f_lo_pool"], 1)
                tiles(body)(e)

            @block.scalar
            def _(e):
                def load_x(e, i, b):
                    e.wait_ge(S["proj"], i + 1)
                    e.activation(xs[b][:, :, :], xnT[:, :, bass.ds(i * PT, PT)], ACT.Copy).then_inc(S["xs"], 1)

                def body(e, i, b, more):
                    e.wait_ge(S["proj"], i + 3)
                    e.activation(sq[:, :], pqk[b][:, :], ACT.Square).then_inc(S["sq"], 1)
                    e.wait_ge(S["ss"], i + 1)
                    e.activation(ss[:, 1, :], ss[:, 0, :], ACT.Sqrt).then_inc(S["sqrt"], 1)
                    if more:
                        load_x(e, i + 1, 1 - b)
                    e.wait_ge(S["mm"], i + 1)
                    for half in range(2):
                        e.wait_ge(S["feat"], 2 * i + half + 1)
                        hs = slice(half * H2, (half + 1) * H2)
                        e.activation(Fh[b][:, hs, 0:NF], F[:, hs, :], ACT.Copy).then_inc(S["f_hi"], 1)
                    e.wait_ge(S["qt"], i + 2)
                    e.activation(qT[0][:, :, bass.ds(i * PT, PT)], pqt[:, :, :], ACT.Copy).then_inc(S["q_hi"], 1)
                load_x(e, 0, 0)
                tiles(body)(e)

            @block.tensor
            def _(e):
                e.sem_inc(S["proj"], 2)
                e.sem_inc(S["qt"], 1)
                e.sem_inc(S["mm"], 2)
                e.wait_ge(S["in"], 16 * 3)
                e.wait_ge(S["vset"], 1)
                for m in range(3):
                    e.matmul(pm[m][:, :], zero[:, 0:P], zero[:, :], start=True, stop=False, skip_group_check=True)

                def project(e, i, b):
                    e.wait_ge(S["xs"], i + 1)
                    e.wait_ge(S["pfree"], i + 1)
                    for o, bank, n in ((0, pqk[b], 2 * C), (2 * C, pv[b], C)):
                        for k in range(KC):
                            e.matmul(bank[:, :], xs[b][:, k, :], w[:, k, o:o + n], start=(k == 0), stop=False)
                        mm = e.matmul(bank[:, :], ones[0:1, 0:PT], wb[:, o:o + n], start=False, stop=True)
                    mm.then_inc(S["proj"], 1)

                def body(e, i, b, more):
                    e.wait_ge(S["qn"], i + 1)
                    e.wait_ge(S["q_lo"], i + 1)
                    for k in range(KC):
                        mm = e.transpose(pqt[:, k, :], qn[:, k * P:(k + 1) * P], ident[0:PT, 0:PT])
                    mm.then_inc(S["qt"], 1)
                    if more:
                        project(e, i + 1, 1 - b)
                    e.wait_ge(S["f_lo"], i + 1)
                    e.wait_ge(S["f_lo_pool"], i + 2)
                    e.wait_ge(S["v_parts"], i + 2)
                    for u in range(HEADS * FCH):
                        h, c, j = u // FCH, u % FCH, u % 15
                        for f, parts in ((Fh[b], v[b]), (Fl[b], v[b][0:2])):
                            for part in parts:
                                mm = e.matmul(pm[u // 15][:, j * VD:(j + 1) * VD], f[:, h, c * P:(c + 1) * P], part[:, h, :],
                                              start=False, stop=False, skip_group_check=True)
                    mm.then_inc(S["mm"], 1)
                project(e, 0, 0)
                tiles(body)(e)

            @block.vector
            def _(e):
                step = counted(e, S["vset"], 0)
                step(e.memset(zero[:, :], 0.0))
                step(e.memset(one[:, :], 1.0))
                for f in Fh + Fl:
                    step(e.memset(f[:, :, NF:FP], 0.0))
                for f in Fh:
                    step(e.memset(f[:, :, NF:NF + 1], 1.0))
                e.wait_ge(S["in"], 16 * 3)
                step(e.tensor_tensor(tsq[:, :], temp[:, :], temp[:, :], ALU.mult))
                step(e.tensor_scalar(factor[:, :, :], tsq[:, :].unsqueeze(2).to_broadcast([P, HEADS, FCH]), 1.0 / 16, None, ALU.mult))
                for c in (0, FCH - 1):
                    step(e.tensor_scalar(factor[0:HD, :, c], factor[0:HD, :, c], 0.5, None, ALU.mult))
                step(e.tensor_scalar(factor[HD:2 * HD, :, FCH - 1], temp[HD:2 * HD, :], SC ** 2, None, ALU.mult))
                step(e.memset(factor[2 * HD:3 * HD, :, FCH - 1], 16 * SC ** 4))
                e.wait_ge(S["set"], 2)
                e.sem_inc(S["pfree"], 2)
                e.sem_inc(S["q_lo"], 1)
                KS = 7

                def body(e, i, b, more):
                    step = counted(e, S["dve"], KS * i)
                    e.wait_ge(S["sq"], i + 1)
                    e.tensor_reduce(ss[:, 0, :], sq[:, :].rearrange("p (h d) -> p h d", h=2 * HEADS), AX.X, ALU.add).then_inc(S["ss"], 1)
                    e.wait_ge(S["v_parts"], i + 1)
                    e.tensor_scalar(vf[:, :, 1:VD], pv[b][:, :].rearrange("p (h d) -> p h d", h=HEADS), mask[:, bass.ds(i, 1)], None, ALU.mult)
                    e.tensor_scalar(vf[:, :, 0:1], one[:, :].unsqueeze(2), mask[:, bass.ds(i, 1)], None, ALU.mult).then_inc(S["vf"], 1)
                    e.wait_ge(S["sqrt"], i + 1)
                    step(e.tensor_scalar(ss[:, 2, 0:HEADS], ss[:, 1, 0:HEADS], SC, 1e-12, ALU.mult, ALU.max))
                    step(e.tensor_scalar(ss[:, 2, HEADS:2 * HEADS], ss[:, 1, HEADS:2 * HEADS], 1e-12, None, ALU.max))
                    step(e.reciprocal(ss[:, 2, :], ss[:, 2, :]))
                    step(e.tensor_scalar(ss[:, 2, 0:HEADS], ss[:, 2, 0:HEADS], 4 * SC * SC, None, ALU.mult))
                    step(e.tensor_scalar(ss[:, 2, HEADS:2 * HEADS], ss[:, 2, HEADS:2 * HEADS], 4 * SC, None, ALU.mult))
                    e.wait_ge(S["qt"], i + 1)
                    e.tensor_tensor(qn[:, :].rearrange("p (h d) -> p h d", h=HEADS), pqk[b][:, 0:C].rearrange("p (h d) -> p h d", h=HEADS),
                                    ss[:, 2, 0:HEADS].unsqueeze(2).to_broadcast([PT, HEADS, HD]), ALU.mult).then_inc(S["qn"], 1)
                    step(e.tensor_tensor(ext[:, :, 0:HD], pqk[b][:, C:2 * C].rearrange("p (h d) -> p h d", h=HEADS),
                                         ss[:, 2, HEADS:2 * HEADS].unsqueeze(2).to_broadcast([PT, HEADS, HD]), ALU.mult))
                    e.sem_inc(S["pfree"], 1)
                    step(e.tensor_copy(ext[:, :, HD:HD + HD // 2], ext[:, :, 0:HD // 2]))
                    win = ext_window()
                    for half in range(2):
                        if half:
                            e.wait_ge(S["f_lo_pool"], i + 1)
                        hs = slice(half * H2, (half + 1) * H2)
                        e.tensor_copy(F[:, hs, ND * HD:NF], ext[:, hs, 0:HD])
                        for h in range(half * H2, (half + 1) * H2):
                            ins = e.tensor_tensor(F[:, h, 0:ND * HD].rearrange("p (d j) -> p d j", d=ND),
                                                  ext[:, h, 0:HD].unsqueeze(1).to_broadcast([PT, ND, HD]), win[:, h, :, :], ALU.mult)
                        ins.then_inc(S["feat"], 1)
                    e.wait_ge(S["f_hi"], 2 * i + 1)
                    e.tensor_tensor(Fl[b][:, 0:H2, 0:NF], F[:, 0:H2, :], Fh[b][:, 0:H2, 0:NF], ALU.subtract).then_inc(S["f_lo"], 1)
                    e.wait_ge(S["q_hi"], i + 1)
                    e.tensor_tensor(qT[1][:, :, bass.ds(i * PT, PT)], pqt[:, :, :], qT[0][:, :, bass.ds(i * PT, PT)], ALU.subtract).then_inc(S["q_lo"], 1)
                tiles(body)(e)
                e.wait_ge(S["mm"], TILES + 2)
                step = counted(e, S["out"], 0)
                for m in range(3):
                    n = min(15, HEADS * FCH - 15 * m)
                    step(e.tensor_copy(M[:, 15 * m:15 * m + n, :], pm[m][:, 0:n * VD].rearrange("p (u e) -> p u e", e=VD)))
                step(e.tensor_tensor(M[:, :, :], M[:, :, :], factor[:, :, :].rearrange("p h c -> p (h c)").unsqueeze(2).to_broadcast([P, HEADS * FCH, VD]), ALU.mult))
                step(e.tensor_copy(m_parts[0][:, :, :], M[:, :, :]))
                step(e.tensor_tensor(M[:, :, :], M[:, :, :], m_parts[0][:, :, :], ALU.subtract))
                step(e.tensor_copy(m_parts[1][:, :, :], M[:, :, :]))
                step(e.tensor_tensor(m_parts[2][:, :, :], M[:, :, :], m_parts[1][:, :, :], ALU.subtract))


def mix_queries(nc, ident, m_parts, qT, yo):
    with ExitStack() as ctx:
        sem = scoped(nc, ctx)

        def sb(name, shape, dt=F32):
            return ctx.enter_context(nc.sbuf_tensor(f"mq_{name}", shape, dt))

        def ps(name, shape):
            return ctx.enter_context(nc.psum_tensor(f"mq_{name}", shape, F32))
        HPC = P // HD
        wrap = sb("wrap", [P, HPC, HD + HD // 2])
        sel = sb("sel", [P, HPC, FP], F16)
        rep = sb("rep", [P, HPC, P], F16)
        ones_row = sb("ones_row", [1, GW], F16)
        one_rows = sb("one_rows", [1, P], F16)
        a = [sb(f"a{b}", [P, GW]) for b in range(2)]
        F = [sb(f"F{c}", [P, GW]) for c in range(FCH)]
        zero = sb("zero", [1, P], F16)
        zero_y = sb("zero_y", [1, 4 * VD], F16)
        Fh = [[sb(f"Fh{b}{c}", [P, GW], F16) for c in range(FCH)] for b in range(2)]
        Fl = [[sb(f"Fl{b}{c}", [P, GW], F16) for c in range(FCH)] for b in range(2)]
        yr = sb("yr", [PT, 4, 1])
        pa = ps("pa", [P, GW])
        pb = [ps(f"pb{c}", [P, GW]) for c in range(FCH)]
        py = [ps(f"py{b}", [PT, 4, VD]) for b in range(2)]
        S = {n: sem(f"mq_{n}") for n in ("set", "ready", "a", "a_out", "b", "feat", "f_hi", "f_lo", "f_lo_pool", "y", "recip", "y_out")}
        TURNS = GROUPS * HEADS
        ON_POOL = (0, 1, 3)
        ON_DVE = [c for c in range(FCH) if c not in ON_POOL]

        def rows(c):
            return 2 * HD if c == FCH - 1 else P

        def turns(body, lead):
            def run(e):
                if lead:
                    lead(e, 0, 0)
                with e.Fori(0, TURNS // 2 - 1) as p:
                    for b in range(2):
                        body(e, p * 2 + b, b, True)
                body(e, TURNS - 2, 0, True)
                body(e, TURNS - 1, 1, False)
            return run

        with nc.Block() as block:
            @block.vector
            def _(e):
                step = counted(e, S["set"], 0)
                for hh in range(HPC):
                    step(e.tensor_copy(wrap[:, hh, 0:HD], ident[:, hh * HD:(hh + 1) * HD]))
                    step(e.tensor_copy(wrap[:, hh, HD:HD + HD // 2], ident[:, hh * HD:hh * HD + HD // 2]))
                step(e.memset(sel[:, :, :], 0.0))
                w4 = wrap[:, :, :].ap
                win = bass.AP(wrap[:, :, :].tensor, wrap[:, :, :].offset, [list(w4[0]), [HD + HD // 2, HPC], [1, ND], [1, HD]])
                for hh in range(HPC):
                    step(e.tensor_copy(sel[:, hh, 0:ND * HD].rearrange("p (d m) -> p d m", d=ND), win[:, hh, :, :]))
                    step(e.tensor_copy(rep[:, hh, :].rearrange("p (r m) -> p r m", m=HD), wrap[:, hh, 0:HD].unsqueeze(1).to_broadcast([P, P // HD, HD])))
                step(e.memset(ones_row[:, :], 1.0))
                step(e.memset(one_rows[:, :], 0.0))
                step(e.memset(one_rows[:, HD:2 * HD], 1.0))
                for b in range(2):
                    for f in (Fh, Fl):
                        step(e.memset(f[b][FCH - 1][:, :], 0.0))
                    step(e.memset(Fh[b][FCH - 1][2 * HD:2 * HD + 1, :], 1.0))
                step(e.memset(zero[:, :], 0.0))
                step(e.memset(zero_y[:, :], 0.0))
                e.sem_inc(S["ready"], 1)
                e.sem_inc(S["f_lo"], len(ON_DVE))
                e.sem_inc(S["feat"], FCH + 1)
                e.sem_inc(S["y_out"], 2)

                def low(e, w, b, c):
                    e.wait_ge(S["f_hi"], w * FCH + c + 1 + FCH)
                    e.wait_ge(S["y"], w + 1)
                    e.tensor_tensor(Fl[b][c][0:rows(c), :], F[c][0:rows(c), :], Fh[b][c][0:rows(c), :], ALU.subtract).then_inc(S["f_lo"], 1)

                def features(e, w, b):
                    e.wait_ge(S["a_out"], w + 2)
                    for c in range(FCH):
                        u = w * FCH + c
                        e.wait_ge(S["b"], u + 1)
                        e.wait_ge(S["f_hi"], u + 1)
                        if c in ON_POOL:
                            e.wait_ge(S["f_lo_pool"], w * len(ON_POOL) + ON_POOL.index(c) + 1)
                        else:
                            e.wait_ge(S["f_lo"], w * len(ON_DVE) + ON_DVE.index(c) + 1)
                        e.tensor_tensor(F[c][0:rows(c), :], a[b][0:rows(c), :], pb[c][0:rows(c), :], ALU.mult).then_inc(S["feat"], 1)
                        if c and c - 1 in ON_DVE:
                            low(e, w, b, c - 1)
                    if FCH - 1 in ON_DVE:
                        low(e, w, b, FCH - 1)

                def answer(e, w, b, more):
                    if more:
                        features(e, w + 1, 1 - b)
                    e.wait_ge(S["y"], w + 3)
                    e.wait_ge(S["y_out"], w + 2)
                    e.reciprocal(yr[:, :, :], py[b][:, :, 0:1]).then_inc(S["recip"], 1)
                    e.wait_ge(S["recip"], w + 1)
                    g, h = w // HEADS, w % HEADS
                    e.tensor_tensor(yo[:, bass.ds(g * 4, 4), bass.ds(h * HD, HD)], py[b][:, :, 1:VD],
                                    yr[:, :, :].to_broadcast([PT, 4, HD]), ALU.mult).then_inc(S["y_out"], 1)
                turns(answer, features)(e)

            @block.scalar
            def _(e):
                e.sem_inc(S["a_out"], 1)
                e.sem_inc(S["f_hi"], FCH)

                def high(e, w, b):
                    e.wait_ge(S["a"], w + 1)
                    e.wait_ge(S["feat"], w * FCH + 1)
                    e.activation(a[b][:, :], pa[:, :], ACT.Copy).then_inc(S["a_out"], 1)
                    for c in range(FCH):
                        e.wait_ge(S["feat"], w * FCH + c + 1 + FCH + 1)
                        e.wait_ge(S["y"], w + 1)
                        e.activation(Fh[b][c][0:rows(c), :], F[c][0:rows(c), :], ACT.Copy).then_inc(S["f_hi"], 1)

                def body(e, w, b, more):
                    if more:
                        high(e, w + 1, 1 - b)
                turns(body, high)(e)

            @block.gpsimd
            def _(e):
                e.sem_inc(S["f_lo_pool"], len(ON_POOL))

                def low(e, w, b):
                    for c in ON_POOL:
                        e.wait_ge(S["f_hi"], w * FCH + c + 1 + FCH)
                        e.wait_ge(S["y"], w + 1)
                        e.tensor_tensor(Fl[b][c][0:rows(c), :], F[c][0:rows(c), :], Fh[b][c][0:rows(c), :], ALU.subtract).then_inc(S["f_lo_pool"], 1)

                def body(e, w, b, more):
                    if more:
                        low(e, w + 1, 1 - b)
                turns(body, low)(e)

            @block.tensor
            def _(e):
                e.sem_inc(S["y"], 2)
                e.wait_ge(S["ready"], 1)

                def vector(e, w, b):
                    e.wait_ge(S["a_out"], w + 1)
                    factor(e, w, pa, rep, 0, False).then_inc(S["a"], 1)

                def factor(e, w, bank, s, o, last_chunk):
                    g, h = w // HEADS, w % HEADS
                    for i in range(2):
                        mm = e.matmul(bank[:, :], s[:, bass.ds(h % HPC, 1), o:o + P].rearrange("p a c -> p (a c)"),
                                      qT[i][:, bass.ds(h // HPC, 1), bass.ds(g * GW, GW)].rearrange("p a c -> p (a c)"),
                                      start=(i == 0), stop=(i == 1 and not last_chunk))
                    if last_chunk:
                        mm = e.matmul(bank[:, :], one_rows[:, :], ones_row[:, :], start=False, stop=True)
                    return mm

                def rotated(e, w, b, c):
                    e.wait_ge(S["feat"], w * FCH + c + 2)
                    factor(e, w, pb[c], sel, c * P, c == FCH - 1).then_inc(S["b"], 1)

                def multiply(e, w, b, c):
                    if c == 0:
                        e.wait_ge(S["y_out"], w + 1)
                        e.matmul(py[b][:, :, :].rearrange("p t e -> p (t e)"), zero[:, 0:PT], zero_y[:, :], start=True, stop=False, skip_group_check=True)
                    e.wait_ge(S["f_hi"], w * FCH + c + 1 + FCH)
                    if c in ON_POOL:
                        e.wait_ge(S["f_lo_pool"], (w + 1) * len(ON_POOL) + ON_POOL.index(c) + 1)
                    else:
                        e.wait_ge(S["f_lo"], (w + 1) * len(ON_DVE) + ON_DVE.index(c) + 1)
                    h = w % HEADS
                    for t in range(4):
                        for f, parts in ((Fh, m_parts), (Fl, m_parts[0:2])):
                            for part in parts:
                                mm = e.matmul(py[b][:, t, :], f[b][c][:, t * PT:(t + 1) * PT],
                                              part[:, bass.ds(h * FCH + c, 1), :].rearrange("p a c -> p (a c)"),
                                              start=False, stop=False, skip_group_check=True)
                    return mm

                def lead(e, w, b):
                    vector(e, w, b)
                    for c in range(FCH):
                        rotated(e, w, b, c)

                def body(e, w, b, more):
                    if more:
                        vector(e, w + 1, 1 - b)
                    for c in range(FCH):
                        if more:
                            rotated(e, w + 1, 1 - b, c)
                        mm = multiply(e, w, b, c)
                    mm.then_inc(S["y"], 1)
                turns(body, lead)(e)


def mix_project(nc, A, acc, ident, ones, yo):
    with ExitStack() as ctx:
        sem = scoped(nc, ctx)

        def sb(name, shape, dt=F32):
            return ctx.enter_context(nc.sbuf_tensor(f"mp_{name}", shape, dt))

        def ps(name, shape):
            return ctx.enter_context(nc.psum_tensor(f"mp_{name}", shape, F32))
        wp = sb("wp", [P, KC, C])
        bp = sb("bp", [1, C])
        ys = [sb(f"ys{b}", [PT, C]) for b in range(2)]
        yT = [sb(f"yT{b}", [P, KC, PT]) for b in range(2)]
        pt = [ps(f"pt{b}", [P, KC, PT]) for b in range(2)]
        po = [ps(f"po{b}", [PT, C]) for b in range(2)]
        S = {n: sem(f"mp_{n}") for n in ("in", "ys", "turned", "yT", "sum", "added")}
        PAIRS = TILES // 2

        def tiles(body):
            def run(e):
                with e.Fori(0, PAIRS - 1) as p:
                    for b in range(2):
                        body(e, p * 2 + b, b, True)
                body(e, TILES - 2, 0, True)
                body(e, TILES - 1, 1, False)
            return run
        with nc.Block() as block:
            @block.sync
            def _(e):
                e.dma_start(wp[:, :, :], A["WprojT"].rearrange("(k p) n -> p k n", p=P)).then_inc(S["in"], 16)
                e.dma_start(bp[:, :], A["L0_mix_bproj"].rearrange("(a n) -> a n", a=1)).then_inc(S["in"], 16)

            @block.scalar
            def _(e):
                def turn(e, i, b):
                    e.wait_ge(S["turned"], i + 1)
                    e.activation(ys[b][:, :], yo[:, bass.ds(i, 1), :].rearrange("p a c -> p (a c)"), ACT.Copy).then_inc(S["ys"], 1)

                def body(e, i, b, more):
                    if more:
                        turn(e, i + 1, 1 - b)
                    e.wait_ge(S["turned"], i + 3)
                    e.wait_ge(S["sum"], i + 1)
                    e.activation(yT[b][:, :, :], pt[b][:, :, :], ACT.Copy).then_inc(S["yT"], 1)
                turn(e, 0, 0)
                tiles(body)(e)

            @block.tensor
            def _(e):
                e.sem_inc(S["turned"], 2)
                e.sem_inc(S["sum"], 2)
                e.wait_ge(S["in"], 32)

                def turn(e, i, b):
                    e.wait_ge(S["ys"], i + 1)
                    e.wait_ge(S["yT"], i + 1)
                    for k in range(KC):
                        mm = e.transpose(pt[b][:, k, :], ys[b][:, k * P:(k + 1) * P], ident[0:PT, 0:PT])
                    mm.then_inc(S["turned"], 1)

                def body(e, i, b, more):
                    if more:
                        turn(e, i + 1, 1 - b)
                    e.wait_ge(S["yT"], i + 3)
                    e.wait_ge(S["added"], i + 1)
                    for k in range(KC):
                        e.matmul(po[b][:, :], yT[b][:, k, :], wp[:, k, :], start=(k == 0), stop=False)
                    e.matmul(po[b][:, :], ones[0:1, 0:PT], bp[:, :], start=False, stop=True).then_inc(S["sum"], 1)
                turn(e, 0, 0)
                tiles(body)(e)

            @block.vector
            def _(e):
                e.sem_inc(S["yT"], 2)
                e.sem_inc(S["added"], 2)

                def body(e, i, b, more):
                    e.wait_ge(S["sum"], i + 3)
                    r = acc[:, bass.ds(i, 1), :].rearrange("p a c -> p (a c)")
                    e.tensor_tensor(r, r, po[b][:, :], ALU.add).then_inc(S["added"], 1)
                tiles(body)(e)


def gnn_step(nc, A, s, tables, cols, idx, keys, tab, iota_keys, tile_keys, ident, sums, ticks):
    last_step = s == STEPS - 1
    with ExitStack() as ctx:
        sem = scoped(nc, ctx)

        def sb(name, shape, dt=F32):
            return ctx.enter_context(nc.sbuf_tensor(f"g{s}_{name}", shape, dt))

        def ps(name, shape):
            return ctx.enter_context(nc.psum_tensor(f"g{s}_{name}", shape, F32))
        names = ("w_in", "w_mm", "w_cp", "idx_ready", "onehot", "used", "tile_done", "tile_out", "keyed",
                 "set", "h_free", "held", "pr", "pz", "pi", "ph", "r", "z", "t1", "t2", "n", "d", "hnew",
                 "turn", "rows_hi", "rows_lo", "hsum", "row_store", "col_store")
        S = {n: sem(f"g{s}_{n}") for n in names}
        h_in = [sem(f"g{s}_h_in{i}") for i in range(2)]
        landed = [nc.alloc_semaphore(f"g{s}_landed{r}") for r in range(R)]
        wc = sb("wc", [P, TYPES, KC, 3 * C])
        wh = sb("wh", [P, TYPES, KC, 3 * C])
        bi = sb("bi", [P, TYPES, 6])
        bh = sb("bh", [P, TYPES, 6])
        brz = sb("brz", [P, TYPES, 6])
        with ExitStack() as wctx:
            wm = wctx.enter_context(nc.sbuf_tensor(f"g{s}_wm", [P, TYPES, KC, C], F32))
            wi = wctx.enter_context(nc.sbuf_tensor(f"g{s}_wi", [P, TYPES, KC, 3 * C], F32))
            pw = [wctx.enter_context(nc.psum_tensor(f"g{s}_pw{i}", [P, 384], F32)) for i in range(2)]
            with nc.Block() as block:
                @block.sync
                def _(e):
                    for t in range(TYPES):
                        e.dma_start(wm[:, t, :, :], A["convT"][t, s].rearrange("(k p) n -> p k n", p=P)).then_inc(S["w_in"], 16)
                        e.dma_start(wi[:, t, :, :], A["wihT"][t].rearrange("(k p) n -> p k n", p=P)).then_inc(S["w_in"], 16)
                        e.dma_start(wh[:, t, :, :], A["whhT"][t].rearrange("(k p) n -> p k n", p=P)).then_inc(S["w_in"], 16)
                        e.dma_start(bi[:, t, :], A["bihT"][:, t, :]).then_inc(S["w_in"], 16)
                        e.dma_start(bh[:, t, :], A["bhhT"][:, t, :]).then_inc(S["w_in"], 16)

                @block.tensor
                def _(e):
                    e.wait_ge(S["w_in"], 16 * 15)
                    n = 0
                    for t in range(TYPES):
                        for m in range(KC):
                            for q in range(2):
                                if n >= 2:
                                    e.wait_ge(S["w_cp"], n - 1)
                                for k in range(KC):
                                    last = e.matmul(pw[n % 2][:, :], wm[:, t, k, m * P:(m + 1) * P], wi[:, t, k, q * 384:(q + 1) * 384], start=(k == 0), stop=(k == KC - 1))
                                last.then_inc(S["w_mm"], 1)
                                n += 1

                @block.vector
                def _(e):
                    e.wait_ge(S["w_in"], 16 * 15)
                    n = 0
                    for t in range(TYPES):
                        for m in range(KC):
                            for q in range(2):
                                n += 1
                                e.wait_ge(S["w_mm"], n)
                                e.tensor_copy(wc[:, t, m, q * 384:(q + 1) * 384], pw[(n - 1) % 2][:, :]).then_inc(S["w_cp"], 1)
                    e.tensor_tensor(brz[:, :, :], bi[:, :, :], bh[:, :, :], ALU.add)
        ring = sb("ring", [P, R, 2 * C], F16)
        islot = [sb(f"islot{r}", [P, 1], I32) for r in range(R)]
        onehot = sb("onehot", [P, DEEP, NKEY], F16)
        zero = sb("zero", [1, 512])
        ah = [sb(f"ah{i}", [P, TYPES, KC, GW]) for i in range(2)]
        hT = [sb(f"hT{i}", [P, TYPES, KC, GW]) for i in range(2)]
        base = sb("base", [P, KC, GW]) if last_step else None
        hn = sb("hn", [P, TYPES, KC, GW])
        rT = sb("rT", [P, GW])
        zT = sb("zT", [P, GW])
        t1 = sb("t1", [P, GW])
        nT = sb("nT", [P, GW])
        dT = sb("dT", [P, GW])
        rowb = sb("rowb", [PT, 4, C]) if last_step else sb("rowb", [PT, 4, 2 * C], F16)
        pagg = [ps(f"pagg{i}", [P, KC, TYPES, DT]) for i in range(2)]
        pr, pz, pi, ph = (ps(n, [P, GW]) for n in ("pr", "pz", "pi", "ph"))
        ptr = [ps(f"ptr{i}", [PT, 2, C]) for i in range(2)]
        NU = TYPES * KC
        TURNS = [(NU, 0)] if last_step else [(KC * (t + 1), t) for t in range(TYPES)]
        NTN = len(TURNS)
        HL = (TYPES + (1 if last_step else 0)) * 16

        def tile_range(e, g, j):
            a = e.value_load(tab[0:1, bass.ds(g * TG + j, 1)], min_val=0, max_val=32000)
            b = e.value_load(tab[0:1, bass.ds(g * TG + j + 1, 1)], min_val=1, max_val=32000)
            return a, b

        def schedule(stage):
            def run(e):
                stage(e, 0, None, 1)
                with e.Fori(0, GROUPS // 2) as p:
                    stage(e, p * 2 + 1, p * 2, 0)
                    stage(e, p * 2 + 2, p * 2 + 1, 1)
                stage(e, None, GROUPS - 1, 0)
            return run

        def pool_stage(e, ga, gg, par):
            if ga is None:
                return
            for j in range(TG):
                q0, q1 = tile_range(e, ga, j)
                with e.Fori(q0, q1) as q:
                    for r in range(R):
                        e.wait_ge(S["idx_ready"], q * R + R + r + 1)
                        e.wait_ge(S["used"], q * R + r + 1 + DEEP - R)
                        hold_pool(e, ticks, S["held"], q * R + R + r)
                        e.indirect_dma_start(ring[:, r, :], None, tables[s], bass.IndirectOffsetOnAxis(ap=islot[r][:, 0:1], axis=0)).then_inc(landed[r], 16)

        def load_h(e, g, par):
            for t in range(TYPES):
                src = cols[0] if s == 0 else cols[s][t]
                e.dma_start(hT[par][:, t, :, :], src[:, :, bass.ds(g * GW, GW)]).then_inc(h_in[par], 16)
            if last_step:
                e.wait_ge(S["turn"], g * 2)
                e.dma_start(base[:, :, :], cols[0][:, :, bass.ds(g * GW, GW)]).then_inc(h_in[par], 16)

        def sync_stage(e, ga, gg, par):
            if gg is None:
                load_h(e, 0, 0)
                return
            if ga is not None:
                e.wait_ge(S["h_free"], gg * NU)
                load_h(e, gg + 1, 1 - par)
            if not last_step:
                for t in range(TYPES):
                    e.wait_ge(S["hnew"], gg * NU + KC * (t + 1))
                    e.dma_start(cols[s + 1][t][:, :, bass.ds(gg * GW, GW)], hn[:, t, :, :]).then_inc(S["col_store"], 16)
                    e.wait_ge(S["rows_lo"], 2 * (gg * TYPES + t + 1))
                    e.dma_start(tables[s + 1][bass.ds(gg * GW + t * NP, GW), :].rearrange("(a p) c -> p a c", p=PT), rowb[:, :, :]).then_inc(S["row_store"], 16)
            else:
                e.wait_ge(S["rows_hi"], 2 * (gg + 1))
                e.dma_start(sums[bass.ds(gg * GW, GW), :].rearrange("(a p) c -> p a c", p=PT), rowb[:, :, :]).then_inc(S["row_store"], 16)

        def pe_stage(e, ga, gg, par):
            for j in range(TG):
                if gg is not None and j == 0:
                    e.wait_ge(S["tile_out"], (gg + 1) * TG + 2)
                    e.wait_ge(h_in[par], loads_done(gg, par))
                products = pe_unit(gg, par, j) if gg is not None and j < NU else []
                if ga is not None:
                    pe_tile(e, ga, j, products)
                else:
                    for product in products:
                        product(e)
                for i, (u, t) in enumerate(TURNS):
                    if gg is not None and j == u:
                        pe_turn(e, gg, i, t)

        def loads_done(g, par):
            return ((g - par) // 2 + 1) * HL if isinstance(g, int) else (g - par) * (HL // 2) + HL

        def pe_tile(e, g, j, products):
            q0, q1 = tile_range(e, g, j)
            pg = pagg[j % 2]
            flat = pg[:, :, :, :].rearrange("p k t d -> p (k t d)")
            e.wait_ge(S["tile_out"], g * TG + (j + 1 if j else 2))
            e.matmul(flat, zero[0:1, 0:P], zero[0:1, 0:KC * NKEY], start=True, stop=False, skip_group_check=True)

            def chunk(q, r):
                slot = (q * R + r) % DEEP
                e.wait_ge(landed[r], q * 16 + 32)
                e.wait_ge(S["onehot"], q * R + r + 2)
                for part in range(2):
                    for k in range(KC):
                        o = part * C + k * P
                        mm = e.matmul(pg[:, k, :, :].rearrange("p t d -> p (t d)"), ring[:, r, o:o + P],
                                      onehot[:, bass.ds(slot, 1), :].rearrange("p a c -> p (a c)"),
                                      start=False, stop=False, skip_group_check=True)
                mm.then_inc(S["used"], 1)
            for r in range(R):
                chunk(q0, r)
                for product in products[r * len(products) // R:(r + 1) * len(products) // R]:
                    product(e)
            with e.If(q1 - q0 - 1 > 0):
                with e.Fori(q0 + 1, q1) as q:
                    for r in range(R):
                        chunk(q, r)
            e.matmul(flat, zero[0:1, 0:P], zero[0:1, 0:KC * NKEY], start=False, stop=True, skip_group_check=True).then_inc(S["tile_done"], 1)

        def pe_unit(g, par, u):
            t, m = u // KC, u % KC
            x_a, x_h = ah[par], hT[par]

            def product(p, gate, x, w, k, first, last, done, free):
                def issue(e):
                    if first:
                        e.wait_ge(S[free], g * NU + u)
                    mm = e.matmul(p[:, :], w[:, t, k, gate * C + m * P:gate * C + m * P + P], x[:, t, k, :], start=first, stop=last)
                    if last:
                        mm.then_inc(S[done], 1)
                return issue
            products = []
            for p, gate, parts, done, free in ((pr, 0, [(wh, x_h), (wc, x_a)], "pr", "r"), (ph, 2, [(wh, x_h)], "ph", "t1"),
                                               (pi, 2, [(wc, x_a)], "pi", "t2"), (pz, 1, [(wh, x_h), (wc, x_a)], "pz", "z")):
                steps = [(w, x, k) for w, x in parts for k in range(KC)]
                for n, (w, x, k) in enumerate(steps):
                    products.append(product(p, gate, x, w, k, n == 0, n == len(steps) - 1, done, free))
            return products

        def pe_turn(e, g, i, t):
            src = base if last_step else hn[:, t, :, :]
            if last_step:
                e.wait_ge(S["hsum"], (g + 1) * NU)
            else:
                e.wait_ge(S["hnew"], g * NU + KC * (t + 1))
            for b in range(2):
                e.wait_ge(S["rows_hi"], 2 * (g * NTN + i))
                if not last_step:
                    e.wait_ge(S["rows_lo"], 2 * (g * NTN + i))
                for c in range(2):
                    for k in range(KC):
                        mm = e.transpose(ptr[b][:, c, k * P:(k + 1) * P], src[:, k, (2 * b + c) * PT:(2 * b + c + 1) * PT], ident[:, :])
                mm.then_inc(S["turn"], 1)

        def act_stage(e, ga, gg, par):
            for j in range(TG):
                if ga is not None:
                    if j == 0 and gg is not None:
                        e.wait_ge(S["pz"], gg * NU)
                    e.wait_ge(S["tile_done"], ga * TG + j + 1)
                    e.activation(ah[1 - par][:, :, :, j * DT:(j + 1) * DT], pagg[j % 2][:, :, :, :].rearrange("p k t d -> p t k d"), ACT.Copy).then_inc(S["tile_out"], 1)
                if gg is not None:
                    if j < NU:
                        act_unit(e, gg, j)
                    for i, (u, t) in enumerate(TURNS):
                        if j == u:
                            n = gg * NTN + i
                            e.wait_ge(S["row_store"], 16 * n)
                            for b in range(2):
                                e.wait_ge(S["turn"], 2 * n + b + 1)
                                e.activation(rowb[:, 2 * b:2 * b + 2, 0:C], ptr[b][:, :, :], ACT.Copy).then_inc(S["rows_hi"], 1)

        def act_unit(e, g, u):
            t, m = u // KC, u % KC
            U = g * NU + u
            e.wait_ge(S["pr"], U + 1)
            e.wait_ge(S["t1"], U)
            e.activation(rT[:, :], pr[:, :], ACT.Sigmoid, bias=brz[:, t, m:m + 1]).then_inc(S["r"], 1)
            e.wait_ge(S["t2"], U + 1)
            e.wait_ge(S["hnew"], U)
            e.activation(nT[:, :], t1[:, :], ACT.Tanh, bias=bi[:, t, 4 + m:5 + m]).then_inc(S["n"], 1)
            e.wait_ge(S["pz"], U + 1)
            e.activation(zT[:, :], pz[:, :], ACT.Sigmoid, bias=brz[:, t, 2 + m:3 + m]).then_inc(S["z"], 1)

        def dve_chunk(e, q, r, q0, first):
            c = nc.s_assert_within((q - q0) * R + first + r, 0, NCH - 1, skip_runtime_bounds_check_because="a tile has at most all the chunks, and R - 1 more")
            n = q * R + r
            e.wait_ge(landed[r], q * 16 + 16)
            e.tensor_copy(islot[r][:, :], idx[:, bass.ds(c, 1)]).then_inc(S["idx_ready"], 1)
            e.wait_ge(S["used"], n + 1)
            e.tensor_scalar(onehot[:, bass.ds(n % DEEP, 1), :].rearrange("p a c -> p (a c)"), tile_keys[:, :, :].rearrange("p t d -> p (t d)"), keys[:, bass.ds(c, 1)], None, ALU.is_equal).then_inc(S["onehot"], 1)

        def dve_gates(e, gg, par, j):
            if gg is None or j < 0:
                return
            if j < NU:
                dve_unit(e, gg, par, j)
            for i, (u, t) in enumerate(TURNS):
                if j == u and not last_step:
                    n = gg * NTN + i
                    for b in range(2):
                        e.wait_ge(S["rows_hi"], 2 * n + b + 1)
                        e.tensor_tensor(rowb[:, 2 * b:2 * b + 2, C:2 * C], ptr[b][:, :, :], rowb[:, 2 * b:2 * b + 2, 0:C], ALU.subtract).then_inc(S["rows_lo"], 1)

        def dve_stage(e, ga, gg, par):
            for j in range(TG):
                if ga is not None:
                    q0, q1 = tile_range(e, ga, j)
                    first = e.value_load(tab[0:1, bass.ds(ga * TG + j + 80, 1)], min_val=0, max_val=400)
                    e.wait_ge(S["keyed"], ga * TG + j + 1)
                    e.wait_ge(S["onehot"], q0 * R + 1)
                    e.tensor_scalar(tile_keys[:, :, :], tile_keys[:, :, :], float(DT), None, ALU.add).then_inc(S["keyed"], 1)
                    e.wait_ge(S["keyed"], ga * TG + j + 2)
                    hold(e, ticks)
                    for r in range(R):
                        dve_chunk(e, q0, r, q0, first)
                dve_gates(e, gg, par, j - 1)
                if ga is not None:
                    with e.If(q1 - q0 - 1 > 0):
                        with e.Fori(q0 + 1, q1) as q:
                            for r in range(R):
                                dve_chunk(e, q, r, q0, first)
            dve_gates(e, gg, par, TG - 1)

        def dve_unit(e, g, par, u):
            t, m = u // KC, u % KC
            U = g * NU + u
            e.wait_ge(S["ph"], U + 1)
            e.wait_ge(S["r"], U + 1)
            e.wait_ge(S["n"], U)
            e.scalar_tensor_tensor(out=t1[:, :], in0=ph[:, :], scalar=bh[:, t, 4 + m:5 + m], in1=rT[:, :], op0=ALU.add, op1=ALU.mult).then_inc(S["t1"], 1)
            e.wait_ge(S["t1"], U + 1)
            e.wait_ge(S["pi"], U + 1)
            e.tensor_tensor(t1[:, :], t1[:, :], pi[:, :], ALU.add).then_inc(S["t2"], 1)
            e.wait_ge(S["n"], U + 1)
            e.wait_ge(h_in[par], loads_done(g, par))
            e.tensor_tensor(dT[:, :], hT[par][:, t, m, :], nT[:, :], ALU.subtract).then_inc(S["d"], 1)
            e.wait_ge(S["d"], 2 * U + 1)
            e.wait_ge(S["z"], U + 1)
            e.tensor_tensor(dT[:, :], dT[:, :], zT[:, :], ALU.mult).then_inc(S["d"], 1)
            e.wait_ge(S["d"], 2 * U + 2)
            if not last_step and m == 0:
                e.wait_ge(S["col_store"], g * 16 * TYPES)
                e.wait_ge(S["turn"], g * 2 * TYPES)
            e.tensor_tensor(hn[:, t, m, :], dT[:, :], nT[:, :], ALU.add).then_inc(S["hnew"], 1)
            if last_step:
                e.wait_ge(S["hnew"], U + 1)
                if u == 0:
                    e.wait_ge(S["turn"], 2 * g)
                e.tensor_tensor(base[:, m, :], base[:, m, :], hn[:, t, m, :], ALU.add).then_inc(S["hsum"], 1)
                e.wait_ge(S["hsum"], U + 1)
            if u == NU - 1:
                e.wait_ge(S["pz"], U + 1)
            e.sem_inc(S["h_free"], 1)

        with nc.Block() as block:
            @block.gpsimd
            def _(e):
                for r in range(R):
                    e.wait_ge(S["idx_ready"], r + 1)
                    hold_pool(e, ticks, S["held"], r)
                    e.indirect_dma_start(ring[:, r, :], None, tables[s], bass.IndirectOffsetOnAxis(ap=islot[r][:, 0:1], axis=0)).then_inc(landed[r], 16)
                schedule(pool_stage)(e)

            @block.sync
            def _(e):
                schedule(sync_stage)(e)
                e.wait_ge(S["row_store"], 16 * NTN * GROUPS)
                if not last_step:
                    e.wait_ge(S["col_store"], 16 * TYPES * GROUPS)

            @block.tensor
            def _(e):
                e.sem_inc(S["used"], DEEP)
                e.sem_inc(S["tile_out"], 2)
                e.wait_ge(S["set"], 1)
                schedule(pe_stage)(e)

            @block.scalar
            def _(e):
                schedule(act_stage)(e)

            @block.vector
            def _(e):
                e.sem_inc(S["onehot"], 1)
                e.memset(zero[:, :], 0.0).then_inc(S["set"], 1)
                for r in range(R):
                    e.tensor_copy(islot[r][:, :], idx[:, r:r + 1]).then_inc(S["idx_ready"], 1)
                e.tensor_scalar(tile_keys[:, :, :], iota_keys[:, :, :], -float(DT), None, ALU.add).then_inc(S["keyed"], 1)
                schedule(dve_stage)(e)


def gnn_out(nc, A, acc, sums, ticks):
    with ExitStack() as ctx:
        sem = scoped(nc, ctx)
        def sb(name, shape, dt=F32):
            return ctx.enter_context(nc.sbuf_tensor(f"go_{name}", shape, dt))
        gm = sb("sums", [PT, TILES, C])
        gam = sb("gamma", [PT, C])
        bet = sb("beta", [PT, C])
        stats = sb("stats", [PT, 6])
        mv = sb("mv", [PT, TILES, 2])
        mv1 = sb("mv1", [PT, 2])
        std = sb("std", [PT, TILES])
        rstd = sb("rstd", [PT, TILES])
        w = sb("work", [PT, C])
        o_in, o_gm, o_d, o_v, o_s = (sem(f"go_{n}") for n in ("loaded", "sums", "dve", "var", "std"))

        def row(t, i):
            return t[:, bass.ds(i, 1), :].rearrange("p a c -> p (a c)")
        with nc.Block() as block:
            @block.sync
            def _(e):
                e.dma_start(gm[:, :, :], sums.rearrange("(i p) c -> p i c", p=PT)).then_inc(o_gm, 16)
                e.dma_start(gam[:, :], A["L0_gnn_ln_gamma"].rearrange("(a c) -> a c", a=1).to_broadcast([PT, C])).then_inc(o_in, 16)
                e.dma_start(bet[:, :], A["L0_gnn_ln_beta"].rearrange("(a c) -> a c", a=1).to_broadcast([PT, C])).then_inc(o_in, 16)

            @block.scalar
            def _(e):
                e.wait_ge(o_v, 1)
                e.activation(std[:, :], rstd[:, :], ACT.Sqrt).then_inc(o_s, 1)

            @block.vector
            def _(e):
                e.wait_ge(o_gm, 16)
                with e.Fori(0, TILES) as i:
                    step = counted(e, o_d, 3 * i)
                    step(e.bn_stats(stats[:, :], row(gm, i)))
                    hold(e, ticks)
                    step(e.bn_aggr(mv1[:, :], stats[:, :]))
                    step(e.tensor_copy(row(mv, i), mv1[:, :]))
                step = counted(e, o_d, 3 * TILES)
                step(e.tensor_scalar(rstd[:, :], mv[:, :, 1], 1e-5, None, ALU.add))
                e.sem_inc(o_v, 1)
                e.wait_ge(o_s, 1)
                step(e.reciprocal(rstd[:, :], std[:, :]))
                e.wait_ge(o_in, 32)
                with e.Fori(0, TILES) as i:
                    step = counted(e, o_d, 3 * TILES + 2 + 5 * i)
                    step(e.tensor_scalar(w[:, :], row(gm, i), mv[:, bass.ds(i, 1), 0], rstd[:, bass.ds(i, 1)], ALU.subtract, ALU.mult))
                    step(e.tensor_tensor(w[:, :], w[:, :], gam[:, :], ALU.mult))
                    step(e.tensor_tensor(w[:, :], w[:, :], bet[:, :], ALU.add))
                    step(e.scalar_tensor_tensor(out=w[:, :], in0=w[:, :], scalar=0.1, in1=w[:, :], op0=ALU.mult, op1=ALU.max))
                    step(e.tensor_tensor(row(acc, i), row(acc, i), w[:, :], ALU.add))


def ffn(nc, A, acc, xnT, ident, ones, out, ticks):
    with ExitStack() as ctx:
        sem = scoped(nc, ctx)
        def sb(name, shape, dt=F32):
            return ctx.enter_context(nc.sbuf_tensor(f"f_{name}", shape, dt))
        gate = sb("gate", [PT, TILES, XPT])
        b1 = sb("b1", [P, XPT, HC])
        with ExitStack() as gctx:
            def gsb(name, shape, dt=F32):
                return gctx.enter_context(nc.sbuf_tensor(f"fg_{name}", shape, dt))

            def gps(name, shape):
                return gctx.enter_context(nc.psum_tensor(f"fg_{name}", shape, F32))
            wg, bg, b2 = gsb("wg", [P, KC, XPT]), gsb("bg", [1, XPT]), gsb("b2", [XPT, C])
            xs, gT = gsb("xs", [P, KC, PT]), gsb("gT", [XPT, PT])
            lg, top = gsb("lg", [PT, XPT]), gsb("top", [PT, 8])
            at = gsb("at", [PT, 8], mybir.dt.uint32)
            atf, ew = gsb("atf", [PT, 8]), gsb("ew", [PT, 4])
            io_i, io = gsb("io_i", [PT, XPT], I32), gsb("io", [PT, XPT])
            g1, g2 = gsb("g1", [PT, XPT]), gsb("g2", [PT, XPT])
            pl, pg, pb = gps("pl", [PT, XPT]), gps("pg", [XPT, PT]), gps("pb", [PT, C])
            f_in, f_xs, f_l, f_d, f_g, f_t, f_tc, f_b, f_e, f_io, f_df = (sem(f"gate_{n}") for n in (
                "loaded", "x", "logits", "dve", "weights", "turned", "copied", "bias", "exp", "iota", "diff"))
            KS = 10
            with nc.Block() as block:
                @block.sync
                def _(e):
                    e.dma_start(wg[:, :, :], A["L0_ffn_Wg"].rearrange("(k p) n -> p k n", p=P)).then_inc(f_in, 16)
                    e.dma_start(bg[:, :], A["L0_ffn_bg"].rearrange("(a n) -> a n", a=1)).then_inc(f_in, 16)
                    e.dma_start(b2[:, :], A["L0_ffn_b2"]).then_inc(f_in, 16)
                    e.dma_start(b1[:, :, :], A["b1T"]).then_inc(f_in, 16)
                    e.wait_ge(f_in, 64)

                @block.gpsimd
                def _(e):
                    e.iota(io_i[:, :], [[1, XPT]], base=0, channel_multiplier=0).then_inc(f_io, 1)

                @block.scalar
                def _(e):
                    with e.Fori(0, TILES) as i:
                        e.wait_ge(f_l, i)
                        e.activation(xs[:, :, :], xnT[:, :, bass.ds(i * PT, PT)], ACT.Copy).then_inc(f_xs, 1)
                        e.wait_ge(f_df, i + 1)
                        e.activation(ew[:, 1:2], ew[:, 0:1], ACT.Exp).then_inc(f_e, 1)
                        e.wait_ge(f_t, i + 1)
                        e.activation(gT[:, :], pg[:, :], ACT.Copy).then_inc(f_tc, 1)

                @block.tensor
                def _(e):
                    e.wait_ge(f_in, 64)
                    with e.Fori(0, TILES) as i:
                        e.wait_ge(f_xs, i + 1)
                        e.wait_ge(f_d, i * KS)
                        for k in range(KC):
                            e.matmul(pl[:, :], xs[:, k, :], wg[:, k, :], start=(k == 0), stop=False)
                        e.matmul(pl[:, :], ones[0:1, 0:PT], bg[:, :], start=False, stop=True).then_inc(f_l, 1)
                        e.wait_ge(f_g, i + 1)
                        e.transpose(pg[:, :], g1[:, :], ident[0:PT, 0:PT]).then_inc(f_t, 1)
                        e.wait_ge(f_tc, i + 1)
                        e.matmul(pb[:, :], gT[:, :], b2[:, :], start=True, stop=True).then_inc(f_b, 1)

                @block.vector
                def _(e):
                    e.wait_ge(f_io, 1)
                    e.tensor_copy(io[:, :], io_i[:, :]).then_inc(f_io, 1)
                    e.wait_ge(f_io, 2)
                    with e.Fori(0, TILES) as i:
                        step = counted(e, f_d, i * KS)
                        e.wait_ge(f_l, i + 1)
                        step(e.tensor_copy(lg[:, :], pl[:, :]))
                        hold(e, ticks)
                        step(e.max(top[:, :], lg[:, :]))
                        hold(e, ticks)
                        step(e.max_index(at[:, :], top[:, :], lg[:, :]))
                        step(e.tensor_copy(atf[:, :], at[:, :]))
                        e.tensor_tensor(ew[:, 0:1], top[:, 1:2], top[:, 0:1], ALU.subtract).then_inc(f_df, 1)
                        e.wait_ge(f_e, i + 1)
                        step(e.tensor_scalar(ew[:, 2:3], ew[:, 1:2], 1.0, None, ALU.add))
                        step(e.reciprocal(ew[:, 2:3], ew[:, 2:3]))
                        step(e.tensor_tensor(ew[:, 3:4], ew[:, 1:2], ew[:, 2:3], ALU.mult))
                        step(e.tensor_scalar(g1[:, :], io[:, :], atf[:, 0:1], ew[:, 2:3], ALU.is_equal, ALU.mult))
                        step(e.tensor_scalar(g2[:, :], io[:, :], atf[:, 1:2], ew[:, 3:4], ALU.is_equal, ALU.mult))
                        e.tensor_tensor(g1[:, :], g1[:, :], g2[:, :], ALU.add).then_inc(f_g, 1)
                        e.wait_ge(f_g, i + 1)
                        e.tensor_copy(gate[:, bass.ds(i, 1), :].rearrange("p a x -> p (a x)"), g1[:, :])
                        e.wait_ge(f_b, i + 1)
                        a = acc[:, bass.ds(i, 1), :].rearrange("p a c -> p (a c)")
                        step(e.tensor_tensor(a, a, pb[:, :], ALU.add))
        w1 = sb("w1", [P, 2, KC, HID])
        w2 = sb("w2", [P, 2, HC, C])
        hid = sb("hid", [P, HC, GW])
        p1 = [ctx.enter_context(nc.psum_tensor(f"f_p1{i}", [P, GW], F32)) for i in range(4)]
        p2 = [ctx.enter_context(nc.psum_tensor(f"f_p2{i}", [PT, C], F32)) for i in range(4)]
        x_in = [sem(f"ffn_weights{i}") for i in range(2)]
        x_p1, x_h, x_p2, x_a, x_o = (sem(f"ffn_{n}") for n in ("hidden_sum", "hidden", "expert_sum", "added", "stored"))
        with nc.Block() as block:
            @block.sync
            def _(e):
                for x in range(XPT):
                    if x >= 2:
                        e.wait_ge(x_p2, (x - 1) * TILES)
                    e.dma_start(w1[:, x % 2, :, :], A["L0_ffn_W1"][x].rearrange("(k p) n -> p k n", p=P)).then_inc(x_in[x % 2], 16)
                    e.dma_start(w2[:, x % 2, :, :], A["L0_ffn_W2"][x].rearrange("(k p) n -> p k n", p=P)).then_inc(x_in[x % 2], 16)
                e.wait_ge(x_a, XPT * TILES + 4)
                n = PT * (TILES - 1)
                e.dma_start(out[0:n, :].rearrange("(i p) c -> p i c", p=PT), acc[:, 0:TILES - 1, :]).then_inc(x_o, 16)
                e.dma_start(out[n:N, :], acc[0:LAST, TILES - 1, :]).then_inc(x_o, 16)
                e.wait_ge(x_o, 32)

            @block.tensor
            def _(e):
                e.sem_inc(x_h, 4)
                e.sem_inc(x_a, 4)
                for x in range(XPT):
                    e.wait_ge(x_in[x % 2], 32 * (x // 2 + 1))
                    with e.Fori(0, GROUPS) as g:
                        for m in range(HC):
                            e.wait_ge(x_h, (x * GROUPS + g) * HC + m + 1)
                            for k in range(KC):
                                mm = e.matmul(p1[m % 4][:, :], w1[:, x % 2, k, m * P:(m + 1) * P], xnT[:, k, bass.ds(g * GW, GW)], start=(k == 0), stop=(k == KC - 1))
                            mm.then_inc(x_p1, 1)
                        e.wait_ge(x_h, (x * GROUPS + g + 1) * HC + 4)
                        for c in range(4):
                            e.wait_ge(x_a, (x * GROUPS + g) * 4 + c + 1)
                            for m in range(HC):
                                mm = e.matmul(p2[c][:, :], hid[:, m, c * PT:(c + 1) * PT], w2[:, x % 2, m, :], start=(m == 0), stop=(m == HC - 1))
                            mm.then_inc(x_p2, 1)

            @block.scalar
            def _(e):
                for x in range(XPT):
                    with e.Fori(0, GROUPS) as g:
                        for m in range(HC):
                            e.wait_ge(x_p1, (x * GROUPS + g) * HC + m + 1)
                            if m == 0:
                                e.wait_ge(x_p2, (x * GROUPS + g) * 4)
                            e.activation(hid[:, m, :], p1[m % 4][:, :], ACT.Gelu, bias=b1[:, x, m:m + 1]).then_inc(x_h, 1)

            @block.vector
            def _(e):
                for x in range(XPT):
                    with e.Fori(0, GROUPS) as g:
                        for c in range(4):
                            e.wait_ge(x_p2, (x * GROUPS + g) * 4 + c + 1)
                            a = acc[:, bass.ds(g * 4 + c, 1), :].rearrange("p a c -> p (a c)")
                            e.scalar_tensor_tensor(out=a, in0=p2[c][:, :], scalar=gate[:, bass.ds(g * 4 + c, 1), x], in1=a, op0=ALU.mult, op1=ALU.add).then_inc(x_a, 1)


def kernel(**inputs):
    import numpy as _np
    import concourse.bacc as _bacc
    from concourse import mybir as _mybir
    from concourse.bass_utils import run_bass_kernel_spmd as _run

    i = {k: _np.asarray(v) for k, v in inputs.items()}
    laid = {n: i[n] for n in ("x", "src", "dst", "edge_type_3", "L0_gnn_ln_gamma", "L0_gnn_ln_beta", "L0_mix_bqkv",
                              "L0_mix_bproj", "L0_mix_temperature", "L0_ffn_Wg", "L0_ffn_bg", "L0_ffn_W1",
                              "L0_ffn_W2", "L0_ffn_b2")}
    laid["convT"] = i["L0_gnn_conv_w"].transpose(0, 1, 3, 2)
    laid["wihT"] = i["L0_gnn_gru_wih"].transpose(0, 2, 1)
    laid["whhT"] = i["L0_gnn_gru_whh"].transpose(0, 2, 1)
    laid["bihT"] = i["L0_gnn_gru_bih"].reshape(3, 6, 128).transpose(2, 0, 1)
    laid["bhhT"] = i["L0_gnn_gru_bhh"].reshape(3, 6, 128).transpose(2, 0, 1)
    laid["WqkvT"] = i["L0_mix_Wqkv"].T
    laid["WprojT"] = i["L0_mix_Wproj"].T
    laid["b1T"] = i["L0_ffn_b1"].reshape(8, 8, 128).transpose(2, 0, 1)
    nc = _bacc.Bacc("TRN2", target_bir_lowering=False, num_devices=1)
    arrays, A = {}, {}
    for name, a in laid.items():
        a = _np.ascontiguousarray(a)
        arrays[f"in_{name}"] = a
        A[name] = nc.dram_tensor(f"in_{name}", a.shape, _mybir.dt.from_np(a.dtype), kind="ExternalInput").ap()
    A["out"] = nc.dram_tensor("out_0", (3125, 256), F32, kind="ExternalOutput").ap()
    gps_layer_kernel(nc, A)
    r = _run(nc, [arrays], core_ids=[0])
    return r.results[0]["out_0"]
```

```python
import concourse.bass as bass
from concourse import mybir
from contextlib import ExitStack

F32 = mybir.dt.float32
F16 = mybir.dt.float16
BF16 = mybir.dt.bfloat16
I16 = mybir.dt.int16
I32 = mybir.dt.int32
ALU = mybir.AluOpType
ACT = mybir.ActivationFunctionType
AX = mybir.AxisListType

N, C, E = 3125, 256, 50000
STEPS, TYPES = 3, 3
P = 128
KC = C // P
PT = 112
TILES = 28
NP = PT * TILES
GW = 4 * PT
GROUPS = NP // GW
LAST = N - PT * (TILES - 1)
DT = 64
TG = GW // DT
NT = GROUPS * TG
NKEY = TYPES * DT
TYPEKEY = 4096
NODST = 4000
EROWS = E // P
EREST = E - EROWS * P
EB = 4
NCH = EB * P
DEEP = 32
R = 8
HEADS, HD = 8, 32
ND = HD // 2 + 1
FEAT = ND * HD + HD + 1
FCH = (FEAT + P - 1) // P
FP = FCH * P
VD = HD + 1
SC = float(HD) ** 0.25
XPT, HID = 8, 1024
HC = HID // P
ST = 2 * P
SLOTS = (2 * NP // ST + XPT) * ST


def counted(eng, sem, base):
    count = [0]

    def step(ins):
        count[0] += 1
        ins.then_inc(sem, 1)
        eng.wait_ge(sem, base + count[0])
        return count[0]
    return step


def hold(e, ticks):
    e.tensor_copy(ticks[0][0:1, 1:2], ticks[0][0:1, 0:1])


def hold_pool(e, ticks, held, n):
    e.wait_ge(held, n + 1)
    t = ticks[1]
    e.tensor_tensor(t[0:1, 1:2], t[0:1, 0:1], t[0:1, 0:1], ALU.add).then_inc(held, 1)


def scoped(nc, ctx):
    mine = []

    def sem(name):
        mine.append(nc.alloc_semaphore(name))
        return mine[-1]

    def give_back():
        nc.clear_and_free_semaphores(mine)
        nc.all_engine_barrier()
    ctx.callback(give_back)
    return sem


def gps_layer_kernel(nc, A):
    def sb(name, shape, dt=F32):
        return nc.alloc_sbuf_tensor(name, shape, dt)

    sem = nc.alloc_semaphore
    out = A["out"]
    table0 = nc.dram_tensor("xn_rows", [NP, 2 * C], F16).ap()
    tables = [table0] + [nc.dram_tensor(f"h_rows{s}", [TYPES * NP, 2 * C], F16).ap() for s in (1, 2)]
    hT0 = nc.dram_tensor("xn_cols", [P, KC, NP], F32).ap()
    hTs = [nc.dram_tensor(f"h_cols{s}", [TYPES, P, KC, NP], F32).ap() for s in (1, 2)]

    sums = nc.dram_tensor("h_sums", [NP, C], F32).ap()
    slots_in = nc.dram_tensor("slots_in", [SLOTS, C], F32).ap()
    slots_out = nc.dram_tensor("slots_out", [SLOTS, C], F32).ap()
    acc = sb("acc", [PT, TILES, C])
    ident = sb("ident", [P, P])
    ones = sb("ones", [1, 512])
    keys = sb("keys", [P, NCH])
    idx0 = sb("idx0", [P, NCH], I32)
    idx1 = sb("idx1", [P, NCH], I32)
    tab = sb("tab", [1, 160], I32)
    iota_keys = sb("iota_keys", [P, TYPES, DT], I16)
    tile_keys = sb("tile_keys", [P, TYPES, DT], I16)
    s_z = sem("const_zeroed")
    s_c = sem("const_ready")
    cdve = sem("const_dve")
    iota_i = sb("iota_i", [P, TYPES, DT], I32)
    ticks = sb("tick_d", [1, 2]), sb("tick_p", [1, 2])
    with nc.Block() as block:
        @block.gpsimd
        def _(e):
            e.memset(ident[:, :], 0.0).then_inc(s_z, 1)
            e.wait_ge(s_z, 1)
            e.affine_select(out=ident[:, :], in_=ident[:, :], compare_op=ALU.not_equal, fill=1.0,
                            base=0, pattern=[[-1, P]], channel_multiplier=1).then_inc(s_c, 1)
            e.memset(ones[:, :], 1.0).then_inc(s_c, 1)
            e.iota(iota_i[:, :, :], [[TYPEKEY, TYPES], [1, DT]], base=0, channel_multiplier=0).then_inc(s_c, 1)

        @block.vector
        def _(e):
            for t in ticks:
                e.memset(t[:, :], 0.0)
            e.wait_ge(s_c, 3)
            e.tensor_copy(iota_keys[:, :, :], iota_i[:, :, :]).then_inc(cdve, 1)
            e.wait_ge(cdve, 1)

    edge_tables(nc, A, ident, keys, idx0, idx1, tab)
    with nc.sbuf_tensor("xnT", [P, KC, NP], F32) as xnT:
        normalise(nc, "in", acc, xnT, ident, load=A["x"], rows=table0, cols=hT0)
        mix(nc, A, acc, xnT, ident, ones)
    for s in range(STEPS):
        gnn_step(nc, A, s, tables, [hT0] + hTs, idx0 if s == 0 else idx1, keys, tab,
                 iota_keys, tile_keys, ident, sums, ticks)
    gnn_out(nc, A, acc, sums)
    ffn(nc, A, acc, ident, ones, slots_in, slots_out, out)


def edge_tables(nc, A, ident, keys, idx0, idx1, tab):
    with ExitStack() as ctx:
        sem = scoped(nc, ctx)
        def sb(name, shape, dt=F32):
            return ctx.enter_context(nc.sbuf_tensor(name, shape, dt))

        def ps(name, shape):
            return ctx.enter_context(nc.psum_tensor(name, shape, F32))
        ei = sb("ei", [P, 3, EB, P], I32)
        ef = sb("ef", [P, 3, EB, P])
        rows = sb("rows", [P, 3, EB, P])
        lim = sb("lim", [P, 2, EB])
        bcast = sb("lim_bcast", [P, 2, EB, NT])
        onesm = sb("onesm", [P, NT])
        base_i = sb("base_i", [1, NT], I32)
        base_r = sb("base_r", [1, NT])
        tlo = sb("tlo", [NT, 1])
        thi = sb("thi", [NT, 1])
        cio_i = sb("cio_i", [NT, NCH], I32)
        cio = sb("cio", [NT, NCH])
        member = sb("member", [NT, NCH])
        work = sb("work", [NT, NCH])
        col = sb("col", [NT, 8])
        col_i = sb("col_i", [NT, 1], I32)
        tri = sb("tri", [NT, NT + 1])
        pt = [ps(f"et{i}", [P, EB, P]) for i in range(3)]
        pl = [ps(f"el{i}", [NT, NCH]) for i in range(2)]
        pb = ps("eb", [NT, 1])
        pr = ps("er", [1, 256])
        e_set, e_in, e_io, e_d, e_row, e_t, e_lim, e_pl, e_n, e_r = (sem(f"edge_{n}") for n in (
            "set", "loaded", "iota", "dve", "rows", "turned", "limits", "limits_turned", "counts", "table"))
        with nc.Block() as block:
            @block.sync
            def _(e):
                e.wait_ge(e_set, 3)
                for k, name in enumerate(("src", "dst", "edge_type_3")):
                    a = A[name]
                    for b in range(3):
                        e.dma_start(ei[:, k, b, :], a[b * P * P:(b + 1) * P * P].rearrange("(r q) -> r q", q=P)).then_inc(e_in, 16)
                    n = EROWS - 3 * P
                    e.dma_start(ei[0:n, k, 3, :], a[3 * P * P:EROWS * P].rearrange("(r q) -> r q", q=P)).then_inc(e_in, 16)
                    e.dma_start(ei[n:n + 1, k, 3, 0:EREST], a[EROWS * P:E].rearrange("(r q) -> r q", r=1)).then_inc(e_in, 16)

            @block.gpsimd
            def _(e):
                e.iota(base_i[:, :], [[DT, NT]], base=0, channel_multiplier=0).then_inc(e_io, 1)
                e.iota(cio_i[:, :], [[1, NCH]], base=0, channel_multiplier=0).then_inc(e_io, 1)
                e.memset(tri[:, :], 1.0).then_inc(e_io, 1)
                e.wait_ge(e_io, 3)
                e.affine_select(out=tri[:, :], in_=tri[:, :], compare_op=ALU.is_gt, fill=0.0,
                                base=0, pattern=[[1, NT + 1]], channel_multiplier=-1).then_inc(e_io, 1)

            @block.vector
            def _(e):
                step = counted(e, e_d, 0)
                e.memset(ei[:, 0, 3, :], 0).then_inc(e_set, 1)
                e.memset(ei[:, 1, 3, :], NODST).then_inc(e_set, 1)
                e.memset(ei[:, 2, 3, :], 0).then_inc(e_set, 1)
                e.memset(onesm[:, :], 1.0)
                e.wait_ge(e_in, 16 * 15)
                step(e.tensor_copy(ef[:, :, :, :], ei[:, :, :, :]))
                e.tensor_copy(rows[:, 0, :, :], ef[:, 0, :, :]).then_inc(e_row, 1)
                e.scalar_tensor_tensor(out=rows[:, 1, :, :], in0=ef[:, 2, :, :], scalar=float(NP), in1=ef[:, 0, :, :], op0=ALU.mult, op1=ALU.add).then_inc(e_row, 1)
                e.scalar_tensor_tensor(out=rows[:, 2, :, :], in0=ef[:, 2, :, :], scalar=float(TYPEKEY), in1=ef[:, 1, :, :], op0=ALU.mult, op1=ALU.add).then_inc(e_row, 1)
                step(e.tensor_reduce(lim[:, 0, :], ef[:, 1, :, :], AX.X, ALU.min))
                step(e.tensor_reduce(lim[:, 1, :], ef[:, 1, :, :], AX.X, ALU.max))
                for k in range(2):
                    for b in range(EB):
                        e.tensor_scalar(bcast[:, k, b, :], onesm[:, :], lim[:, k, b:b + 1], None, ALU.mult).then_inc(e_lim, 1)
                e.wait_ge(e_io, 4)
                step(e.tensor_copy(base_r[:, :], base_i[:, :]))
                e.tensor_copy(cio[:, :], cio_i[:, :]).then_inc(e_lim, 1)
                e.wait_ge(e_t, 3)
                for k, t in enumerate((idx0, idx1, keys)):
                    e.tensor_copy(t[:, :], pt[k][:, :, :].rearrange("p a b -> p (a b)")).then_inc(e_row, 1)
                e.wait_ge(e_pl, 3)
                step(e.tensor_copy(tlo[:, :], pb[:, :]))
                step(e.tensor_scalar(thi[:, :], tlo[:, :], float(DT - 1), None, ALU.add))
                step(e.tensor_scalar(work[:, :], pl[0][:, :], thi[:, 0:1], None, ALU.is_le))
                step(e.scalar_tensor_tensor(out=member[:, :], in0=pl[1][:, :], scalar=tlo[:, 0:1], in1=work[:, :], op0=ALU.is_ge, op1=ALU.mult))
                step(e.scalar_tensor_tensor(out=work[:, :], in0=cio[:, :], scalar=-1024.0, in1=member[:, :], op0=ALU.add, op1=ALU.mult))
                step(e.tensor_reduce(col[:, 0:1], work[:, :], AX.X, ALU.min))
                step(e.scalar_tensor_tensor(out=work[:, :], in0=cio[:, :], scalar=1.0, in1=member[:, :], op0=ALU.add, op1=ALU.mult))
                step(e.tensor_reduce(col[:, 1:2], work[:, :], AX.X, ALU.max))
                step(e.tensor_scalar(col[:, 2:3], col[:, 1:2], 0.0, None, ALU.is_gt))
                step(e.scalar_tensor_tensor(out=col[:, 3:4], in0=col[:, 0:1], scalar=1024.0, in1=col[:, 2:3], op0=ALU.add, op1=ALU.mult))
                step(e.tensor_scalar(col[:, 4:5], col[:, 3:4], 1.0, None, ALU.add))
                step(e.tensor_tensor(col[:, 5:6], col[:, 4:5], col[:, 1:2], ALU.max))
                step(e.scalar_tensor_tensor(out=col[:, 6:7], in0=col[:, 5:6], scalar=float(R - 1), in1=col[:, 3:4], op0=ALU.add, op1=ALU.subtract))
                step(e.tensor_copy(col_i[:, :], col[:, 6:7]))
                step(e.tensor_scalar(col_i[:, :], col_i[:, :], R.bit_length() - 1, None, ALU.logical_shift_right))
                e.tensor_copy(col[:, 7:8], col_i[:, :]).then_inc(e_n, 1)
                e.wait_ge(e_r, 1)
                e.tensor_copy(tab[:, 0:NT + 1], pr[:, 0:NT + 1]).then_inc(e_n, 1)
                e.tensor_copy(tab[:, 80:80 + NT], pr[:, 80:80 + NT]).then_inc(e_n, 1)

            @block.tensor
            def _(e):
                e.wait_ge(e_row, 3)
                for k in range(3):
                    for b in range(EB):
                        last = e.transpose(pt[k][:, b, :], rows[:, k, b, :], ident[:, :])
                    last.then_inc(e_t, 1)
                e.wait_ge(e_lim, 9)
                for k in range(2):
                    for b in range(EB):
                        last = e.matmul(pl[k][:, b * P:(b + 1) * P], bcast[:, k, b, :], ident[:, :], start=True, stop=True)
                    last.then_inc(e_pl, 1)
                e.matmul(pb[:, :], base_r[:, :], ident[0:1, 0:1], start=True, stop=True).then_inc(e_pl, 1)
                e.wait_ge(e_n, 1)
                e.matmul(pr[:, 0:NT + 1], col[:, 7:8], tri[:, :], start=True, stop=True)
                e.matmul(pr[:, 80:80 + NT], col[:, 3:4], ident[0:NT, 0:NT], start=True, stop=True).then_inc(e_r, 1)


def normalise(nc, tag, acc, xnT, ident, load=None, rows=None, cols=None, keep=None):
    with ExitStack() as ctx:
        sem = scoped(nc, ctx)
        stats = ctx.enter_context(nc.sbuf_tensor(f"{tag}_stats", [PT, TILES, 6], F32))
        mv = ctx.enter_context(nc.sbuf_tensor(f"{tag}_mv", [PT, TILES, 2], F32))
        rstd = ctx.enter_context(nc.sbuf_tensor(f"{tag}_rstd", [PT, TILES], F32))
        std = ctx.enter_context(nc.sbuf_tensor(f"{tag}_std", [PT, TILES], F32))
        gm = ctx.enter_context(nc.sbuf_tensor(f"{tag}_gm", [PT, TILES, 2 * C], F16)) if rows is not None else None
        xr = ctx.enter_context(nc.sbuf_tensor(f"{tag}_xr", [PT, 2, C], F32))
        pt = [ctx.enter_context(nc.psum_tensor(f"{tag}_pt{i}", [P, KC, 256], F32)) for i in range(2)]
        n_z, n_in, n_d, n_v, n_s, n_x, n_t, n_c, n_o, n_g, n_l, n_b = (sem(f"norm_{tag}_{n}") for n in (
            "zeroed", "loaded", "dve", "var", "std", "rows", "turned", "copied", "stored", "high", "low", "stats"))
        with nc.Block() as block:
            @block.vector
            def _(e):
                if load is not None:
                    e.memset(acc[:, TILES - 1, :], 0.0).then_inc(n_z, 1)
                    e.wait_ge(n_in, 32)
                with e.Fori(0, TILES) as i:
                    e.bn_stats(stats[:, bass.ds(i, 1), :].rearrange("p a c -> p (a c)"), acc[:, bass.ds(i, 1), :].rearrange("p a c -> p (a c)")).then_inc(n_b, 1)
                e.wait_ge(n_b, TILES)
                for i in range(TILES):
                    e.bn_aggr(mv[:, i, :], stats[:, i, :]).then_inc(n_b, 1)
                e.wait_ge(n_b, 2 * TILES)
                step = counted(e, n_d, 0)
                step(e.tensor_scalar(rstd[:, :], mv[:, :, 1], 1e-5, None, ALU.add))
                e.sem_inc(n_v, 1)
                e.wait_ge(n_s, 1)
                step(e.reciprocal(rstd[:, :], std[:, :]))
                with e.Fori(0, TILES // 2) as pair:
                    i = pair * 2
                    for b in range(2):
                        e.wait_ge(n_t, i + b + 1)
                        if keep is not None:
                            e.wait_ge(n_g, i + b + 1)
                        e.tensor_scalar(xr[:, b, :], acc[:, bass.ds(i + b, 1), :].rearrange("p a c -> p (a c)"),
                                        mv[:, bass.ds(i + b, 1), 0], rstd[:, bass.ds(i + b, 1)],
                                        ALU.subtract, ALU.mult).then_inc(n_x, 1)
                        if rows is not None:
                            e.wait_ge(n_g, i + b + 1)
                            e.tensor_tensor(gm[:, bass.ds(i + b, 1), C:2 * C].rearrange("p a c -> p (a c)"), xr[:, b, :],
                                            gm[:, bass.ds(i + b, 1), 0:C].rearrange("p a c -> p (a c)"), ALU.subtract).then_inc(n_l, 1)

            @block.scalar
            def _(e):
                e.wait_ge(n_v, 1)
                e.activation(std[:, :], rstd[:, :], ACT.Sqrt).then_inc(n_s, 1)
                if keep is not None:
                    e.sem_inc(n_g, 2)
                with e.Fori(0, TILES // 2) as pair:
                    i = pair * 2
                    for b in range(2):
                        e.wait_ge(n_x, i + b + 1)
                        if rows is not None:
                            e.activation(gm[:, bass.ds(i + b, 1), 0:C].rearrange("p a c -> p (a c)"), xr[:, b, :], ACT.Copy).then_inc(n_g, 1)
                        if keep is not None:
                            e.activation(keep[:, bass.ds(i + b, 1), :].rearrange("p a c -> p (a c)"), xr[:, b, :], ACT.Copy).then_inc(n_g, 1)
                        e.wait_ge(n_t, i + b + 3)
                        e.activation(xnT[:, :, bass.ds((i + b) * PT, PT)], pt[b][:, :, 0:PT], ACT.Copy).then_inc(n_c, 1)

            @block.tensor
            def _(e):
                e.sem_inc(n_c, 2)
                e.sem_inc(n_t, 2)
                with e.Fori(0, TILES // 2) as pair:
                    i = pair * 2
                    for b in range(2):
                        e.wait_ge(n_x, i + b + 1)
                        e.wait_ge(n_c, i + b + 1)
                        for k in range(KC):
                            last = e.transpose(pt[b][:, k, 0:PT], xr[:, b, k * P:(k + 1) * P], ident[0:PT, 0:PT])
                        last.then_inc(n_t, 1)

            @block.sync
            def _(e):
                if load is not None:
                    n = PT * (TILES - 1)
                    e.dma_start(acc[:, 0:TILES - 1, :], load[0:n, :].rearrange("(i p) c -> p i c", p=PT)).then_inc(n_in, 16)
                    e.wait_ge(n_z, 1)
                    e.dma_start(acc[0:LAST, TILES - 1, :], load[n:N, :]).then_inc(n_in, 16)
                    e.wait_ge(n_l, TILES)
                    e.dma_start(rows.rearrange("(i p) c -> p i c", p=PT), gm[:, :, :]).then_inc(n_o, 16)
                    e.wait_ge(n_c, TILES + 2)
                    e.dma_start(cols, xnT[:, :, :]).then_inc(n_o, 16)
                    e.wait_ge(n_o, 32)


def mix(nc, A, acc, xnT, ident, ones):
    with ExitStack() as ctx:
        m_parts = ctx.enter_context(nc.sbuf_tensor("moments", [P, HEADS * FCH, 3, VD], BF16))
        qT = [ctx.enter_context(nc.sbuf_tensor(f"q_cols{i}", [P, KC, NP], F16)) for i in range(2)]
        mix_moments(nc, A, xnT, ident, ones, m_parts, qT)
        yo = ctx.enter_context(nc.sbuf_tensor("mix_y", [PT, TILES, C], F32))
        mix_queries(nc, ident, m_parts, qT, yo)
        mix_project(nc, A, acc, ident, ones, yo)


def mix_moments(nc, A, xnT, ident, ones, m_parts, qT):
    with ExitStack() as ctx:
        sem = scoped(nc, ctx)

        def sb(name, shape, dt=F32):
            return ctx.enter_context(nc.sbuf_tensor(f"mk_{name}", shape, dt))

        def ps(name, shape):
            return ctx.enter_context(nc.psum_tensor(f"mk_{name}", shape, F32))
        w = sb("w", [P, KC, 3 * C])
        wb = sb("wb", [1, 3 * C])
        temp = sb("temp", [P, HEADS])
        tsq = sb("tsq", [P, HEADS])
        factor = sb("factor", [P, HEADS, FCH])
        M = sb("M", [P, HEADS * FCH, VD])
        mask = sb("mask", [PT, TILES])
        xs = [sb(f"xs{b}", [P, KC, PT]) for b in range(2)]
        sq = sb("sq", [PT, 2 * C])
        ss = sb("ss", [PT, 3, 2 * HEADS])
        one = sb("one", [PT, HEADS])
        ext = sb("ext", [PT, HEADS, HD + HD // 2])
        qn = sb("qn", [PT, C])
        F = sb("F", [PT, HEADS, ND * HD + HD])
        Fh, Fl = ([sb(f"F{n}{b}", [PT, HEADS, FP], F16) for b in range(2)] for n in "hl")
        vf, vr = sb("vf", [PT, HEADS, VD]), sb("vr", [PT, HEADS, VD])
        v = [[sb(f"v{b}{i}", [PT, HEADS, VD], BF16) for i in range(3)] for b in range(2)]
        zero = sb("zero", [P, 15 * VD])
        pqk = [ps(f"pqk{b}", [PT, 2 * C]) for b in range(2)]
        pv = [ps(f"pv{b}", [PT, C]) for b in range(2)]
        pm = [ps(f"pm{i}", [P, 15 * VD]) for i in range(3)]
        pqt = ps("pqt", [P, KC, PT])
        S = {n: sem(f"mk_{n}") for n in ("in", "set", "vset", "dve", "pool", "xs", "proj", "pfree", "sq", "ss", "sqrt", "qn", "qt",
                                         "q_hi", "q_lo", "feat", "f_hi", "f_lo", "f_lo_pool", "vf", "v_parts", "mm", "out")}
        NF = ND * HD + HD
        H2 = HEADS // 2
        PAIRS = TILES // 2

        def tiles(body):
            def run(e):
                with e.Fori(0, PAIRS - 1) as p:
                    for b in range(2):
                        body(e, p * 2 + b, b, True)
                body(e, TILES - 2, 0, True)
                body(e, TILES - 1, 1, False)
            return run

        def ext_window():
            a = ext[:, :, :].ap
            return bass.AP(ext[:, :, :].tensor, ext[:, :, :].offset, [list(a[0]), [HD + HD // 2, HEADS], [1, ND], [1, HD]])

        with nc.Block() as block:
            @block.sync
            def _(e):
                e.dma_start(w[:, :, :], A["WqkvT"].rearrange("(k p) n -> p k n", p=P)).then_inc(S["in"], 16)
                e.dma_start(wb[:, :], A["L0_mix_bqkv"].rearrange("(a n) -> a n", a=1)).then_inc(S["in"], 16)
                e.dma_start(temp[:, :], A["L0_mix_temperature"].rearrange("a h b c -> (a b c) h").to_broadcast([P, HEADS])).then_inc(S["in"], 16)

            @block.gpsimd
            def _(e):
                e.memset(mask[:, :], 1.0 / N).then_inc(S["set"], 1)
                e.wait_ge(S["set"], 1)
                m = mask[:, TILES - 1:TILES]
                e.affine_select(out=m, in_=m, compare_op=ALU.is_ge, fill=0.0, base=LAST - 1,
                                pattern=[[0, 1]], channel_multiplier=-1).then_inc(S["set"], 1)
                e.sem_inc(S["v_parts"], 1)
                e.wait_ge(S["vset"], 1)
                none = zero[0:PT, 0:HEADS * VD].rearrange("p (h e) -> p h e", h=HEADS)
                e.sem_inc(S["f_lo_pool"], 1)

                def body(e, i, b, more):
                    n = 3 * i
                    e.wait_ge(S["vf"], i + 1)
                    e.wait_ge(S["mm"], i + 1)
                    e.tensor_tensor(v[b][0][:, :, :], vf[:, :, :], none, ALU.subtract).then_inc(S["pool"], 1)
                    e.wait_ge(S["pool"], n + 1)
                    e.tensor_tensor(vr[:, :, :], vf[:, :, :], v[b][0][:, :, :], ALU.subtract).then_inc(S["pool"], 1)
                    e.wait_ge(S["pool"], n + 2)
                    e.tensor_tensor(v[b][1][:, :, :], vr[:, :, :], none, ALU.subtract).then_inc(S["pool"], 1)
                    e.wait_ge(S["pool"], n + 3)
                    e.tensor_tensor(v[b][2][:, :, :], vr[:, :, :], v[b][1][:, :, :], ALU.subtract).then_inc(S["v_parts"], 1)
                    e.wait_ge(S["f_hi"], 2 * i + 2)
                    e.tensor_tensor(Fl[b][:, H2:HEADS, 0:NF], F[:, H2:HEADS, :], Fh[b][:, H2:HEADS, 0:NF], ALU.subtract).then_inc(S["f_lo_pool"], 1)
                tiles(body)(e)

            @block.scalar
            def _(e):
                def load_x(e, i, b):
                    e.wait_ge(S["proj"], i + 1)
                    e.activation(xs[b][:, :, :], xnT[:, :, bass.ds(i * PT, PT)], ACT.Copy).then_inc(S["xs"], 1)

                def body(e, i, b, more):
                    e.wait_ge(S["proj"], i + 3)
                    e.activation(sq[:, :], pqk[b][:, :], ACT.Square).then_inc(S["sq"], 1)
                    e.wait_ge(S["ss"], i + 1)
                    e.activation(ss[:, 1, :], ss[:, 0, :], ACT.Sqrt).then_inc(S["sqrt"], 1)
                    if more:
                        load_x(e, i + 1, 1 - b)
                    e.wait_ge(S["mm"], i + 1)
                    for half in range(2):
                        e.wait_ge(S["feat"], 2 * i + half + 1)
                        hs = slice(half * H2, (half + 1) * H2)
                        e.activation(Fh[b][:, hs, 0:NF], F[:, hs, :], ACT.Copy).then_inc(S["f_hi"], 1)
                    e.wait_ge(S["qt"], i + 2)
                    e.activation(qT[0][:, :, bass.ds(i * PT, PT)], pqt[:, :, :], ACT.Copy).then_inc(S["q_hi"], 1)
                load_x(e, 0, 0)
                tiles(body)(e)

            @block.tensor
            def _(e):
                e.sem_inc(S["proj"], 2)
                e.sem_inc(S["qt"], 1)
                e.sem_inc(S["mm"], 2)
                e.wait_ge(S["in"], 16 * 3)
                e.wait_ge(S["vset"], 1)
                for m in range(3):
                    e.matmul(pm[m][:, :], zero[:, 0:P], zero[:, :], start=True, stop=False, skip_group_check=True)

                def project(e, i, b):
                    e.wait_ge(S["xs"], i + 1)
                    e.wait_ge(S["pfree"], i + 1)
                    for o, bank, n in ((0, pqk[b], 2 * C), (2 * C, pv[b], C)):
                        for k in range(KC):
                            e.matmul(bank[:, :], xs[b][:, k, :], w[:, k, o:o + n], start=(k == 0), stop=False)
                        mm = e.matmul(bank[:, :], ones[0:1, 0:PT], wb[:, o:o + n], start=False, stop=True)
                    mm.then_inc(S["proj"], 1)

                def body(e, i, b, more):
                    e.wait_ge(S["qn"], i + 1)
                    e.wait_ge(S["q_lo"], i + 1)
                    for k in range(KC):
                        mm = e.transpose(pqt[:, k, :], qn[:, k * P:(k + 1) * P], ident[0:PT, 0:PT])
                    mm.then_inc(S["qt"], 1)
                    if more:
                        project(e, i + 1, 1 - b)
                    e.wait_ge(S["f_lo"], i + 1)
                    e.wait_ge(S["f_lo_pool"], i + 2)
                    e.wait_ge(S["v_parts"], i + 2)
                    for u in range(HEADS * FCH):
                        h, c, j = u // FCH, u % FCH, u % 15
                        for f, parts in ((Fh[b], v[b]), (Fl[b], v[b][0:2])):
                            for part in parts:
                                mm = e.matmul(pm[u // 15][:, j * VD:(j + 1) * VD], f[:, h, c * P:(c + 1) * P], part[:, h, :],
                                              start=False, stop=False, skip_group_check=True)
                    mm.then_inc(S["mm"], 1)
                project(e, 0, 0)
                tiles(body)(e)

            @block.vector
            def _(e):
                step = counted(e, S["vset"], 0)
                step(e.memset(zero[:, :], 0.0))
                step(e.memset(one[:, :], 1.0))
                for f in Fh + Fl:
                    step(e.memset(f[:, :, NF:FP], 0.0))
                for f in Fh:
                    step(e.memset(f[:, :, NF:NF + 1], 1.0))
                e.wait_ge(S["in"], 16 * 3)
                step(e.tensor_tensor(tsq[:, :], temp[:, :], temp[:, :], ALU.mult))
                step(e.tensor_scalar(factor[:, :, :], tsq[:, :].unsqueeze(2).to_broadcast([P, HEADS, FCH]), 1.0 / 16, None, ALU.mult))
                for c in (0, FCH - 1):
                    step(e.tensor_scalar(factor[0:HD, :, c], factor[0:HD, :, c], 0.5, None, ALU.mult))
                step(e.tensor_scalar(factor[HD:2 * HD, :, FCH - 1], temp[HD:2 * HD, :], SC ** 2, None, ALU.mult))
                step(e.memset(factor[2 * HD:3 * HD, :, FCH - 1], 16 * SC ** 4))
                e.wait_ge(S["set"], 2)
                e.sem_inc(S["pfree"], 2)
                e.sem_inc(S["q_lo"], 1)
                KS = 7

                def body(e, i, b, more):
                    step = counted(e, S["dve"], KS * i)
                    e.wait_ge(S["sq"], i + 1)
                    e.tensor_reduce(ss[:, 0, :], sq[:, :].rearrange("p (h d) -> p h d", h=2 * HEADS), AX.X, ALU.add).then_inc(S["ss"], 1)
                    e.wait_ge(S["v_parts"], i + 1)
                    e.tensor_scalar(vf[:, :, 1:VD], pv[b][:, :].rearrange("p (h d) -> p h d", h=HEADS), mask[:, bass.ds(i, 1)], None, ALU.mult)
                    e.tensor_scalar(vf[:, :, 0:1], one[:, :].unsqueeze(2), mask[:, bass.ds(i, 1)], None, ALU.mult).then_inc(S["vf"], 1)
                    e.wait_ge(S["sqrt"], i + 1)
                    step(e.tensor_scalar(ss[:, 2, 0:HEADS], ss[:, 1, 0:HEADS], SC, 1e-12, ALU.mult, ALU.max))
                    step(e.tensor_scalar(ss[:, 2, HEADS:2 * HEADS], ss[:, 1, HEADS:2 * HEADS], 1e-12, None, ALU.max))
                    step(e.reciprocal(ss[:, 2, :], ss[:, 2, :]))
                    step(e.tensor_scalar(ss[:, 2, 0:HEADS], ss[:, 2, 0:HEADS], 4 * SC * SC, None, ALU.mult))
                    step(e.tensor_scalar(ss[:, 2, HEADS:2 * HEADS], ss[:, 2, HEADS:2 * HEADS], 4 * SC, None, ALU.mult))
                    e.wait_ge(S["qt"], i + 1)
                    e.tensor_tensor(qn[:, :].rearrange("p (h d) -> p h d", h=HEADS), pqk[b][:, 0:C].rearrange("p (h d) -> p h d", h=HEADS),
                                    ss[:, 2, 0:HEADS].unsqueeze(2).to_broadcast([PT, HEADS, HD]), ALU.mult).then_inc(S["qn"], 1)
                    step(e.tensor_tensor(ext[:, :, 0:HD], pqk[b][:, C:2 * C].rearrange("p (h d) -> p h d", h=HEADS),
                                         ss[:, 2, HEADS:2 * HEADS].unsqueeze(2).to_broadcast([PT, HEADS, HD]), ALU.mult))
                    e.sem_inc(S["pfree"], 1)
                    step(e.tensor_copy(ext[:, :, HD:HD + HD // 2], ext[:, :, 0:HD // 2]))
                    win = ext_window()
                    for half in range(2):
                        if half:
                            e.wait_ge(S["f_lo_pool"], i + 1)
                        hs = slice(half * H2, (half + 1) * H2)
                        e.tensor_copy(F[:, hs, ND * HD:NF], ext[:, hs, 0:HD])
                        for h in range(half * H2, (half + 1) * H2):
                            ins = e.tensor_tensor(F[:, h, 0:ND * HD].rearrange("p (d j) -> p d j", d=ND),
                                                  ext[:, h, 0:HD].unsqueeze(1).to_broadcast([PT, ND, HD]), win[:, h, :, :], ALU.mult)
                        ins.then_inc(S["feat"], 1)
                    e.wait_ge(S["f_hi"], 2 * i + 1)
                    e.tensor_tensor(Fl[b][:, 0:H2, 0:NF], F[:, 0:H2, :], Fh[b][:, 0:H2, 0:NF], ALU.subtract).then_inc(S["f_lo"], 1)
                    e.wait_ge(S["q_hi"], i + 1)
                    e.tensor_tensor(qT[1][:, :, bass.ds(i * PT, PT)], pqt[:, :, :], qT[0][:, :, bass.ds(i * PT, PT)], ALU.subtract).then_inc(S["q_lo"], 1)
                tiles(body)(e)
                e.wait_ge(S["mm"], TILES + 2)
                step = counted(e, S["out"], 0)
                for m in range(3):
                    n = min(15, HEADS * FCH - 15 * m)
                    step(e.tensor_copy(M[:, 15 * m:15 * m + n, :], pm[m][:, 0:n * VD].rearrange("p (u e) -> p u e", e=VD)))
                step(e.tensor_tensor(M[:, :, :], M[:, :, :], factor[:, :, :].rearrange("p h c -> p (h c)").unsqueeze(2).to_broadcast([P, HEADS * FCH, VD]), ALU.mult))
                step(e.tensor_copy(m_parts[:, :, 0, :], M[:, :, :]))
                step(e.tensor_tensor(M[:, :, :], M[:, :, :], m_parts[:, :, 0, :], ALU.subtract))
                step(e.tensor_copy(m_parts[:, :, 1, :], M[:, :, :]))
                step(e.tensor_tensor(m_parts[:, :, 2, :], M[:, :, :], m_parts[:, :, 1, :], ALU.subtract))


def mix_queries(nc, ident, m_parts, qT, yo):
    with ExitStack() as ctx:
        sem = scoped(nc, ctx)

        def sb(name, shape, dt=F32):
            return ctx.enter_context(nc.sbuf_tensor(f"mq_{name}", shape, dt))

        def ps(name, shape):
            return ctx.enter_context(nc.psum_tensor(f"mq_{name}", shape, F32))
        HPC = P // HD
        wrap = sb("wrap", [P, HPC, HD + HD // 2])
        sel = sb("sel", [P, HPC, FP], F16)
        rep = sb("rep", [P, HPC, P], F16)
        ones_row = sb("ones_row", [1, GW], F16)
        one_rows = sb("one_rows", [1, P], F16)
        a = [sb(f"a{b}", [P, GW]) for b in range(2)]
        F = [sb(f"F{c}", [P, GW]) for c in range(FCH)]
        zero = sb("zero", [1, P], F16)
        zero_y = sb("zero_y", [1, 4 * 3 * VD], F16)
        Fh = [[sb(f"Fh{b}{c}", [P, GW], F16) for c in range(FCH)] for b in range(2)]
        Fl = [[sb(f"Fl{b}{c}", [P, GW], F16) for c in range(FCH)] for b in range(2)]
        yr = sb("yr", [PT, 4, 1])
        ysum = sb("ysum", [PT, 4, VD])
        pa = ps("pa", [P, GW])
        pb = [ps(f"pb{c}", [P, GW]) for c in range(FCH)]
        py = [ps(f"py{b}", [PT, 4, 3, VD]) for b in range(2)]
        S = {n: sem(f"mq_{n}") for n in ("set", "ready", "a", "a_out", "b", "feat", "f_hi", "f_lo", "f_lo_pool", "y", "recip", "y_out")}
        TURNS = GROUPS * HEADS
        ON_POOL = (0, 1, 3)
        ON_DVE = [c for c in range(FCH) if c not in ON_POOL]

        def rows(c):
            return 2 * HD if c == FCH - 1 else P

        def turns(body, lead):
            def run(e):
                if lead:
                    lead(e, 0, 0)
                with e.Fori(0, TURNS // 2 - 1) as p:
                    for b in range(2):
                        body(e, p * 2 + b, b, True)
                body(e, TURNS - 2, 0, True)
                body(e, TURNS - 1, 1, False)
            return run

        with nc.Block() as block:
            @block.vector
            def _(e):
                step = counted(e, S["set"], 0)
                for hh in range(HPC):
                    step(e.tensor_copy(wrap[:, hh, 0:HD], ident[:, hh * HD:(hh + 1) * HD]))
                    step(e.tensor_copy(wrap[:, hh, HD:HD + HD // 2], ident[:, hh * HD:hh * HD + HD // 2]))
                step(e.memset(sel[:, :, :], 0.0))
                w4 = wrap[:, :, :].ap
                win = bass.AP(wrap[:, :, :].tensor, wrap[:, :, :].offset, [list(w4[0]), [HD + HD // 2, HPC], [1, ND], [1, HD]])
                for hh in range(HPC):
                    step(e.tensor_copy(sel[:, hh, 0:ND * HD].rearrange("p (d m) -> p d m", d=ND), win[:, hh, :, :]))
                    step(e.tensor_copy(rep[:, hh, :].rearrange("p (r m) -> p r m", m=HD), wrap[:, hh, 0:HD].unsqueeze(1).to_broadcast([P, P // HD, HD])))
                step(e.memset(ones_row[:, :], 1.0))
                step(e.memset(one_rows[:, :], 0.0))
                step(e.memset(one_rows[:, HD:2 * HD], 1.0))
                for b in range(2):
                    for f in (Fh, Fl):
                        step(e.memset(f[b][FCH - 1][:, :], 0.0))
                    step(e.memset(Fh[b][FCH - 1][2 * HD:2 * HD + 1, :], 1.0))
                step(e.memset(zero[:, :], 0.0))
                step(e.memset(zero_y[:, :], 0.0))
                e.sem_inc(S["ready"], 1)
                e.sem_inc(S["f_lo"], len(ON_DVE))
                e.sem_inc(S["feat"], FCH + 1)
                e.sem_inc(S["y_out"], 2)

                def low(e, w, b, c):
                    e.wait_ge(S["f_hi"], w * FCH + c + 1 + FCH)
                    e.wait_ge(S["y"], w + 1)
                    e.tensor_tensor(Fl[b][c][0:rows(c), :], F[c][0:rows(c), :], Fh[b][c][0:rows(c), :], ALU.subtract).then_inc(S["f_lo"], 1)

                def features(e, w, b):
                    e.wait_ge(S["a_out"], w + 2)
                    for c in range(FCH):
                        u = w * FCH + c
                        e.wait_ge(S["b"], u + 1)
                        e.wait_ge(S["f_hi"], u + 1)
                        if c in ON_POOL:
                            e.wait_ge(S["f_lo_pool"], w * len(ON_POOL) + ON_POOL.index(c) + 1)
                        else:
                            e.wait_ge(S["f_lo"], w * len(ON_DVE) + ON_DVE.index(c) + 1)
                        e.tensor_tensor(F[c][0:rows(c), :], a[b][0:rows(c), :], pb[c][0:rows(c), :], ALU.mult).then_inc(S["feat"], 1)
                        if c and c - 1 in ON_DVE:
                            low(e, w, b, c - 1)
                    if FCH - 1 in ON_DVE:
                        low(e, w, b, FCH - 1)

                def answer(e, w, b, more):
                    if more:
                        features(e, w + 1, 1 - b)
                    e.wait_ge(S["y"], w + 3)
                    e.wait_ge(S["y_out"], w + 2)
                    e.tensor_reduce(ysum[:, :, :], py[b][:, :, :, :].rearrange("p t i e -> p t e i"), AX.X, ALU.add).then_inc(S["recip"], 1)
                    e.wait_ge(S["recip"], w * 2 + 1)
                    e.reciprocal(yr[:, :, :], ysum[:, :, 0:1]).then_inc(S["recip"], 1)
                    e.wait_ge(S["recip"], w * 2 + 2)
                    g, h = w // HEADS, w % HEADS
                    e.tensor_tensor(yo[:, bass.ds(g * 4, 4), bass.ds(h * HD, HD)], ysum[:, :, 1:VD],
                                    yr[:, :, :].to_broadcast([PT, 4, HD]), ALU.mult).then_inc(S["y_out"], 1)
                turns(answer, features)(e)

            @block.scalar
            def _(e):
                e.sem_inc(S["a_out"], 1)
                e.sem_inc(S["f_hi"], FCH)

                def high(e, w, b):
                    e.wait_ge(S["a"], w + 1)
                    e.wait_ge(S["feat"], w * FCH + 1)
                    e.activation(a[b][:, :], pa[:, :], ACT.Copy).then_inc(S["a_out"], 1)
                    for c in range(FCH):
                        e.wait_ge(S["feat"], w * FCH + c + 1 + FCH + 1)
                        e.wait_ge(S["y"], w + 1)
                        e.activation(Fh[b][c][0:rows(c), :], F[c][0:rows(c), :], ACT.Copy).then_inc(S["f_hi"], 1)

                def body(e, w, b, more):
                    if more:
                        high(e, w + 1, 1 - b)
                turns(body, high)(e)

            @block.gpsimd
            def _(e):
                e.sem_inc(S["f_lo_pool"], len(ON_POOL))

                def low(e, w, b):
                    for c in ON_POOL:
                        e.wait_ge(S["f_hi"], w * FCH + c + 1 + FCH)
                        e.wait_ge(S["y"], w + 1)
                        e.tensor_tensor(Fl[b][c][0:rows(c), :], F[c][0:rows(c), :], Fh[b][c][0:rows(c), :], ALU.subtract).then_inc(S["f_lo_pool"], 1)

                def body(e, w, b, more):
                    if more:
                        low(e, w + 1, 1 - b)
                turns(body, low)(e)

            @block.tensor
            def _(e):
                e.sem_inc(S["y"], 2)
                e.wait_ge(S["ready"], 1)

                def vector(e, w, b):
                    e.wait_ge(S["a_out"], w + 1)
                    factor(e, w, pa, rep, 0, False).then_inc(S["a"], 1)

                def factor(e, w, bank, s, o, last_chunk):
                    g, h = w // HEADS, w % HEADS
                    for i in range(2):
                        mm = e.matmul(bank[:, :], s[:, bass.ds(h % HPC, 1), o:o + P].rearrange("p a c -> p (a c)"),
                                      qT[i][:, bass.ds(h // HPC, 1), bass.ds(g * GW, GW)].rearrange("p a c -> p (a c)"),
                                      start=(i == 0), stop=(i == 1 and not last_chunk))
                    if last_chunk:
                        mm = e.matmul(bank[:, :], one_rows[:, :], ones_row[:, :], start=False, stop=True)
                    return mm

                def rotated(e, w, b, c):
                    e.wait_ge(S["feat"], w * FCH + c + 2)
                    factor(e, w, pb[c], sel, c * P, c == FCH - 1).then_inc(S["b"], 1)

                def multiply(e, w, b, c):
                    if c == 0:
                        e.wait_ge(S["y_out"], w + 1)
                        e.matmul(py[b][:, :, :, :].rearrange("p t i e -> p (t i e)"), zero[:, 0:PT], zero_y[:, :], start=True, stop=False, skip_group_check=True)
                    e.wait_ge(S["f_hi"], w * FCH + c + 1 + FCH)
                    if c in ON_POOL:
                        e.wait_ge(S["f_lo_pool"], (w + 1) * len(ON_POOL) + ON_POOL.index(c) + 1)
                    else:
                        e.wait_ge(S["f_lo"], (w + 1) * len(ON_DVE) + ON_DVE.index(c) + 1)
                    h = w % HEADS
                    for t in range(4):
                        for f, parts in ((Fh, 3), (Fl, 2)):
                            mm = e.matmul(py[b][:, t, 0:parts, :].rearrange("p i e -> p (i e)"), f[b][c][:, t * PT:(t + 1) * PT],
                                          m_parts[:, bass.ds(h * FCH + c, 1), 0:parts, :].rearrange("p a i c -> p (a i c)"),
                                          start=False, stop=False, skip_group_check=True)
                    return mm

                def lead(e, w, b):
                    vector(e, w, b)
                    for c in range(FCH):
                        rotated(e, w, b, c)

                def body(e, w, b, more):
                    if more:
                        vector(e, w + 1, 1 - b)
                    for c in range(FCH):
                        if more:
                            rotated(e, w + 1, 1 - b, c)
                        mm = multiply(e, w, b, c)
                    mm.then_inc(S["y"], 1)
                turns(body, lead)(e)


def mix_project(nc, A, acc, ident, ones, yo):
    with ExitStack() as ctx:
        sem = scoped(nc, ctx)

        def sb(name, shape, dt=F32):
            return ctx.enter_context(nc.sbuf_tensor(f"mp_{name}", shape, dt))

        def ps(name, shape):
            return ctx.enter_context(nc.psum_tensor(f"mp_{name}", shape, F32))
        wp = sb("wp", [P, KC, C])
        bp = sb("bp", [1, C])
        ys = [sb(f"ys{b}", [PT, C]) for b in range(2)]
        yT = [sb(f"yT{b}", [P, KC, PT]) for b in range(2)]
        pt = [ps(f"pt{b}", [P, KC, PT]) for b in range(2)]
        po = [ps(f"po{b}", [PT, C]) for b in range(2)]
        S = {n: sem(f"mp_{n}") for n in ("in", "ys", "turned", "yT", "sum", "added")}
        PAIRS = TILES // 2

        def tiles(body):
            def run(e):
                with e.Fori(0, PAIRS - 1) as p:
                    for b in range(2):
                        body(e, p * 2 + b, b, True)
                body(e, TILES - 2, 0, True)
                body(e, TILES - 1, 1, False)
            return run
        with nc.Block() as block:
            @block.sync
            def _(e):
                e.dma_start(wp[:, :, :], A["WprojT"].rearrange("(k p) n -> p k n", p=P)).then_inc(S["in"], 16)
                e.dma_start(bp[:, :], A["L0_mix_bproj"].rearrange("(a n) -> a n", a=1)).then_inc(S["in"], 16)

            @block.scalar
            def _(e):
                def turn(e, i, b):
                    e.wait_ge(S["turned"], i + 1)
                    e.activation(ys[b][:, :], yo[:, bass.ds(i, 1), :].rearrange("p a c -> p (a c)"), ACT.Copy).then_inc(S["ys"], 1)

                def body(e, i, b, more):
                    if more:
                        turn(e, i + 1, 1 - b)
                    e.wait_ge(S["turned"], i + 3)
                    e.wait_ge(S["sum"], i + 1)
                    e.activation(yT[b][:, :, :], pt[b][:, :, :], ACT.Copy).then_inc(S["yT"], 1)
                turn(e, 0, 0)
                tiles(body)(e)

            @block.tensor
            def _(e):
                e.sem_inc(S["turned"], 2)
                e.sem_inc(S["sum"], 2)
                e.wait_ge(S["in"], 32)

                def turn(e, i, b):
                    e.wait_ge(S["ys"], i + 1)
                    e.wait_ge(S["yT"], i + 1)
                    for k in range(KC):
                        mm = e.transpose(pt[b][:, k, :], ys[b][:, k * P:(k + 1) * P], ident[0:PT, 0:PT])
                    mm.then_inc(S["turned"], 1)

                def body(e, i, b, more):
                    if more:
                        turn(e, i + 1, 1 - b)
                    e.wait_ge(S["yT"], i + 3)
                    e.wait_ge(S["added"], i + 1)
                    for k in range(KC):
                        e.matmul(po[b][:, :], yT[b][:, k, :], wp[:, k, :], start=(k == 0), stop=False)
                    e.matmul(po[b][:, :], ones[0:1, 0:PT], bp[:, :], start=False, stop=True).then_inc(S["sum"], 1)
                turn(e, 0, 0)
                tiles(body)(e)

            @block.vector
            def _(e):
                e.sem_inc(S["yT"], 2)
                e.sem_inc(S["added"], 2)

                def body(e, i, b, more):
                    e.wait_ge(S["sum"], i + 3)
                    r = acc[:, bass.ds(i, 1), :].rearrange("p a c -> p (a c)")
                    e.tensor_tensor(r, r, po[b][:, :], ALU.add).then_inc(S["added"], 1)
                tiles(body)(e)


def gnn_step(nc, A, s, tables, cols, idx, keys, tab, iota_keys, tile_keys, ident, sums, ticks):
    last_step = s == STEPS - 1
    with ExitStack() as ctx:
        sem = scoped(nc, ctx)

        def sb(name, shape, dt=F32):
            return ctx.enter_context(nc.sbuf_tensor(f"g{s}_{name}", shape, dt))

        def ps(name, shape):
            return ctx.enter_context(nc.psum_tensor(f"g{s}_{name}", shape, F32))
        names = ("w_in", "w_mm", "w_cp", "idx_ready", "onehot", "used", "tile_done", "tile_out", "keyed",
                 "set", "h_free", "held", "pr", "pz", "pi", "ph", "r", "z", "t1", "t2", "n", "d", "hnew",
                 "turn", "rows_hi", "rows_lo", "hsum", "row_store", "col_store")
        S = {n: sem(f"g{s}_{n}") for n in names}
        h_in = [sem(f"g{s}_h_in{i}") for i in range(2)]
        landed = [nc.alloc_semaphore(f"g{s}_landed{r}") for r in range(R)]
        wc = sb("wc", [P, TYPES, KC, 3 * C])
        wh = sb("wh", [P, TYPES, KC, 3 * C])
        bi = sb("bi", [P, TYPES, 6])
        bh = sb("bh", [P, TYPES, 6])
        brz = sb("brz", [P, TYPES, 6])
        with ExitStack() as wctx:
            wm = wctx.enter_context(nc.sbuf_tensor(f"g{s}_wm", [P, TYPES, KC, C], F32))
            wi = wctx.enter_context(nc.sbuf_tensor(f"g{s}_wi", [P, TYPES, KC, 3 * C], F32))
            pw = [wctx.enter_context(nc.psum_tensor(f"g{s}_pw{i}", [P, 384], F32)) for i in range(2)]
            with nc.Block() as block:
                @block.sync
                def _(e):
                    for t in range(TYPES):
                        e.dma_start(wm[:, t, :, :], A["convT"][t, s].rearrange("(k p) n -> p k n", p=P)).then_inc(S["w_in"], 16)
                        e.dma_start(wi[:, t, :, :], A["wihT"][t].rearrange("(k p) n -> p k n", p=P)).then_inc(S["w_in"], 16)
                        e.dma_start(wh[:, t, :, :], A["whhT"][t].rearrange("(k p) n -> p k n", p=P)).then_inc(S["w_in"], 16)
                        e.dma_start(bi[:, t, :], A["bihT"][:, t, :]).then_inc(S["w_in"], 16)
                        e.dma_start(bh[:, t, :], A["bhhT"][:, t, :]).then_inc(S["w_in"], 16)

                @block.tensor
                def _(e):
                    e.wait_ge(S["w_in"], 16 * 15)
                    n = 0
                    for t in range(TYPES):
                        for m in range(KC):
                            for q in range(2):
                                if n >= 2:
                                    e.wait_ge(S["w_cp"], n - 1)
                                for k in range(KC):
                                    last = e.matmul(pw[n % 2][:, :], wm[:, t, k, m * P:(m + 1) * P], wi[:, t, k, q * 384:(q + 1) * 384], start=(k == 0), stop=(k == KC - 1))
                                last.then_inc(S["w_mm"], 1)
                                n += 1

                @block.vector
                def _(e):
                    e.wait_ge(S["w_in"], 16 * 15)
                    n = 0
                    for t in range(TYPES):
                        for m in range(KC):
                            for q in range(2):
                                n += 1
                                e.wait_ge(S["w_mm"], n)
                                e.tensor_copy(wc[:, t, m, q * 384:(q + 1) * 384], pw[(n - 1) % 2][:, :]).then_inc(S["w_cp"], 1)
                    e.tensor_tensor(brz[:, :, :], bi[:, :, :], bh[:, :, :], ALU.add)
        ring = sb("ring", [P, R, 2 * C], F16)
        islot = [sb(f"islot{r}", [P, 1], I32) for r in range(R)]
        onehot = sb("onehot", [P, DEEP, NKEY], F16)
        zero = sb("zero", [1, 512], F16)
        ah = [sb(f"ah{i}", [P, TYPES, KC, GW]) for i in range(2)]
        hT = [sb(f"hT{i}", [P, TYPES, KC, GW]) for i in range(2)]
        base = sb("base", [P, KC, GW]) if last_step else None
        hn = sb("hn", [P, TYPES, KC, GW])
        rT = sb("rT", [P, GW])
        zT = sb("zT", [P, GW])
        t1 = sb("t1", [P, GW])
        nT = sb("nT", [P, GW])
        dT = sb("dT", [P, GW])
        rowb = sb("rowb", [PT, 4, C]) if last_step else sb("rowb", [PT, 4, 2 * C], F16)
        pagg = [ps(f"pagg{i}", [P, KC, TYPES, DT]) for i in range(2)]
        pr, pz, pi, ph = (ps(n, [P, GW]) for n in ("pr", "pz", "pi", "ph"))
        ptr = [ps(f"ptr{i}", [PT, 2, C]) for i in range(2)]
        NU = TYPES * KC
        TURNS = [(NU, 0)] if last_step else [(KC * (t + 1), t) for t in range(TYPES)]
        NTN = len(TURNS)
        HL = (TYPES + (1 if last_step else 0)) * 16

        def tile_range(e, g, j):
            a = e.value_load(tab[0:1, bass.ds(g * TG + j, 1)], min_val=0, max_val=32000)
            b = e.value_load(tab[0:1, bass.ds(g * TG + j + 1, 1)], min_val=1, max_val=32000)
            return a, b

        def schedule(stage):
            def run(e):
                stage(e, 0, None, 1)
                with e.Fori(0, GROUPS // 2) as p:
                    stage(e, p * 2 + 1, p * 2, 0)
                    stage(e, p * 2 + 2, p * 2 + 1, 1)
                stage(e, None, GROUPS - 1, 0)
            return run

        def pool_stage(e, ga, gg, par):
            if ga is None:
                return
            for j in range(TG):
                q0, q1 = tile_range(e, ga, j)
                with e.Fori(q0, q1) as q:
                    for r in range(R):
                        e.wait_ge(S["idx_ready"], q * R + R + r + 1)
                        e.wait_ge(S["used"], q * R + r + 1 + DEEP - R)
                        hold_pool(e, ticks, S["held"], q * R + R + r)
                        e.indirect_dma_start(ring[:, r, :], None, tables[s], bass.IndirectOffsetOnAxis(ap=islot[r][:, 0:1], axis=0)).then_inc(landed[r], 16)

        def load_h(e, g, par):
            for t in range(TYPES):
                src = cols[0] if s == 0 else cols[s][t]
                e.dma_start(hT[par][:, t, :, :], src[:, :, bass.ds(g * GW, GW)]).then_inc(h_in[par], 16)
            if last_step:
                e.wait_ge(S["turn"], g * 2 + 1)
                e.dma_start(base[:, :, :], cols[0][:, :, bass.ds(g * GW, GW)]).then_inc(h_in[par], 16)

        def sync_stage(e, ga, gg, par):
            if gg is None:
                load_h(e, 0, 0)
                return
            if ga is not None:
                e.wait_ge(S["h_free"], gg * NU + 1)
                load_h(e, gg + 1, 1 - par)
            if not last_step:
                for t in range(TYPES):
                    e.wait_ge(S["hnew"], gg * NU + KC * (t + 1) + 1)
                    e.dma_start(cols[s + 1][t][:, :, bass.ds(gg * GW, GW)], hn[:, t, :, :]).then_inc(S["col_store"], 16)
                    e.wait_ge(S["rows_lo"], 2 * (gg * TYPES + t + 1) + 1)
                    e.dma_start(tables[s + 1][bass.ds(gg * GW + t * NP, GW), :].rearrange("(a p) c -> p a c", p=PT), rowb[:, :, :]).then_inc(S["row_store"], 16)
            else:
                e.wait_ge(S["rows_hi"], 2 * (gg + 1) + 1)
                e.dma_start(sums[bass.ds(gg * GW, GW), :].rearrange("(a p) c -> p a c", p=PT), rowb[:, :, :]).then_inc(S["row_store"], 16)

        def pe_stage(e, ga, gg, par):
            for j in range(TG):
                if gg is not None and j == 0:
                    e.wait_ge(S["tile_out"], (gg + 1) * TG + 2)
                    e.wait_ge(h_in[par], loads_done(gg, par))
                products = pe_unit(gg, par, j) if gg is not None and j < NU else []
                if ga is not None:
                    pe_tile(e, ga, j, products)
                else:
                    for product in products:
                        product(e)
                for i, (u, t) in enumerate(TURNS):
                    if gg is not None and j == u:
                        pe_turn(e, gg, i, t)

        def loads_done(g, par):
            return ((g - par) // 2 + 1) * HL if isinstance(g, int) else (g - par) * (HL // 2) + HL

        def pe_tile(e, g, j, products):
            q0, q1 = tile_range(e, g, j)
            pg = pagg[j % 2]
            flat = pg[:, :, :, :].rearrange("p k t d -> p (k t d)")
            e.wait_ge(S["tile_out"], g * TG + (j + 1 if j else 2))
            e.matmul(flat, zero[0:1, 0:P], zero[0:1, 0:KC * NKEY], start=True, stop=False, skip_group_check=True)

            def chunk(q, r):
                slot = (q * R + r) % DEEP
                e.wait_ge(landed[r], q * 16 + 32)
                e.wait_ge(S["onehot"], q * R + r + 2)
                for part in range(2):
                    for k in range(KC):
                        o = part * C + k * P
                        mm = e.matmul(pg[:, k, :, :].rearrange("p t d -> p (t d)"), ring[:, r, o:o + P],
                                      onehot[:, bass.ds(slot, 1), :].rearrange("p a c -> p (a c)"),
                                      start=False, stop=False, skip_group_check=True)
                mm.then_inc(S["used"], 1)
            for r in range(R):
                chunk(q0, r)
                for product in products[r * len(products) // R:(r + 1) * len(products) // R]:
                    product(e)
            with e.If(q1 - q0 - 1 > 0):
                with e.Fori(q0 + 1, q1) as q:
                    for r in range(R):
                        chunk(q, r)
            e.matmul(flat, zero[0:1, 0:P], zero[0:1, 0:KC * NKEY], start=False, stop=True, skip_group_check=True).then_inc(S["tile_done"], 1)

        def pe_unit(g, par, u):
            t, m = u // KC, u % KC
            x_a, x_h = ah[par], hT[par]

            def product(p, gate, x, w, k, first, last, done, free):
                def issue(e):
                    if first:
                        e.wait_ge(S[free], g * NU + u + 1)
                    mm = e.matmul(p[:, :], w[:, t, k, gate * C + m * P:gate * C + m * P + P], x[:, t, k, :], start=first, stop=last)
                    if last:
                        mm.then_inc(S[done], 1)
                return issue
            products = []
            for p, gate, parts, done, free in ((pr, 0, [(wh, x_h), (wc, x_a)], "pr", "r"), (ph, 2, [(wh, x_h)], "ph", "t1"),
                                               (pi, 2, [(wc, x_a)], "pi", "t2"), (pz, 1, [(wh, x_h), (wc, x_a)], "pz", "z")):
                steps = [(w, x, k) for w, x in parts for k in range(KC)]
                for n, (w, x, k) in enumerate(steps):
                    products.append(product(p, gate, x, w, k, n == 0, n == len(steps) - 1, done, free))
            return products

        def pe_turn(e, g, i, t):
            src = base if last_step else hn[:, t, :, :]
            if last_step:
                e.wait_ge(S["hsum"], (g + 1) * NU)
            else:
                e.wait_ge(S["hnew"], g * NU + KC * (t + 1) + 1)
            for b in range(2):
                e.wait_ge(S["rows_hi"], 2 * (g * NTN + i) + 1)
                if not last_step:
                    e.wait_ge(S["rows_lo"], 2 * (g * NTN + i) + 1)
                for c in range(2):
                    for k in range(KC):
                        mm = e.transpose(ptr[b][:, c, k * P:(k + 1) * P], src[:, k, (2 * b + c) * PT:(2 * b + c + 1) * PT], ident[:, :])
                mm.then_inc(S["turn"], 1)

        def act_stage(e, ga, gg, par):
            for j in range(TG):
                if ga is not None:
                    if j == 0 and gg is not None:
                        e.wait_ge(S["pz"], gg * NU + 1)
                    e.wait_ge(S["tile_done"], ga * TG + j + 1)
                    e.activation(ah[1 - par][:, :, :, j * DT:(j + 1) * DT], pagg[j % 2][:, :, :, :].rearrange("p k t d -> p t k d"), ACT.Copy).then_inc(S["tile_out"], 1)
                if gg is not None:
                    if j < NU:
                        act_unit(e, gg, j)
                    for i, (u, t) in enumerate(TURNS):
                        if j == u:
                            n = gg * NTN + i
                            e.wait_ge(S["row_store"], 16 * n + 1)
                            for b in range(2):
                                e.wait_ge(S["turn"], 2 * n + b + 2)
                                e.activation(rowb[:, 2 * b:2 * b + 2, 0:C], ptr[b][:, :, :], ACT.Copy).then_inc(S["rows_hi"], 1)

        def act_unit(e, g, u):
            t, m = u // KC, u % KC
            U = g * NU + u
            e.wait_ge(S["pr"], U + 1)
            e.wait_ge(S["t1"], U + 1)
            e.activation(rT[:, :], pr[:, :], ACT.Sigmoid, bias=brz[:, t, m:m + 1]).then_inc(S["r"], 1)
            e.wait_ge(S["t2"], U + 2)
            e.wait_ge(S["hnew"], U + 1)
            e.activation(nT[:, :], t1[:, :], ACT.Tanh, bias=bi[:, t, 4 + m:5 + m]).then_inc(S["n"], 1)
            e.wait_ge(S["pz"], U + 2)
            e.activation(zT[:, :], pz[:, :], ACT.Sigmoid, bias=brz[:, t, 2 + m:3 + m]).then_inc(S["z"], 1)

        def dve_chunk(e, q, r, q0, first):
            c = nc.s_assert_within((q - q0) * R + first + r, 0, NCH - 1, skip_runtime_bounds_check_because="a tile has at most all the chunks, and R - 1 more")
            n = q * R + r
            e.wait_ge(landed[r], q * 16 + 16)
            e.tensor_copy(islot[r][:, :], idx[:, bass.ds(c, 1)]).then_inc(S["idx_ready"], 1)
            e.wait_ge(S["used"], n + 1)
            e.tensor_scalar(onehot[:, bass.ds(n % DEEP, 1), :].rearrange("p a c -> p (a c)"), tile_keys[:, :, :].rearrange("p t d -> p (t d)"), keys[:, bass.ds(c, 1)], None, ALU.is_equal).then_inc(S["onehot"], 1)

        def dve_gates(e, gg, par, j):
            if gg is None or j < 0:
                return
            if j < NU:
                dve_unit(e, gg, par, j)
            for i, (u, t) in enumerate(TURNS):
                if j == u and not last_step:
                    n = gg * NTN + i
                    for b in range(2):
                        e.wait_ge(S["rows_hi"], 2 * n + b + 2)
                        e.tensor_tensor(rowb[:, 2 * b:2 * b + 2, C:2 * C], ptr[b][:, :, :], rowb[:, 2 * b:2 * b + 2, 0:C], ALU.subtract).then_inc(S["rows_lo"], 1)

        def dve_stage(e, ga, gg, par):
            for j in range(TG):
                if ga is not None:
                    q0, q1 = tile_range(e, ga, j)
                    first = e.value_load(tab[0:1, bass.ds(ga * TG + j + 80, 1)], min_val=0, max_val=400)
                    e.wait_ge(S["keyed"], ga * TG + j + 1)
                    e.wait_ge(S["onehot"], q0 * R + 1)
                    e.tensor_scalar(tile_keys[:, :, :], tile_keys[:, :, :], float(DT), None, ALU.add).then_inc(S["keyed"], 1)
                    e.wait_ge(S["keyed"], ga * TG + j + 2)
                    hold(e, ticks)
                    for r in range(R):
                        dve_chunk(e, q0, r, q0, first)
                dve_gates(e, gg, par, j - 1)
                if ga is not None:
                    with e.If(q1 - q0 - 1 > 0):
                        with e.Fori(q0 + 1, q1) as q:
                            for r in range(R):
                                dve_chunk(e, q, r, q0, first)
            dve_gates(e, gg, par, TG - 1)

        def dve_unit(e, g, par, u):
            t, m = u // KC, u % KC
            U = g * NU + u
            e.wait_ge(S["ph"], U + 1)
            e.wait_ge(S["r"], U + 2)
            e.wait_ge(S["n"], U + 1)
            e.scalar_tensor_tensor(out=t1[:, :], in0=ph[:, :], scalar=bh[:, t, 4 + m:5 + m], in1=rT[:, :], op0=ALU.add, op1=ALU.mult).then_inc(S["t1"], 1)
            e.wait_ge(S["t1"], U + 2)
            e.wait_ge(S["pi"], U + 1)
            e.tensor_tensor(t1[:, :], t1[:, :], pi[:, :], ALU.add).then_inc(S["t2"], 1)
            e.wait_ge(S["n"], U + 2)
            e.wait_ge(h_in[par], loads_done(g, par))
            e.tensor_tensor(dT[:, :], hT[par][:, t, m, :], nT[:, :], ALU.subtract).then_inc(S["d"], 1)
            e.wait_ge(S["d"], 2 * U + 1)
            e.wait_ge(S["z"], U + 2)
            e.tensor_tensor(dT[:, :], dT[:, :], zT[:, :], ALU.mult).then_inc(S["d"], 1)
            e.wait_ge(S["d"], 2 * U + 2)
            if not last_step and m == 0:
                e.wait_ge(S["col_store"], g * 16 * TYPES + 1)
                e.wait_ge(S["turn"], g * 2 * TYPES + 1)
            e.tensor_tensor(hn[:, t, m, :], dT[:, :], nT[:, :], ALU.add).then_inc(S["hnew"], 1)
            if last_step:
                e.wait_ge(S["hnew"], U + 2)
                if u == 0:
                    e.wait_ge(S["turn"], 2 * g + 1)
                e.tensor_tensor(base[:, m, :], base[:, m, :], hn[:, t, m, :], ALU.add).then_inc(S["hsum"], 1)
                e.wait_ge(S["hsum"], U + 1)
            if u == NU - 1:
                e.wait_ge(S["pz"], U + 2)
            e.sem_inc(S["h_free"], 1)

        with nc.Block() as block:
            @block.gpsimd
            def _(e):
                e.sem_inc(S["held"], 1)
                for r in range(R):
                    e.wait_ge(S["idx_ready"], r + 1)
                    hold_pool(e, ticks, S["held"], r)
                    e.indirect_dma_start(ring[:, r, :], None, tables[s], bass.IndirectOffsetOnAxis(ap=islot[r][:, 0:1], axis=0)).then_inc(landed[r], 16)
                schedule(pool_stage)(e)

            @block.sync
            def _(e):
                schedule(sync_stage)(e)
                e.wait_ge(S["row_store"], 16 * NTN * GROUPS + 1)
                if not last_step:
                    e.wait_ge(S["col_store"], 16 * TYPES * GROUPS + 1)

            @block.tensor
            def _(e):
                e.sem_inc(S["used"], DEEP)
                for name in ("h_free", "turn", "pz", "row_store", "t1", "hnew", "rows_hi", "rows_lo", "n", "col_store", "r", "t2", "z"):
                    e.sem_inc(S[name], 1)
                e.sem_inc(S["tile_out"], 2)
                e.wait_ge(S["set"], 1)
                schedule(pe_stage)(e)

            @block.scalar
            def _(e):
                schedule(act_stage)(e)

            @block.vector
            def _(e):
                e.sem_inc(S["onehot"], 1)
                e.memset(zero[:, :], 0.0).then_inc(S["set"], 1)
                for r in range(R):
                    e.tensor_copy(islot[r][:, :], idx[:, r:r + 1]).then_inc(S["idx_ready"], 1)
                e.tensor_scalar(tile_keys[:, :, :], iota_keys[:, :, :], -float(DT), None, ALU.add).then_inc(S["keyed"], 1)
                schedule(dve_stage)(e)


def gnn_out(nc, A, acc, sums):
    with ExitStack() as ctx:
        sem = scoped(nc, ctx)
        def sb(name, shape, dt=F32):
            return ctx.enter_context(nc.sbuf_tensor(f"go_{name}", shape, dt))
        gm = sb("sums", [PT, TILES, C])
        gam = sb("gamma", [PT, C])
        bet = sb("beta", [PT, C])
        stats = sb("stats", [PT, TILES, 6])
        mv = sb("mv", [PT, TILES, 2])
        std = sb("std", [PT, TILES])
        rstd = sb("rstd", [PT, TILES])
        o_in, o_gm, o_d, o_v, o_s, o_n, o_b = (sem(f"go_{n}") for n in ("loaded", "sums", "dve", "var", "std", "normalised", "stats"))

        def row(t, i):
            return t[:, bass.ds(i, 1), :].rearrange("p a c -> p (a c)")
        with nc.Block() as block:
            @block.sync
            def _(e):
                e.dma_start(gm[:, :, :], sums.rearrange("(i p) c -> p i c", p=PT)).then_inc(o_gm, 16)
                e.dma_start(gam[:, :], A["L0_gnn_ln_gamma"].rearrange("(a c) -> a c", a=1).to_broadcast([PT, C])).then_inc(o_in, 16)
                e.dma_start(bet[:, :], A["L0_gnn_ln_beta"].rearrange("(a c) -> a c", a=1).to_broadcast([PT, C])).then_inc(o_in, 16)

            @block.scalar
            def _(e):
                e.wait_ge(o_v, 1)
                e.activation(std[:, :], rstd[:, :], ACT.Sqrt).then_inc(o_s, 1)

            @block.vector
            def _(e):
                e.wait_ge(o_gm, 16)
                with e.Fori(0, TILES) as i:
                    e.bn_stats(row(stats, i), row(gm, i)).then_inc(o_b, 1)
                e.wait_ge(o_b, TILES)
                for i in range(TILES):
                    e.bn_aggr(mv[:, i, :], stats[:, i, :]).then_inc(o_b, 1)
                e.wait_ge(o_b, 2 * TILES)
                step = counted(e, o_d, 0)
                step(e.tensor_scalar(rstd[:, :], mv[:, :, 1], 1e-5, None, ALU.add))
                e.sem_inc(o_v, 1)
                e.wait_ge(o_s, 1)
                step(e.reciprocal(rstd[:, :], std[:, :]))
                e.wait_ge(o_in, 32)
                with e.Fori(0, TILES) as i:
                    e.tensor_scalar(row(gm, i), row(gm, i), mv[:, bass.ds(i, 1), 0], rstd[:, bass.ds(i, 1)], ALU.subtract, ALU.mult).then_inc(o_n, 1)
                e.wait_ge(o_n, TILES)
                step = counted(e, o_d, 2)
                step(e.tensor_tensor(gm[:, :, :], gm[:, :, :], gam[:, :].unsqueeze(1).to_broadcast([PT, TILES, C]), ALU.mult))
                step(e.tensor_tensor(gm[:, :, :], gm[:, :, :], bet[:, :].unsqueeze(1).to_broadcast([PT, TILES, C]), ALU.add))
                step(e.scalar_tensor_tensor(out=gm[:, :, :], in0=gm[:, :, :], scalar=0.1, in1=gm[:, :, :], op0=ALU.mult, op1=ALU.max))
                step(e.tensor_tensor(acc[:, :, :], acc[:, :, :], gm[:, :, :], ALU.add))


def ffn(nc, A, acc, ident, ones, slots_in, slots_out, out):
    with ExitStack() as ctx:
        choice = ctx.enter_context(nc.sbuf_tensor("choice", [PT, TILES, 4], F32))
        pos = ctx.enter_context(nc.sbuf_tensor("slot_of", [PT, 2, TILES], I32))
        first_tile = ctx.enter_context(nc.sbuf_tensor("first_tile", [1, XPT + 1], I32))
        with ExitStack() as rctx:
            rows = rctx.enter_context(nc.sbuf_tensor("xf_rows", [PT, TILES, C], F32))
            with nc.sbuf_tensor("xfT", [P, KC, NP], F32) as xfT:
                normalise(nc, "ffn", acc, xfT, ident, keep=rows)
                ffn_gate(nc, A, xfT, ones, choice, slots_in, slots_out)
            ffn_route(nc, ones, choice, pos, first_tile, rows, slots_in)
        with nc.sbuf_tensor("slots_T", [P, KC, SLOTS], F32) as slotsT:
            ffn_turn(nc, ident, slots_in, slotsT)
            ffn_experts(nc, A, slotsT, first_tile, slots_out)
        ffn_combine(nc, acc, choice, pos, slots_out, out)


def ffn_gate(nc, A, xnT, ones, choice, slots_in, slots_out):
    with ExitStack() as ctx:
        sem = scoped(nc, ctx)

        def sb(name, shape, dt=F32):
            return ctx.enter_context(nc.sbuf_tensor(f"fg_{name}", shape, dt))
        wg, bg = sb("wg", [P, KC, XPT]), sb("bg", [1, XPT])
        none = sb("none", [P, C])
        xs = [sb(f"xs{b}", [P, KC, PT]) for b in range(2)]
        io_i, io = sb("io_i", [PT, XPT], I32), sb("io", [PT, XPT])
        lg = sb("lg", [PT, TILES, XPT])
        at_top = sb("at_top", [PT, TILES, XPT])
        top = sb("top", [PT, 2, TILES])
        ew = sb("ew", [PT, TILES])
        pl = ctx.enter_context(nc.psum_tensor("fg_pl", [PT, TILES, XPT], F32))
        f_in, f_io, f_set, f_xs, f_l, f_d, f_df, f_e, f_z = (sem(f"gate_{n}") for n in (
            "loaded", "iota", "set", "x", "logits", "dve", "diff", "exp", "zeroed"))
        with nc.Block() as block:
            @block.sync
            def _(e):
                e.dma_start(wg[:, :, :], A["L0_ffn_Wg"].rearrange("(k p) n -> p k n", p=P)).then_inc(f_in, 16)
                e.dma_start(bg[:, :], A["L0_ffn_bg"].rearrange("(a n) -> a n", a=1)).then_inc(f_in, 16)
                e.wait_ge(f_set, 1)
                with e.Fori(0, SLOTS // P) as k:
                    e.dma_start(slots_in[bass.ds(k * P, P), :], none[:, :]).then_inc(f_z, 16)
                used = 2 * NP // ST * ST // P
                with e.Fori(used, SLOTS // P) as k:
                    e.dma_start(slots_out[bass.ds(k * P, P), :], none[:, :]).then_inc(f_z, 16)
                e.wait_ge(f_z, 16 * (2 * (SLOTS // P) - used))

            @block.gpsimd
            def _(e):
                e.iota(io_i[:, :], [[1, XPT]], base=0, channel_multiplier=0).then_inc(f_io, 1)

            @block.scalar
            def _(e):
                with e.Fori(0, TILES // 2) as pair:
                    for b in range(2):
                        i = pair * 2 + b
                        e.wait_ge(f_l, i + 1)
                        e.activation(xs[b][:, :, :], xnT[:, :, bass.ds(i * PT, PT)], ACT.Copy).then_inc(f_xs, 1)
                e.wait_ge(f_df, 1)
                e.activation(ew[:, :], top[:, 1, :], ACT.Exp).then_inc(f_e, 1)

            @block.tensor
            def _(e):
                e.sem_inc(f_l, 2)
                e.wait_ge(f_in, 32)
                with e.Fori(0, TILES // 2) as pair:
                    for b in range(2):
                        i = pair * 2 + b
                        out = pl[:, bass.ds(i, 1), :].rearrange("p a x -> p (a x)")
                        e.wait_ge(f_xs, i + 1)
                        for k in range(KC):
                            e.matmul(out, xs[b][:, k, :], wg[:, k, :], start=(k == 0), stop=False)
                        e.matmul(out, ones[0:1, 0:PT], bg[:, :], start=False, stop=True).then_inc(f_l, 1)

            @block.vector
            def _(e):
                step = counted(e, f_d, 0)
                e.memset(none[:, :], 0.0).then_inc(f_set, 1)
                e.wait_ge(f_io, 1)
                step(e.tensor_copy(io[:, :], io_i[:, :]))
                iob = io[:, :].unsqueeze(1).to_broadcast([PT, TILES, XPT])
                e.wait_ge(f_l, TILES + 2)
                step(e.tensor_copy(lg[:, :, :], pl[:, :, :]))
                for k in range(2):
                    step(e.tensor_reduce(top[:, k, :], lg[:, :, :], AX.X, ALU.max))
                    step(e.tensor_tensor(at_top[:, :, :], lg[:, :, :], top[:, k, :].unsqueeze(2).to_broadcast([PT, TILES, XPT]), ALU.is_equal))
                    step(e.scalar_tensor_tensor(out=at_top[:, :, :], in0=iob, scalar=-float(XPT), in1=at_top[:, :, :], op0=ALU.add, op1=ALU.mult))
                    step(e.tensor_reduce(ew[:, :], at_top[:, :, :], AX.X, ALU.min))
                    step(e.tensor_scalar(choice[:, :, k], ew[:, :], float(XPT), None, ALU.add))
                    if k == 0:
                        step(e.tensor_tensor(at_top[:, :, :], iob, choice[:, :, 0:1].to_broadcast([PT, TILES, XPT]), ALU.is_equal))
                        step(e.scalar_tensor_tensor(out=lg[:, :, :], in0=at_top[:, :, :], scalar=-3.0e38, in1=lg[:, :, :], op0=ALU.mult, op1=ALU.add))
                e.tensor_tensor(top[:, 1, :], top[:, 1, :], top[:, 0, :], ALU.subtract).then_inc(f_df, 1)
                e.wait_ge(f_e, 1)
                step(e.tensor_scalar(top[:, 0, :], ew[:, :], 1.0, None, ALU.add))
                step(e.reciprocal(choice[:, :, 2], top[:, 0, :]))
                step(e.tensor_tensor(choice[:, :, 3], ew[:, :], choice[:, :, 2], ALU.mult))


def ffn_route(nc, ones, choice, pos, first_tile, rows, slots_in):
    with ExitStack() as ctx:
        sem = scoped(nc, ctx)

        def sb(name, shape, dt=F32):
            return ctx.enter_context(nc.sbuf_tensor(f"fr_{name}", shape, dt))
        io_i, io = sb("io_i", [PT, XPT], I32), sb("io", [PT, XPT])
        before = sb("before", [PT, PT])
        column = sb("column", [PT, 1])
        taken = sb("taken", [PT, TILES, XPT])
        mine = [sb(f"mine{k}", [PT, TILES, XPT]) for k in range(2)]
        total = sb("total", [1, TILES, XPT])
        run = sb("run", [1, TILES + 1, XPT])
        count_i, count = sb("count_i", [1, XPT], I32), sb("count", [1, XPT])
        start = sb("start", [1, XPT + 1])
        base = sb("base", [1, XPT])
        offset = sb("offset", [1, TILES, XPT])
        posf = sb("posf", [PT, 2, TILES])
        pr = ctx.enter_context(nc.psum_tensor("fr_ranks_sum", [PT, TILES * XPT], F32))
        pc = ctx.enter_context(nc.psum_tensor("fr_counts_sum", [1, TILES * XPT], F32))
        r_io, r_d, r_taken, r_count, r_off, r_rank, r_pos = (sem(f"route_{n}") for n in (
            "iota", "dve", "taken", "counts", "offsets", "ranks", "slots"))
        scattered = nc.alloc_semaphore("scattered")
        with nc.Block() as block:
            @block.gpsimd
            def _(e):
                e.iota(io_i[:, :], [[1, XPT]], base=0, channel_multiplier=0).then_inc(r_io, 1)
                e.memset(column[:, :], 1.0).then_inc(r_io, 1)
                e.memset(before[:, :], 1.0).then_inc(r_io, 1)
                e.wait_ge(r_io, 3)
                e.affine_select(out=before[:, :], in_=before[:, :], compare_op=ALU.is_gt, fill=0.0,
                                base=0, pattern=[[1, PT]], channel_multiplier=-1).then_inc(r_io, 1)
                e.wait_ge(r_pos, 1)
                for i in range(TILES):
                    for k in range(2):
                        e.indirect_dma_start(slots_in, bass.IndirectOffsetOnAxis(ap=pos[:, k, i:i + 1], axis=0), rows[:, i, :], None).then_inc(scattered, 16)
                e.wait_ge(scattered, 16 * 2 * TILES)

            @block.vector
            def _(e):
                step = counted(e, r_d, 0)
                e.wait_ge(r_io, 4)
                step(e.tensor_copy(io[:, :], io_i[:, :]))
                for k in range(2):
                    step(e.tensor_tensor(mine[k][:, :, :], io[:, :].unsqueeze(1).to_broadcast([PT, TILES, XPT]),
                                         choice[:, :, k:k + 1].to_broadcast([PT, TILES, XPT]), ALU.is_equal))
                e.tensor_tensor(taken[:, :, :], mine[0][:, :, :], mine[1][:, :, :], ALU.add).then_inc(r_taken, 1)
                e.wait_ge(r_count, 1)
                step(e.tensor_copy(total[:, :, :], pc[:, :].rearrange("p (t x) -> p t x", x=XPT)))
                step(e.memset(run[:, 0, :], 0.0))
                for i in range(TILES):
                    step(e.tensor_tensor(run[:, i + 1, :], run[:, i, :], total[:, i, :], ALU.add))
                step(e.tensor_scalar(count[:, :], run[:, TILES, :], 1.0, float(ST - 1), ALU.max, ALU.add))
                step(e.tensor_copy(count_i[:, :], count[:, :]))
                step(e.tensor_scalar(count_i[:, :], count_i[:, :], ST.bit_length() - 1, None, ALU.logical_shift_right))
                step(e.tensor_copy(count[:, :], count_i[:, :]))
                step(e.memset(start[:, 0:1], 0.0))
                for x in range(XPT):
                    step(e.tensor_tensor(start[:, x + 1:x + 2], start[:, x:x + 1], count[:, x:x + 1], ALU.add))
                step(e.tensor_copy(first_tile[:, :], start[:, :]))
                step(e.tensor_scalar(base[:, :], start[:, 0:XPT], float(ST), None, ALU.mult))
                e.tensor_tensor(offset[:, :, :], run[:, 0:TILES, :], base[:, :].unsqueeze(1).to_broadcast([1, TILES, XPT]), ALU.add).then_inc(r_off, 1)
                e.wait_ge(r_rank, 1)
                for k in range(2):
                    step(e.tensor_tensor(mine[k][:, :, :], mine[k][:, :, :], pr[:, :].rearrange("p (t x) -> p t x", x=XPT), ALU.mult))
                    step(e.tensor_reduce(posf[:, k, :], mine[k][:, :, :], AX.X, ALU.add))
                e.tensor_copy(pos[:, :, :], posf[:, :, :]).then_inc(r_pos, 1)

            @block.tensor
            def _(e):
                e.wait_ge(r_taken, 1)
                flat = taken[:, :, :].rearrange("p t x -> p (t x)")
                e.matmul(pc[:, :], column[:, :], flat, start=True, stop=True).then_inc(r_count, 1)
                e.matmul(pr[:, :], before[:, :], flat, start=True, stop=False)
                e.wait_ge(r_off, 1)
                e.matmul(pr[:, :], ones[0:1, 0:PT], offset[:, :, :].rearrange("p t x -> p (t x)"), start=False, stop=True).then_inc(r_rank, 1)


def ffn_turn(nc, ident, slots_in, slotsT):
    with ExitStack() as ctx:
        sem = scoped(nc, ctx)
        PART = 8
        LOADS = SLOTS // P // PART
        xr = [ctx.enter_context(nc.sbuf_tensor(f"ft_x{b}", [P, PART, C], F32)) for b in range(2)]
        pt = [ctx.enter_context(nc.psum_tensor(f"ft_p{b}", [P, KC, 2 * P], F32)) for b in range(2)]
        loaded = [sem(f"ft_loaded{b}") for b in range(2)]
        turned, copied = sem("ft_turned"), sem("ft_copied")
        H = PART // 2
        with nc.Block() as block:
            @block.sync
            def _(e):
                with e.Fori(0, LOADS // 2) as pair:
                    for b in range(2):
                        n = pair * 2 + b
                        e.wait_ge(turned, n * H + H)
                        e.dma_start(xr[b][:, :, :], slots_in[bass.ds(n * PART * P, PART * P), :].rearrange("(a p) c -> p a c", p=P)).then_inc(loaded[b], 16)

            @block.tensor
            def _(e):
                e.sem_inc(turned, 2 * H)
                e.sem_inc(copied, 2)
                with e.Fori(0, LOADS // 2) as pair:
                    for b in range(2):
                        n = pair * 2 + b
                        e.wait_ge(loaded[b], pair * 16 + 16)
                        for q in range(H):
                            e.wait_ge(copied, n * H + q + 1)
                            for k in range(KC):
                                for a in range(2):
                                    mm = e.transpose(pt[q % 2][:, k, a * P:(a + 1) * P], xr[b][:, 2 * q + a, k * P:(k + 1) * P], ident[:, :])
                            mm.then_inc(turned, 1)

            @block.scalar
            def _(e):
                with e.Fori(0, LOADS) as n:
                    for q in range(H):
                        e.wait_ge(turned, n * H + q + 1 + 2 * H)
                        e.activation(slotsT[:, :, bass.ds(n * (PART * P) + q * 2 * P, 2 * P)], pt[q % 2][:, :, :], ACT.Copy).then_inc(copied, 1)


def ffn_experts(nc, A, slotsT, first_tile, slots_out):
    with ExitStack() as ctx:
        sem = scoped(nc, ctx)

        def sb(name, shape, dt=F32):
            return ctx.enter_context(nc.sbuf_tensor(f"f_{name}", shape, dt))
        b1 = sb("b1", [P, XPT, HC])
        b2 = sb("b2", [P, XPT, C])
        w1 = sb("w1", [P, 2, KC, HID])
        w2 = sb("w2", [P, 2, HC, C])
        hid = sb("hid", [P, HC, ST])
        ys = sb("ys", [P, 2, C])
        p1 = [ctx.enter_context(nc.psum_tensor(f"f_p1{i}", [P, ST], F32)) for i in range(4)]
        p2 = [ctx.enter_context(nc.psum_tensor(f"f_p2{i}", [P, C], F32)) for i in range(2)]
        x_in = [sem(f"ffn_weights{i}") for i in range(2)]
        x_st = [sem(f"ffn_stored{i}") for i in range(2)]
        x_b, x_p1, x_h, x_p2, x_y, x_done = (sem(f"ffn_{n}") for n in ("bias", "hidden_sum", "hidden", "expert_sum", "rows", "expert_done"))
        NFT = SLOTS // ST

        def tiles(e, x):
            t0 = e.value_load(first_tile[0:1, x:x + 1], min_val=0, max_val=NFT - 1)
            t1 = e.value_load(first_tile[0:1, x + 1:x + 2], min_val=1, max_val=NFT)
            return e.Fori(t0, t1)
        with nc.Block() as block:
            @block.sync
            def _(e):
                def load(x):
                    e.dma_start(w1[:, x % 2, :, :], A["L0_ffn_W1"][x].rearrange("(k p) n -> p k n", p=P)).then_inc(x_in[x % 2], 16)
                    e.dma_start(w2[:, x % 2, :, :], A["L0_ffn_W2"][x].rearrange("(k p) n -> p k n", p=P)).then_inc(x_in[x % 2], 16)
                e.dma_start(b1[:, :, :], A["b1T"]).then_inc(x_b, 16)
                e.dma_start(b2[:, :, :], A["L0_ffn_b2"].rearrange("(a x) c -> a x c", a=1).to_broadcast([P, XPT, C])).then_inc(x_b, 16)
                load(0)
                for x in range(XPT):
                    if x >= 1:
                        e.wait_ge(x_done, x)
                    if x + 1 < XPT:
                        load(x + 1)
                    with tiles(e, x) as t:
                        for c in range(2):
                            e.wait_ge(x_y, t * 2 + c + 1 + 2)
                            e.dma_start(slots_out[bass.ds(t * ST + c * P, P), :], ys[:, c, :]).then_inc(x_st[c], 16)

            @block.tensor
            def _(e):
                e.sem_inc(x_h, 4)
                e.sem_inc(x_y, 2)
                e.sem_inc(x_p2, 2)
                for x in range(XPT):
                    e.wait_ge(x_in[x % 2], 32 * (x // 2 + 1))
                    with tiles(e, x) as t:
                        for m in range(HC):
                            e.wait_ge(x_h, t * HC + m + 1)
                            for k in range(KC):
                                mm = e.matmul(p1[m % 4][:, :], w1[:, x % 2, k, m * P:(m + 1) * P], slotsT[:, k, bass.ds(t * ST, ST)], start=(k == 0), stop=(k == KC - 1))
                            mm.then_inc(x_p1, 1)
                        e.wait_ge(x_h, (t + 1) * HC + 4)
                        for c in range(2):
                            e.wait_ge(x_y, t * 2 + c + 1)
                            for m in range(HC):
                                mm = e.matmul(p2[c][:, :], hid[:, m, c * P:(c + 1) * P], w2[:, x % 2, m, :], start=(m == 0), stop=(m == HC - 1))
                            mm.then_inc(x_p2, 1)
                    e.sem_inc(x_done, 1)

            @block.scalar
            def _(e):
                e.wait_ge(x_b, 32)
                for x in range(XPT):
                    with tiles(e, x) as t:
                        for m in range(HC):
                            e.wait_ge(x_p1, t * HC + m + 1)
                            if m == 0:
                                e.wait_ge(x_p2, t * 2 + 2)
                            e.activation(hid[:, m, :], p1[m % 4][:, :], ACT.Gelu, bias=b1[:, x, m:m + 1]).then_inc(x_h, 1)

            @block.vector
            def _(e):
                e.wait_ge(x_b, 32)
                for c in range(2):
                    e.sem_inc(x_st[c], 16)
                for x in range(XPT):
                    with tiles(e, x) as t:
                        for c in range(2):
                            e.wait_ge(x_p2, t * 2 + c + 1 + 2)
                            e.wait_ge(x_st[c], t * 16 + 16)
                            e.tensor_tensor(ys[:, c, :], p2[c][:, :], b2[:, x, :], ALU.add).then_inc(x_y, 1)
                end = e.value_load(first_tile[0:1, XPT:XPT + 1], min_val=1, max_val=NFT)
                for c in range(2):
                    e.wait_ge(x_st[c], end * 16 + 16)
                    e.memset(ys[0:1, c, 0:1], 0.0)


def ffn_combine(nc, acc, choice, pos, slots_out, out):
    with ExitStack() as ctx:
        sem = scoped(nc, ctx)
        RING = 8
        y = [ctx.enter_context(nc.sbuf_tensor(f"fc_y{r}", [PT, C], F32)) for r in range(RING)]
        used, c_o = sem("fc_used"), sem("fc_stored")
        landed = [nc.alloc_semaphore(f"fc_landed{r}") for r in range(RING)]
        with nc.Block() as block:
            @block.gpsimd
            def _(e):
                for n in range(2 * TILES):
                    if n >= RING:
                        e.wait_ge(used, n - RING + 1)
                    e.indirect_dma_start(y[n % RING][:, :], None, slots_out, bass.IndirectOffsetOnAxis(ap=pos[:, n % 2, n // 2:n // 2 + 1], axis=0)).then_inc(landed[n % RING], 16)

            @block.vector
            def _(e):
                for n in range(2 * TILES):
                    e.wait_ge(landed[n % RING], 16 * (n // RING + 1))
                    if n % 2:
                        e.wait_ge(used, n)
                    e.scalar_tensor_tensor(out=acc[:, n // 2, :], in0=y[n % RING][:, :], scalar=choice[:, n // 2, 2 + n % 2:3 + n % 2],
                                           in1=acc[:, n // 2, :], op0=ALU.mult, op1=ALU.add).then_inc(used, 1)

            @block.sync
            def _(e):
                n = PT * (TILES - 1)
                h = TILES // 2
                e.wait_ge(used, 2 * h)
                e.dma_start(out[0:h * PT, :].rearrange("(i p) c -> p i c", p=PT), acc[:, 0:h, :]).then_inc(c_o, 16)
                e.wait_ge(used, 2 * TILES)
                e.dma_start(out[h * PT:n, :].rearrange("(i p) c -> p i c", p=PT), acc[:, h:TILES - 1, :]).then_inc(c_o, 16)
                e.dma_start(out[n:N, :], acc[0:LAST, TILES - 1, :]).then_inc(c_o, 16)
                e.wait_ge(c_o, 48)


def kernel(**inputs):
    import numpy as _np
    import concourse.bacc as _bacc
    from concourse import mybir as _mybir
    from concourse.bass_utils import run_bass_kernel_spmd as _run

    i = {k: _np.asarray(v) for k, v in inputs.items()}
    laid = {n: i[n] for n in ("x", "src", "dst", "edge_type_3", "L0_gnn_ln_gamma", "L0_gnn_ln_beta", "L0_mix_bqkv",
                              "L0_mix_bproj", "L0_mix_temperature", "L0_ffn_Wg", "L0_ffn_bg", "L0_ffn_W1",
                              "L0_ffn_W2", "L0_ffn_b2")}
    laid["convT"] = i["L0_gnn_conv_w"].transpose(0, 1, 3, 2)
    laid["wihT"] = i["L0_gnn_gru_wih"].transpose(0, 2, 1)
    laid["whhT"] = i["L0_gnn_gru_whh"].transpose(0, 2, 1)
    laid["bihT"] = i["L0_gnn_gru_bih"].reshape(3, 6, 128).transpose(2, 0, 1)
    laid["bhhT"] = i["L0_gnn_gru_bhh"].reshape(3, 6, 128).transpose(2, 0, 1)
    laid["WqkvT"] = i["L0_mix_Wqkv"].T
    laid["WprojT"] = i["L0_mix_Wproj"].T
    laid["b1T"] = i["L0_ffn_b1"].reshape(8, 8, 128).transpose(2, 0, 1)
    nc = _bacc.Bacc("TRN2", target_bir_lowering=False, num_devices=1)
    arrays, A = {}, {}
    for name, a in laid.items():
        a = _np.ascontiguousarray(a)
        arrays[f"in_{name}"] = a
        A[name] = nc.dram_tensor(f"in_{name}", a.shape, _mybir.dt.from_np(a.dtype), kind="ExternalInput").ap()
    A["out"] = nc.dram_tensor("out_0", (3125, 256), F32, kind="ExternalOutput").ap()
    gps_layer_kernel(nc, A)
    r = _run(nc, [arrays], core_ids=[0])
    return r.results[0]["out_0"]
```
